# Optimizing a Trainium2 kernel written in Bass

```python
import numpy as np
import jax
import jax.numpy as jnp

def _softmax(x, axis=-1):
    return jax.nn.softmax(x, axis=axis)

def _gelu(x):
    return jax.nn.gelu(x, approximate=True)

def _silu(x):
    return jax.nn.silu(x)

def _sigmoid(x):
    return jax.nn.sigmoid(x)

def _layernorm(x, axis=-1, eps=1e-05):
    m = jnp.mean(x, axis=axis, keepdims=True)
    v = jnp.var(x, axis=axis, keepdims=True)
    return (x - m) / jnp.sqrt(v + eps)

def _scatter_add(tgt, idx, src, axis=0):
    return tgt.at[idx].add(src)

def _segment_sum(src, seg, n):
    return jax.ops.segment_sum(src, seg, n)
kernel_name = 'mk_xattn_seq_d4_seqx_r8_ad2cfe'

def setup_inputs(seed: int=0):
    np.random.seed(seed)
    _w = jnp.asarray

    def _rec_inputs():
        import jax
        import jax.numpy as jnp
        _rk = jax.random.key(seed)
        x = -0.0002928 + 1 * jax.random.normal(jax.random.fold_in(_rk, 1), (16, 64, 256), jnp.float32)
        _lenS = 64 - jax.random.randint(jax.random.fold_in(_rk, 7), (16,), 0, max(1, 64 // 4) + 1, jnp.int32)
        _lenS2 = 64 - jax.random.randint(jax.random.fold_in(_rk, 8), (16,), 0, max(1, 64 // 4) + 1, jnp.int32)
        _ctx_2048P = jax.random.normal(jax.random.fold_in(_rk, 11), (16, 16, 256), jnp.float32)
        _ctx_2048c = jax.random.dirichlet(jax.random.fold_in(_rk, 511), 0.3 * jnp.ones((16,), jnp.float32), (16, 64))
        _ctx_2048t = jnp.einsum('bsk,bkd->bsd', _ctx_2048c, _ctx_2048P)
        _ctx_2048t = _ctx_2048t * jax.lax.rsqrt(jnp.mean(jnp.square(_ctx_2048t)) + 1e-12) * 0.953939
        ctx_2048 = -1.39393e-06 + 0.999914 * (_ctx_2048t + 0.3 * jax.random.normal(jax.random.fold_in(_rk, 611), (16, 64, 256), jnp.float32))
        _validS = jnp.arange(64)[None, :] < _lenS[:, None]
        _validS2 = jnp.arange(64)[None, :] < _lenS2[:, None]
        _causal = jnp.tril(jnp.ones((64, 64), dtype=bool))
        mask_1x1xSxS2_fc1 = jnp.where(jnp.broadcast_to(_validS2[0:1, None, None, :], (1, 1, 64, 64)), 1.0, 0.0).astype(jnp.float32)
        mask_Bx1xSxS2_ff1 = jnp.where(jnp.ones((16, 1, 64, 64), dtype=bool), 1.0, 0.0).astype(jnp.float32)
        return (x, ctx_2048, mask_1x1xSxS2_fc1, mask_Bx1xSxS2_ff1)
    x, ctx_2048, mask_1x1xSxS2_fc1, mask_Bx1xSxS2_ff1 = _rec_inputs()

    def _L0_xattn_setup():
        import jax, jax.numpy as jnp
        import numpy as np
        H = 256
        NH = 16
        HD = H // NH
        EPS = 1e-05

        def gelu(x):
            return 0.5 * x * (1.0 + jnp.tanh(0.7978845608028654 * x * (1.0 + 0.044715 * x * x)))

        def layernorm(x, scale, bias):
            m = jnp.mean(x, axis=-1, keepdims=True)
            v = jnp.mean(jnp.square(x - m), axis=-1, keepdims=True)
            return (x - m) * jax.lax.rsqrt(v + EPS) * scale + bias

        def split_heads(x):
            b, s, _ = x.shape
            return x.reshape(b, s, NH, HD).transpose(0, 2, 1, 3)

        def merge_heads(x):
            b, nh, s, hd = x.shape
            return x.transpose(0, 2, 1, 3).reshape(b, s, nh * hd)

        def attention(q, k, v, mask):
            scores = jnp.einsum('bhqd,bhkd->bhqk', q, k) / jnp.sqrt(jnp.float32(HD))
            scores = scores * mask - 10000.0 * (1.0 - mask)
            probs = jax.nn.softmax(scores, axis=-1)
            return jnp.einsum('bhqk,bhkd->bhqd', probs, v)
        key = jax.random.key(seed)
        ks = jax.random.split(key, 16)
        b, s, t = (2, 128, 128)
        w = lambda k, i, o: jax.random.normal(k, (i, o), jnp.float32) * 0.02
        inp = {'hidden_states': jax.random.normal(ks[0], (b, s, H), jnp.float32), 'encoder_states': jax.random.normal(ks[1], (b, t, H), jnp.float32), 'ltor_mask': jnp.tril(jnp.ones((1, 1, s, s), jnp.float32)), 'cross_mask': jnp.ones((b, 1, s, t), jnp.float32), 'ln1_s': jnp.ones((H,), jnp.float32), 'ln1_b': jnp.zeros((H,), jnp.float32), 'w_qkv': w(ks[2], H, 3 * H), 'b_qkv': jnp.zeros((3 * H,), jnp.float32), 'w_ao': w(ks[3], H, H), 'b_ao': jnp.zeros((H,), jnp.float32), 'ln2_s': jnp.ones((H,), jnp.float32), 'ln2_b': jnp.zeros((H,), jnp.float32), 'w_q': w(ks[4], H, H), 'b_q': jnp.zeros((H,), jnp.float32), 'w_kv': w(ks[5], H, 2 * H), 'b_kv': jnp.zeros((2 * H,), jnp.float32), 'w_co': w(ks[6], H, H), 'b_co': jnp.zeros((H,), jnp.float32), 'ln3_s': jnp.ones((H,), jnp.float32), 'ln3_b': jnp.zeros((H,), jnp.float32), 'w1': w(ks[7], H, 4 * H), 'b1': jnp.zeros((4 * H,), jnp.float32), 'w2': w(ks[8], 4 * H, H), 'b2': jnp.zeros((H,), jnp.float32)}
        return inp
    _L0_xattn_all = _L0_xattn_setup()
    _L0_xattn_in = {k: v for k, v in _L0_xattn_all.items() if k in ('ln1_s', 'ln1_b', 'w_qkv', 'b_qkv', 'w_ao', 'b_ao', 'ln2_s', 'ln2_b', 'w_q', 'b_q', 'w_kv', 'b_kv', 'w_co', 'b_co', 'ln3_s', 'ln3_b', 'w1', 'b1', 'w2', 'b2')}
    del _L0_xattn_all

    def _L1_xattn_setup():
        import jax, jax.numpy as jnp
        import numpy as np
        EPS = 1e-05

        def _inorm(x):
            m = jnp.mean(x, axis=-1, keepdims=True)
            v = jnp.var(x, axis=-1, keepdims=True)
            return (x - m) * jax.lax.rsqrt(v + EPS)

        def _conv1x1(W, b, x):
            return jnp.einsum('oc,bct->bot', W, x) + b[None, :, None]
        key = jax.random.key(seed)
        ks = jax.random.split(key, 10)
        B, C, T = (4, 64, 256)
        s = 1.0 / np.sqrt(C)
        return {'x_c': jax.random.normal(ks[0], (B, C, T), jnp.float32), 'x_s': jax.random.normal(ks[1], (B, C, T), jnp.float32), 'Wn': jax.random.normal(ks[2], (C, C), jnp.float32) * s, 'bn': jax.random.normal(ks[3], (C,), jnp.float32) * s, 'Wm': jax.random.normal(ks[4], (C, C), jnp.float32) * s, 'bm': jax.random.normal(ks[5], (C,), jnp.float32) * s, 'Wl': jax.random.normal(ks[6], (C, C), jnp.float32) * s, 'bl': jax.random.normal(ks[7], (C,), jnp.float32) * s, 'Wo': jax.random.normal(ks[8], (C, C), jnp.float32) * s, 'bo': jax.random.normal(ks[9], (C,), jnp.float32) * s}
    _L1_xattn_all = _L1_xattn_setup()
    _L1_xattn_in = {k: v for k, v in _L1_xattn_all.items() if k in ('Wn', 'bn', 'Wm', 'bm', 'Wl', 'bl', 'Wo', 'bo')}
    del _L1_xattn_all

    def _L2_xattn_setup():
        import jax, jax.numpy as jnp
        import numpy as np
        B, Q, S1, S2 = (4, 32, 256, 256)
        D, H, K, F = (256, 16, 128, 1024)
        LN_EPS = 1e-05

        def _layer_norm(x, scale, offset):
            mu = jnp.mean(x, axis=-1, keepdims=True)
            var = jnp.var(x, axis=-1, keepdims=True)
            return (x - mu) * jax.lax.rsqrt(var + LN_EPS) * scale + offset

        def _cross_attention(q_in, kv_in, wq, bq, wk, bk, wv, bv, wo, bo, bias_k, bias_v):
            b, q_len, _ = q_in.shape
            t = kv_in.shape[1]
            qh = (q_in @ wq + bq).reshape(b, q_len, H, K)
            kh = (kv_in @ wk + bk).reshape(b, t, H, K)
            vh = (kv_in @ wv + bv).reshape(b, t, H, K)
            kh = jnp.concatenate([kh, jnp.broadcast_to(bias_k, (b, 1, H, K))], axis=1)
            vh = jnp.concatenate([vh, jnp.broadcast_to(bias_v, (b, 1, H, K))], axis=1)
            scale = jnp.sqrt(jnp.asarray(K, q_in.dtype))
            logits = jnp.einsum('bqhk,bthk->bhqt', qh, kh) / scale
            weights = jax.nn.softmax(logits, axis=-1)
            ctx = jnp.einsum('bhqt,bthk->bqhk', weights, vh).reshape(b, q_len, H * K)
            return ctx @ wo + bo

        def _forward(x, xf_1, xf_2, ln1_scale, ln1_offset, wq1, bq1, wk1, bk1, wv1, bv1, wo1, bo1, bias_k1, bias_v1, ln2_scale, ln2_offset, wq2, bq2, wk2, bk2, wv2, bv2, wo2, bo2, bias_k2, bias_v2, ln_mlp_scale, ln_mlp_offset, w_fc1, b_fc1, w_fc2, b_fc2):
            res = x
            h = _layer_norm(x, ln1_scale, ln1_offset)
            x = res + _cross_attention(h, xf_1, wq1, bq1, wk1, bk1, wv1, bv1, wo1, bo1, bias_k1, bias_v1)
            res = x
            h = _layer_norm(x, ln2_scale, ln2_offset)
            x = res + _cross_attention(h, xf_2, wq2, bq2, wk2, bk2, wv2, bv2, wo2, bo2, bias_k2, bias_v2)
            h = _layer_norm(x, ln_mlp_scale, ln_mlp_offset)
            h = jax.nn.gelu(h @ w_fc1 + b_fc1, approximate=False) @ w_fc2 + b_fc2
            return x + h
        key = jax.random.key(seed)
        ks = iter(jax.random.split(key, 64))

        def rn(shape, s=0.02):
            return jax.random.normal(next(ks), shape, jnp.float32) * s
        inp = {'x': rn((B, Q, D), 1.0), 'xf_1': rn((B, S1, D), 1.0), 'xf_2': rn((B, S2, D), 1.0)}
        for i in (1, 2):
            inp[f'ln{i}_scale'] = jnp.ones((D,), jnp.float32)
            inp[f'ln{i}_offset'] = jnp.zeros((D,), jnp.float32)
            inp[f'wq{i}'] = rn((D, H * K))
            inp[f'bq{i}'] = jnp.zeros((H * K,), jnp.float32)
            inp[f'wk{i}'] = rn((D, H * K))
            inp[f'bk{i}'] = jnp.zeros((H * K,), jnp.float32)
            inp[f'wv{i}'] = rn((D, H * K))
            inp[f'bv{i}'] = jnp.zeros((H * K,), jnp.float32)
            inp[f'wo{i}'] = rn((H * K, D))
            inp[f'bo{i}'] = jnp.zeros((D,), jnp.float32)
            inp[f'bias_k{i}'] = rn((1, 1, H, K))
            inp[f'bias_v{i}'] = rn((1, 1, H, K))
        inp['ln_mlp_scale'] = jnp.ones((D,), jnp.float32)
        inp['ln_mlp_offset'] = jnp.zeros((D,), jnp.float32)
        inp['w_fc1'] = rn((D, F))
        inp['b_fc1'] = jnp.zeros((F,), jnp.float32)
        inp['w_fc2'] = rn((F, D))
        inp['b_fc2'] = jnp.zeros((D,), jnp.float32)
        return inp
    _L2_xattn_all = _L2_xattn_setup()
    _L2_xattn_in = {k: v for k, v in _L2_xattn_all.items() if k in ('ln1_scale', 'ln1_offset', 'wq1', 'bq1', 'wk1', 'bk1', 'wv1', 'bv1', 'wo1', 'bo1', 'bias_k1', 'bias_v1', 'ln2_scale', 'ln2_offset', 'wq2', 'bq2', 'wk2', 'bk2', 'wv2', 'bv2', 'wo2', 'bo2', 'bias_k2', 'bias_v2', 'ln_mlp_scale', 'ln_mlp_offset', 'w_fc1', 'b_fc1', 'w_fc2', 'b_fc2')}
    del _L2_xattn_all

    def _L3_xattn_setup():
        import jax, jax.numpy as jnp
        import numpy as np
        E, H, L, B = (256, 32, 128, 4)
        S = E // H
        DM, DD = (32, 64)

        def _ln(x, w, b, eps=1e-05):
            m = x.mean(-1, keepdims=True)
            v = ((x - m) ** 2).mean(-1, keepdims=True)
            return (x - m) / jnp.sqrt(v + eps) * w + b

        def _block(x, state, ln1_w, ln1_b, ln2_w, ln2_b, maa_x, maa_w1, maa_w2, maa_stack, time_decay, td_w1, td_w2, u, Wr, Wk, Wv, Wg, Wo, gn_w, gn_b, ffn_maa_k, ffn_maa_r, Wfk, Wfr, Wfv):
            b, l, e = x.shape
            h = u.shape[0]
            s_ = e // h
            xa = _ln(x, ln1_w, ln1_b)
            sx = jnp.concatenate([state[:, 1:2] - xa[:, :1], xa[:, :-1] - xa[:, 1:]], axis=1)
            xxx = jnp.tanh((xa + sx * maa_x) @ maa_w1).reshape(b, l, 5, DM)
            xxx = jnp.einsum('blfd,fde->blfe', xxx, maa_w2)
            xm = xa[:, :, None] + sx[:, :, None] * (maa_stack + xxx)
            xk, xw, xv, xr, xg = (xm[:, :, j] for j in range(5))
            w = jnp.exp(-jnp.exp(time_decay + jnp.tanh(xw @ td_w1) @ td_w2)).reshape(b, l, h, s_)
            r = (xr @ Wr.T).reshape(b, l, h, s_)
            k = (xk @ Wk.T).reshape(b, l, h, s_)
            v = (xv @ Wv.T).reshape(b, l, h, s_)
            g = jax.nn.silu(xg @ Wg.T)
            s0 = state[:, 2:2 + s_].reshape(b, h, s_, s_)

            def step(s, rkvw):
                r_t, k_t, v_t, w_t = rkvw
                a = k_t[..., :, None] * v_t[..., None, :]
                out = jnp.einsum('bhi,bhij->bhj', r_t, u * a + s)
                s = a + w_t[..., :, None] * s
                return (s, out)
            rkvw = tuple((jnp.moveaxis(t, 1, 0) for t in (r, k, v, w)))
            _, out = jax.lax.scan(step, s0, rkvw)
            out = jnp.moveaxis(out, 0, 1).reshape(b, l, e)
            og = out.reshape(b, l, h, s_)
            m = og.mean(-1, keepdims=True)
            va = ((og - m) ** 2).mean(-1, keepdims=True)
            og = ((og - m) / jnp.sqrt(va + 1e-05)).reshape(b, l, e) * gn_w + gn_b
            x1 = x + og * g @ Wo.T
            xc = _ln(x1, ln2_w, ln2_b)
            sx2 = jnp.concatenate([state[:, 0:1] - xc[:, :1], xc[:, :-1] - xc[:, 1:]], axis=1)
            xk2 = xc + sx2 * ffn_maa_k
            xr2 = xc + sx2 * ffn_maa_r
            rr = jax.nn.sigmoid(xr2 @ Wfr.T)
            kk = jnp.square(jax.nn.relu(xk2 @ Wfk.T))
            return x1 + rr * (kk @ Wfv.T)
        key = jax.random.key(seed)
        ks = jax.random.split(key, 24)
        sc = 0.02
        d = {'x': jax.random.normal(ks[0], (B, L, E), jnp.float32), 'state': jax.random.normal(ks[1], (B, 2 + S, E), jnp.float32) * 0.1, 'ln1_w': jnp.ones((E,), jnp.float32), 'ln1_b': jnp.zeros((E,), jnp.float32), 'ln2_w': jnp.ones((E,), jnp.float32), 'ln2_b': jnp.zeros((E,), jnp.float32), 'maa_x': jax.random.normal(ks[2], (E,), jnp.float32) * 0.1, 'maa_w1': jax.random.normal(ks[3], (E, 5 * DM), jnp.float32) * sc, 'maa_w2': jax.random.normal(ks[4], (5, DM, E), jnp.float32) * sc, 'maa_stack': jax.random.normal(ks[5], (1, 5, E), jnp.float32) * 0.1, 'time_decay': jax.random.normal(ks[6], (E,), jnp.float32) * 0.5, 'td_w1': jax.random.normal(ks[7], (E, DD), jnp.float32) * sc, 'td_w2': jax.random.normal(ks[8], (DD, E), jnp.float32) * sc, 'u': jax.random.normal(ks[9], (H, S, 1), jnp.float32) * 0.1, 'Wr': jax.random.normal(ks[10], (E, E), jnp.float32) * sc, 'Wk': jax.random.normal(ks[11], (E, E), jnp.float32) * sc, 'Wv': jax.random.normal(ks[12], (E, E), jnp.float32) * sc, 'Wg': jax.random.normal(ks[13], (E, E), jnp.float32) * sc, 'Wo': jax.random.normal(ks[14], (E, E), jnp.float32) * sc, 'gn_w': jnp.ones((E,), jnp.float32), 'gn_b': jnp.zeros((E,), jnp.float32), 'ffn_maa_k': jax.random.normal(ks[15], (E,), jnp.float32) * 0.1, 'ffn_maa_r': jax.random.normal(ks[16], (E,), jnp.float32) * 0.1, 'Wfk': jax.random.normal(ks[17], (E, E), jnp.float32) * sc, 'Wfr': jax.random.normal(ks[18], (E, E), jnp.float32) * sc, 'Wfv': jax.random.normal(ks[19], (E, E), jnp.float32) * sc}
        return d
    _L3_xattn_all = _L3_xattn_setup()
    _L3_xattn_in = {k: v for k, v in _L3_xattn_all.items() if k in ('ln1_w', 'ln1_b', 'ln2_w', 'ln2_b', 'maa_x', 'maa_w1', 'maa_w2', 'maa_stack', 'time_decay', 'td_w1', 'td_w2', 'u', 'Wr', 'Wk', 'Wv', 'Wg', 'Wo', 'gn_w', 'gn_b', 'ffn_maa_k', 'ffn_maa_r', 'Wfk', 'Wfr', 'Wfv')}
    del _L3_xattn_all
    return {'x': x, 'ctx_2048': ctx_2048, 'mask_1x1xSxS2_fc1': mask_1x1xSxS2_fc1, 'mask_Bx1xSxS2_ff1': mask_Bx1xSxS2_ff1, 'L0_xattn_ln1_s': _L0_xattn_in['ln1_s'], 'L0_xattn_ln1_b': _L0_xattn_in['ln1_b'], 'L0_xattn_w_qkv': _L0_xattn_in['w_qkv'], 'L0_xattn_b_qkv': _L0_xattn_in['b_qkv'], 'L0_xattn_w_ao': _L0_xattn_in['w_ao'], 'L0_xattn_b_ao': _L0_xattn_in['b_ao'], 'L0_xattn_ln2_s': _L0_xattn_in['ln2_s'], 'L0_xattn_ln2_b': _L0_xattn_in['ln2_b'], 'L0_xattn_w_q': _L0_xattn_in['w_q'], 'L0_xattn_b_q': _L0_xattn_in['b_q'], 'L0_xattn_w_kv': _L0_xattn_in['w_kv'], 'L0_xattn_b_kv': _L0_xattn_in['b_kv'], 'L0_xattn_w_co': _L0_xattn_in['w_co'], 'L0_xattn_b_co': _L0_xattn_in['b_co'], 'L0_xattn_ln3_s': _L0_xattn_in['ln3_s'], 'L0_xattn_ln3_b': _L0_xattn_in['ln3_b'], 'L0_xattn_w1': _L0_xattn_in['w1'], 'L0_xattn_b1': _L0_xattn_in['b1'], 'L0_xattn_w2': _L0_xattn_in['w2'], 'L0_xattn_b2': _L0_xattn_in['b2'], 'L1_xattn_Wn': _L1_xattn_in['Wn'], 'L1_xattn_bn': _L1_xattn_in['bn'], 'L1_xattn_Wm': _L1_xattn_in['Wm'], 'L1_xattn_bm': _L1_xattn_in['bm'], 'L1_xattn_Wl': _L1_xattn_in['Wl'], 'L1_xattn_bl': _L1_xattn_in['bl'], 'L1_xattn_Wo': _L1_xattn_in['Wo'], 'L1_xattn_bo': _L1_xattn_in['bo'], 'L2_xattn_ln1_scale': _L2_xattn_in['ln1_scale'], 'L2_xattn_ln1_offset': _L2_xattn_in['ln1_offset'], 'L2_xattn_wq1': _L2_xattn_in['wq1'], 'L2_xattn_bq1': _L2_xattn_in['bq1'], 'L2_xattn_wk1': _L2_xattn_in['wk1'], 'L2_xattn_bk1': _L2_xattn_in['bk1'], 'L2_xattn_wv1': _L2_xattn_in['wv1'], 'L2_xattn_bv1': _L2_xattn_in['bv1'], 'L2_xattn_wo1': _L2_xattn_in['wo1'], 'L2_xattn_bo1': _L2_xattn_in['bo1'], 'L2_xattn_bias_k1': _L2_xattn_in['bias_k1'], 'L2_xattn_bias_v1': _L2_xattn_in['bias_v1'], 'L2_xattn_ln2_scale': _L2_xattn_in['ln2_scale'], 'L2_xattn_ln2_offset': _L2_xattn_in['ln2_offset'], 'L2_xattn_wq2': _L2_xattn_in['wq2'], 'L2_xattn_bq2': _L2_xattn_in['bq2'], 'L2_xattn_wk2': _L2_xattn_in['wk2'], 'L2_xattn_bk2': _L2_xattn_in['bk2'], 'L2_xattn_wv2': _L2_xattn_in['wv2'], 'L2_xattn_bv2': _L2_xattn_in['bv2'], 'L2_xattn_wo2': _L2_xattn_in['wo2'], 'L2_xattn_bo2': _L2_xattn_in['bo2'], 'L2_xattn_bias_k2': _L2_xattn_in['bias_k2'], 'L2_xattn_bias_v2': _L2_xattn_in['bias_v2'], 'L2_xattn_ln_mlp_scale': _L2_xattn_in['ln_mlp_scale'], 'L2_xattn_ln_mlp_offset': _L2_xattn_in['ln_mlp_offset'], 'L2_xattn_w_fc1': _L2_xattn_in['w_fc1'], 'L2_xattn_b_fc1': _L2_xattn_in['b_fc1'], 'L2_xattn_w_fc2': _L2_xattn_in['w_fc2'], 'L2_xattn_b_fc2': _L2_xattn_in['b_fc2'], 'L3_xattn_ln1_w': _L3_xattn_in['ln1_w'], 'L3_xattn_ln1_b': _L3_xattn_in['ln1_b'], 'L3_xattn_ln2_w': _L3_xattn_in['ln2_w'], 'L3_xattn_ln2_b': _L3_xattn_in['ln2_b'], 'L3_xattn_maa_x': _L3_xattn_in['maa_x'], 'L3_xattn_maa_w1': _L3_xattn_in['maa_w1'], 'L3_xattn_maa_w2': _L3_xattn_in['maa_w2'], 'L3_xattn_maa_stack': _L3_xattn_in['maa_stack'], 'L3_xattn_time_decay': _L3_xattn_in['time_decay'], 'L3_xattn_td_w1': _L3_xattn_in['td_w1'], 'L3_xattn_td_w2': _L3_xattn_in['td_w2'], 'L3_xattn_u': _L3_xattn_in['u'], 'L3_xattn_Wr': _L3_xattn_in['Wr'], 'L3_xattn_Wk': _L3_xattn_in['Wk'], 'L3_xattn_Wv': _L3_xattn_in['Wv'], 'L3_xattn_Wg': _L3_xattn_in['Wg'], 'L3_xattn_Wo': _L3_xattn_in['Wo'], 'L3_xattn_gn_w': _L3_xattn_in['gn_w'], 'L3_xattn_gn_b': _L3_xattn_in['gn_b'], 'L3_xattn_ffn_maa_k': _L3_xattn_in['ffn_maa_k'], 'L3_xattn_ffn_maa_r': _L3_xattn_in['ffn_maa_r'], 'L3_xattn_Wfk': _L3_xattn_in['Wfk'], 'L3_xattn_Wfr': _L3_xattn_in['Wfr'], 'L3_xattn_Wfv': _L3_xattn_in['Wfv']}

def reference(x, ctx_2048, mask_1x1xSxS2_fc1, mask_Bx1xSxS2_ff1, L0_xattn_ln1_s, L0_xattn_ln1_b, L0_xattn_w_qkv, L0_xattn_b_qkv, L0_xattn_w_ao, L0_xattn_b_ao, L0_xattn_ln2_s, L0_xattn_ln2_b, L0_xattn_w_q, L0_xattn_b_q, L0_xattn_w_kv, L0_xattn_b_kv, L0_xattn_w_co, L0_xattn_b_co, L0_xattn_ln3_s, L0_xattn_ln3_b, L0_xattn_w1, L0_xattn_b1, L0_xattn_w2, L0_xattn_b2, L1_xattn_Wn, L1_xattn_bn, L1_xattn_Wm, L1_xattn_bm, L1_xattn_Wl, L1_xattn_bl, L1_xattn_Wo, L1_xattn_bo, L2_xattn_ln1_scale, L2_xattn_ln1_offset, L2_xattn_wq1, L2_xattn_bq1, L2_xattn_wk1, L2_xattn_bk1, L2_xattn_wv1, L2_xattn_bv1, L2_xattn_wo1, L2_xattn_bo1, L2_xattn_bias_k1, L2_xattn_bias_v1, L2_xattn_ln2_scale, L2_xattn_ln2_offset, L2_xattn_wq2, L2_xattn_bq2, L2_xattn_wk2, L2_xattn_bk2, L2_xattn_wv2, L2_xattn_bv2, L2_xattn_wo2, L2_xattn_bo2, L2_xattn_bias_k2, L2_xattn_bias_v2, L2_xattn_ln_mlp_scale, L2_xattn_ln_mlp_offset, L2_xattn_w_fc1, L2_xattn_b_fc1, L2_xattn_w_fc2, L2_xattn_b_fc2, L3_xattn_ln1_w, L3_xattn_ln1_b, L3_xattn_ln2_w, L3_xattn_ln2_b, L3_xattn_maa_x, L3_xattn_maa_w1, L3_xattn_maa_w2, L3_xattn_maa_stack, L3_xattn_time_decay, L3_xattn_td_w1, L3_xattn_td_w2, L3_xattn_u, L3_xattn_Wr, L3_xattn_Wk, L3_xattn_Wv, L3_xattn_Wg, L3_xattn_Wo, L3_xattn_gn_w, L3_xattn_gn_b, L3_xattn_ffn_maa_k, L3_xattn_ffn_maa_r, L3_xattn_Wfk, L3_xattn_Wfr, L3_xattn_Wfv):
    import jax
    import jax.numpy as jnp

    def _L0_xattn_ref(hidden_states, encoder_states, ltor_mask, cross_mask, ln1_s, ln1_b, w_qkv, b_qkv, w_ao, b_ao, ln2_s, ln2_b, w_q, b_q, w_kv, b_kv, w_co, b_co, ln3_s, ln3_b, w1, b1, w2, b2):
        import jax, jax.numpy as jnp
        import numpy as np
        H = 256
        NH = 16
        HD = H // NH
        EPS = 1e-05

        def gelu(x):
            return 0.5 * x * (1.0 + jnp.tanh(0.7978845608028654 * x * (1.0 + 0.044715 * x * x)))

        def layernorm(x, scale, bias):
            m = jnp.mean(x, axis=-1, keepdims=True)
            v = jnp.mean(jnp.square(x - m), axis=-1, keepdims=True)
            return (x - m) * jax.lax.rsqrt(v + EPS) * scale + bias

        def split_heads(x):
            b, s, _ = x.shape
            return x.reshape(b, s, NH, HD).transpose(0, 2, 1, 3)

        def merge_heads(x):
            b, nh, s, hd = x.shape
            return x.transpose(0, 2, 1, 3).reshape(b, s, nh * hd)

        def attention(q, k, v, mask):
            scores = jnp.einsum('bhqd,bhkd->bhqk', q, k) / jnp.sqrt(jnp.float32(HD))
            scores = scores * mask - 10000.0 * (1.0 - mask)
            probs = jax.nn.softmax(scores, axis=-1)
            return jnp.einsum('bhqk,bhkd->bhqd', probs, v)
        ln_out = layernorm(hidden_states, ln1_s, ln1_b)
        qkv = ln_out @ w_qkv + b_qkv
        q, k, v = jnp.split(qkv, 3, axis=-1)
        ctx = merge_heads(attention(split_heads(q), split_heads(k), split_heads(v), ltor_mask))
        attn_out = ctx @ w_ao + b_ao
        x = hidden_states + attn_out
        ln_out = layernorm(x, ln2_s, ln2_b)
        q = ln_out @ w_q + b_q
        kv = encoder_states @ w_kv + b_kv
        k, v = jnp.split(kv, 2, axis=-1)
        ctx = merge_heads(attention(split_heads(q), split_heads(k), split_heads(v), cross_mask))
        cross_out = ctx @ w_co + b_co
        x = x + cross_out
        ln_out = layernorm(x, ln3_s, ln3_b)
        mlp_out = gelu(ln_out @ w1 + b1) @ w2 + b2
        return x + mlp_out

    def _L1_xattn_ref(x_c, x_s, Wn, bn, Wm, bm, Wl, bl, Wo, bo):
        import jax, jax.numpy as jnp
        import numpy as np
        EPS = 1e-05

        def _inorm(x):
            m = jnp.mean(x, axis=-1, keepdims=True)
            v = jnp.var(x, axis=-1, keepdims=True)
            return (x - m) * jax.lax.rsqrt(v + EPS)

        def _conv1x1(W, b, x):
            return jnp.einsum('oc,bct->bot', W, x) + b[None, :, None]
        Mn = _conv1x1(Wn, bn, _inorm(x_c))
        Mm = _conv1x1(Wm, bm, _inorm(x_s))
        A = jax.nn.softmax(jnp.einsum('bct,bcs->bts', Mn, Mm), axis=-1)
        Ml = _conv1x1(Wl, bl, x_s)
        Mo = jnp.einsum('bcs,bts->bct', Ml, A)
        return _conv1x1(Wo, bo, Mo) + x_c

    def _L2_xattn_ref(x, xf_1, xf_2, ln1_scale, ln1_offset, wq1, bq1, wk1, bk1, wv1, bv1, wo1, bo1, bias_k1, bias_v1, ln2_scale, ln2_offset, wq2, bq2, wk2, bk2, wv2, bv2, wo2, bo2, bias_k2, bias_v2, ln_mlp_scale, ln_mlp_offset, w_fc1, b_fc1, w_fc2, b_fc2):
        import jax, jax.numpy as jnp
        import numpy as np
        B, Q, S1, S2 = (4, 32, 256, 256)
        D, H, K, F = (256, 16, 128, 1024)
        LN_EPS = 1e-05

        def _layer_norm(x, scale, offset):
            mu = jnp.mean(x, axis=-1, keepdims=True)
            var = jnp.var(x, axis=-1, keepdims=True)
            return (x - mu) * jax.lax.rsqrt(var + LN_EPS) * scale + offset

        def _cross_attention(q_in, kv_in, wq, bq, wk, bk, wv, bv, wo, bo, bias_k, bias_v):
            b, q_len, _ = q_in.shape
            t = kv_in.shape[1]
            qh = (q_in @ wq + bq).reshape(b, q_len, H, K)
            kh = (kv_in @ wk + bk).reshape(b, t, H, K)
            vh = (kv_in @ wv + bv).reshape(b, t, H, K)
            kh = jnp.concatenate([kh, jnp.broadcast_to(bias_k, (b, 1, H, K))], axis=1)
            vh = jnp.concatenate([vh, jnp.broadcast_to(bias_v, (b, 1, H, K))], axis=1)
            scale = jnp.sqrt(jnp.asarray(K, q_in.dtype))
            logits = jnp.einsum('bqhk,bthk->bhqt', qh, kh) / scale
            weights = jax.nn.softmax(logits, axis=-1)
            ctx = jnp.einsum('bhqt,bthk->bqhk', weights, vh).reshape(b, q_len, H * K)
            return ctx @ wo + bo

        def _forward(x, xf_1, xf_2, ln1_scale, ln1_offset, wq1, bq1, wk1, bk1, wv1, bv1, wo1, bo1, bias_k1, bias_v1, ln2_scale, ln2_offset, wq2, bq2, wk2, bk2, wv2, bv2, wo2, bo2, bias_k2, bias_v2, ln_mlp_scale, ln_mlp_offset, w_fc1, b_fc1, w_fc2, b_fc2):
            res = x
            h = _layer_norm(x, ln1_scale, ln1_offset)
            x = res + _cross_attention(h, xf_1, wq1, bq1, wk1, bk1, wv1, bv1, wo1, bo1, bias_k1, bias_v1)
            res = x
            h = _layer_norm(x, ln2_scale, ln2_offset)
            x = res + _cross_attention(h, xf_2, wq2, bq2, wk2, bk2, wv2, bv2, wo2, bo2, bias_k2, bias_v2)
            h = _layer_norm(x, ln_mlp_scale, ln_mlp_offset)
            h = jax.nn.gelu(h @ w_fc1 + b_fc1, approximate=False) @ w_fc2 + b_fc2
            return x + h
        return _forward(x, xf_1, xf_2, ln1_scale, ln1_offset, wq1, bq1, wk1, bk1, wv1, bv1, wo1, bo1, bias_k1, bias_v1, ln2_scale, ln2_offset, wq2, bq2, wk2, bk2, wv2, bv2, wo2, bo2, bias_k2, bias_v2, ln_mlp_scale, ln_mlp_offset, w_fc1, b_fc1, w_fc2, b_fc2)

    def _L3_xattn_ref(x, state, ln1_w, ln1_b, ln2_w, ln2_b, maa_x, maa_w1, maa_w2, maa_stack, time_decay, td_w1, td_w2, u, Wr, Wk, Wv, Wg, Wo, gn_w, gn_b, ffn_maa_k, ffn_maa_r, Wfk, Wfr, Wfv):
        import jax, jax.numpy as jnp
        import numpy as np
        E, H, L, B = (256, 32, 128, 4)
        S = E // H
        DM, DD = (32, 64)

        def _ln(x, w, b, eps=1e-05):
            m = x.mean(-1, keepdims=True)
            v = ((x - m) ** 2).mean(-1, keepdims=True)
            return (x - m) / jnp.sqrt(v + eps) * w + b

        def _block(x, state, ln1_w, ln1_b, ln2_w, ln2_b, maa_x, maa_w1, maa_w2, maa_stack, time_decay, td_w1, td_w2, u, Wr, Wk, Wv, Wg, Wo, gn_w, gn_b, ffn_maa_k, ffn_maa_r, Wfk, Wfr, Wfv):
            b, l, e = x.shape
            h = u.shape[0]
            s_ = e // h
            xa = _ln(x, ln1_w, ln1_b)
            sx = jnp.concatenate([state[:, 1:2] - xa[:, :1], xa[:, :-1] - xa[:, 1:]], axis=1)
            xxx = jnp.tanh((xa + sx * maa_x) @ maa_w1).reshape(b, l, 5, DM)
            xxx = jnp.einsum('blfd,fde->blfe', xxx, maa_w2)
            xm = xa[:, :, None] + sx[:, :, None] * (maa_stack + xxx)
            xk, xw, xv, xr, xg = (xm[:, :, j] for j in range(5))
            w = jnp.exp(-jnp.exp(time_decay + jnp.tanh(xw @ td_w1) @ td_w2)).reshape(b, l, h, s_)
            r = (xr @ Wr.T).reshape(b, l, h, s_)
            k = (xk @ Wk.T).reshape(b, l, h, s_)
            v = (xv @ Wv.T).reshape(b, l, h, s_)
            g = jax.nn.silu(xg @ Wg.T)
            s0 = state[:, 2:2 + s_].reshape(b, h, s_, s_)

            def step(s, rkvw):
                r_t, k_t, v_t, w_t = rkvw
                a = k_t[..., :, None] * v_t[..., None, :]
                out = jnp.einsum('bhi,bhij->bhj', r_t, u * a + s)
                s = a + w_t[..., :, None] * s
                return (s, out)
            rkvw = tuple((jnp.moveaxis(t, 1, 0) for t in (r, k, v, w)))
            _, out = jax.lax.scan(step, s0, rkvw)
            out = jnp.moveaxis(out, 0, 1).reshape(b, l, e)
            og = out.reshape(b, l, h, s_)
            m = og.mean(-1, keepdims=True)
            va = ((og - m) ** 2).mean(-1, keepdims=True)
            og = ((og - m) / jnp.sqrt(va + 1e-05)).reshape(b, l, e) * gn_w + gn_b
            x1 = x + og * g @ Wo.T
            xc = _ln(x1, ln2_w, ln2_b)
            sx2 = jnp.concatenate([state[:, 0:1] - xc[:, :1], xc[:, :-1] - xc[:, 1:]], axis=1)
            xk2 = xc + sx2 * ffn_maa_k
            xr2 = xc + sx2 * ffn_maa_r
            rr = jax.nn.sigmoid(xr2 @ Wfr.T)
            kk = jnp.square(jax.nn.relu(xk2 @ Wfk.T))
            return x1 + rr * (kk @ Wfv.T)
        return _block(x, state, ln1_w, ln1_b, ln2_w, ln2_b, maa_x, maa_w1, maa_w2, maa_stack, time_decay, td_w1, td_w2, u, Wr, Wk, Wv, Wg, Wo, gn_w, gn_b, ffn_maa_k, ffn_maa_r, Wfk, Wfr, Wfv)
    x = _L0_xattn_ref(x, ctx_2048, mask_1x1xSxS2_fc1, mask_Bx1xSxS2_ff1, L0_xattn_ln1_s, L0_xattn_ln1_b, L0_xattn_w_qkv, L0_xattn_b_qkv, L0_xattn_w_ao, L0_xattn_b_ao, L0_xattn_ln2_s, L0_xattn_ln2_b, L0_xattn_w_q, L0_xattn_b_q, L0_xattn_w_kv, L0_xattn_b_kv, L0_xattn_w_co, L0_xattn_b_co, L0_xattn_ln3_s, L0_xattn_ln3_b, L0_xattn_w1, L0_xattn_b1, L0_xattn_w2, L0_xattn_b2)
    x = _L1_xattn_ref(x, ctx_2048, L1_xattn_Wn, L1_xattn_bn, L1_xattn_Wm, L1_xattn_bm, L1_xattn_Wl, L1_xattn_bl, L1_xattn_Wo, L1_xattn_bo)
    x = _L2_xattn_ref(x, ctx_2048, ctx_2048, L2_xattn_ln1_scale, L2_xattn_ln1_offset, L2_xattn_wq1, L2_xattn_bq1, L2_xattn_wk1, L2_xattn_bk1, L2_xattn_wv1, L2_xattn_bv1, L2_xattn_wo1, L2_xattn_bo1, L2_xattn_bias_k1, L2_xattn_bias_v1, L2_xattn_ln2_scale, L2_xattn_ln2_offset, L2_xattn_wq2, L2_xattn_bq2, L2_xattn_wk2, L2_xattn_bk2, L2_xattn_wv2, L2_xattn_bv2, L2_xattn_wo2, L2_xattn_bo2, L2_xattn_bias_k2, L2_xattn_bias_v2, L2_xattn_ln_mlp_scale, L2_xattn_ln_mlp_offset, L2_xattn_w_fc1, L2_xattn_b_fc1, L2_xattn_w_fc2, L2_xattn_b_fc2)
    x = _L3_xattn_ref(x, ctx_2048, L3_xattn_ln1_w, L3_xattn_ln1_b, L3_xattn_ln2_w, L3_xattn_ln2_b, L3_xattn_maa_x, L3_xattn_maa_w1, L3_xattn_maa_w2, L3_xattn_maa_stack, L3_xattn_time_decay, L3_xattn_td_w1, L3_xattn_td_w2, L3_xattn_u, L3_xattn_Wr, L3_xattn_Wk, L3_xattn_Wv, L3_xattn_Wg, L3_xattn_Wo, L3_xattn_gn_w, L3_xattn_gn_b, L3_xattn_ffn_maa_k, L3_xattn_ffn_maa_r, L3_xattn_Wfk, L3_xattn_Wfr, L3_xattn_Wfv)
    return x

_drawn_inputs = setup_inputs


def setup_inputs(seed=0):
    import zlib

    import numpy as np

    out = dict(_drawn_inputs(seed))
    spreads = {'L0_xattn_ln1_s': (1.0, 0.6),
     'L0_xattn_ln1_b': (0.0, 0.284),
     'L0_xattn_b_qkv': (0.0, 0.1),
     'L0_xattn_b_ao': (0.0, 0.1),
     'L0_xattn_ln2_s': (1.0, 0.6),
     'L0_xattn_ln2_b': (0.0, 0.8),
     'L0_xattn_b_q': (0.0, 2.0),
     'L0_xattn_b_kv': (0.0, 0.1),
     'L0_xattn_b_co': (0.0, 0.1),
     'L0_xattn_ln3_s': (1.0, 0.2),
     'L0_xattn_ln3_b': (0.0, 0.1),
     'L0_xattn_b1': (0.0, 0.1),
     'L0_xattn_b2': (0.0, 0.1),
     'L2_xattn_ln1_scale': (1.0, 0.6),
     'L2_xattn_ln1_offset': (0.0, 0.8),
     'L2_xattn_bq1': (0.0, 0.8),
     'L2_xattn_bk1': (0.0, 2.0),
     'L2_xattn_bv1': (0.0, 0.1),
     'L2_xattn_bo1': (0.0, 0.1),
     'L2_xattn_ln2_scale': (1.0, 0.6),
     'L2_xattn_ln2_offset': (0.0, 0.8),
     'L2_xattn_bq2': (0.0, 0.8),
     'L2_xattn_bk2': (0.0, 2.0),
     'L2_xattn_bv2': (0.0, 0.1),
     'L2_xattn_bo2': (0.0, 0.1),
     'L2_xattn_ln_mlp_scale': (1.0, 0.6),
     'L2_xattn_ln_mlp_offset': (0.0, 0.8),
     'L2_xattn_b_fc1': (0.0, 0.364),
     'L2_xattn_b_fc2': (0.0, 0.1),
     'L3_xattn_ln1_w': (1.0, 0.6),
     'L3_xattn_ln1_b': (0.0, 0.8),
     'L3_xattn_ln2_w': (1.0, 0.6),
     'L3_xattn_ln2_b': (0.0, 0.8),
     'L3_xattn_gn_w': (1.0, 0.6),
     'L3_xattn_gn_b': (0.0, 0.8)}
    factors = {'L0_xattn_w_q': 8.0,
     'L1_xattn_bm': 64.0,
     'L2_xattn_wq1': 8.0,
     'L2_xattn_wk1': 8.0,
     'L2_xattn_bias_k1': 64.0,
     'L2_xattn_bias_v1': 64.0,
     'L2_xattn_wq2': 8.0,
     'L2_xattn_wk2': 8.0,
     'L2_xattn_bias_k2': 64.0,
     'L2_xattn_bias_v2': 64.0,
     'L3_xattn_maa_x': 8.0,
     'L3_xattn_maa_w1': 8.0,
     'L3_xattn_maa_w2': 8.0,
     'L3_xattn_maa_stack': 4.293,
     'L3_xattn_time_decay': 4.096,
     'L3_xattn_td_w1': 8.0,
     'L3_xattn_td_w2': 8.0,
     'L3_xattn_u': 8.0,
     'L3_xattn_ffn_maa_k': 8.0,
     'L3_xattn_ffn_maa_r': 8.0,
     'L3_xattn_Wfk': 4.393,
     'L3_xattn_Wfr': 8.0,
     'L3_xattn_Wfv': 4.109,
     'L1_xattn_bl': 5.328,
     'L1_xattn_bo': 5.226}
    for name, (base, spread) in spreads.items():
        noise = np.random.default_rng([zlib.crc32(name.encode()), seed]).standard_normal(out[name].shape)
        drawn = base * np.exp(spread * noise) if base else spread * noise
        out[name] = jnp.asarray(drawn.astype(out[name].dtype))
    for name, factor in factors.items():
        out[name] = (out[name] * factor).astype(out[name].dtype)
    return out
```

```python
from contextlib import ExitStack

import concourse.bass as bass
from concourse import mybir

F32 = mybir.dt.float32
ALU = mybir.AluOpType
ACT = mybir.ActivationFunctionType
AX = mybir.AxisListType.X

P = 128
B, S, D = 16, 64, 256
TILES = B * S // P
KD = D // P
STREAMS = 2
ROUNDS = TILES // STREAMS
EPS = 1e-5
MASKED = 10000.0

NH0, HD0 = 16, 16
HB = P // HD0
DIAG = P + 2 * HD0
NH2, HD2 = 16, 128
T2 = S + 1
F = 1024
HS = 8
DM, ND = 32, 5
DD = 64

COLS = [("ln1_s", 2), ("ln1_b", 2), ("bq_self", 2), ("bk_self", 2), ("bv_self", 2), ("ln2_s", 2), ("ln2_b", 2),
        ("bq_cross", 2), ("bk_cross", 2), ("bv_cross", 2), ("ln3_s", 2), ("ln3_b", 2),
        ("bn", 1), ("bm", 1), ("bl", 1), ("bo", 1),
        ("w1_s", 2), ("w1_b", 2), ("w2_s", 2), ("w2_b", 2), ("wm_s", 2), ("wm_b", 2),
        ("r1_w", 2), ("r1_b", 2), ("r2_w", 2), ("r2_b", 2), ("maa_x", 2), ("maa_stack", 10), ("decay", 2),
        ("u", 2), ("ffn_k", 2), ("ffn_r", 2), ("pow", 1)]
COL = {}
for _name, _n in COLS:
    COL[_name] = sum(n for m, n in COLS if m in COL)
NCOL = sum(n for _, n in COLS)
ROWS = ["b_ao", "b_co", "b2", "bo1", "bo2", "b_fc2", "gn_w", "gn_b"]
PACK_A = 3 * KD * P + 5
MLP_A = KD * P + 1


STEPS = {
    "attn0 tensor": [
        "self_turned", "self_qk", "self_v", "self_scores", "self_pT0", "self_pT1", "self_ctx", "self_out",
        "cross_turned", "cross_qk", "cross_v", "cross_scores", "cross_pT0", "cross_pT1", "cross_ctx",
        "cross_out", "mlp_turned"
    ],
    "attn0 scalar": [
        "self_hT", "self_q", "self_v", "self_exp", "self_pT", "self_ctx", "cross_hT", "cross_q", "cross_v",
        "cross_exp", "cross_pT", "cross_ctx", "mlp_hT"
    ],
    "attn0 vector": [
        "self_stats", "self_mv", "self_eps", "self_xn", "self_k", "self_mul", "self_masked", "self_max",
        "self_shifted", "self_psum", "self_rc", "self_p", "self_pT", "self_sum", "cross_stats", "cross_mv",
        "cross_eps", "cross_xn", "cross_k", "cross_mul", "cross_masked", "cross_max", "cross_shifted",
        "cross_psum", "cross_rc", "cross_p", "cross_pT", "cross_sum", "mlp_stats", "mlp_mv", "mlp_eps",
        "mlp_xn"
    ],
    "attn0 gpsimd": ["enc", "self_rstd", "cross_rstd", "mlp_rstd"],
    "mlp0 tensor": ["fc1_0", "fc1_1", "fc2"],
    "mlp0 scalar": ["gelu0", "gelu1"],
    "mlp0 vector": [],
    "mlp0 gpsimd": [],
    "inorm tensor": ["mmm", "scores", "pT0", "pT1", "mo", "out", "n_turned"],
    "inorm scalar": ["mm", "ml", "exp", "pT", "mo", "n_hT"],
    "inorm vector": [
        "x_stats", "x_mv", "x_eps", "x_xn", "c_stats", "c_mv", "c_eps", "c_xn", "max", "neg", "rc", "p", "pT",
        "sum", "n_stats", "n_mv", "n_eps", "n_xn"
    ],
    "inorm gpsimd": ["copy", "x_rstd", "c_rstd", "n_rstd"],
    "heads1 tensor": ["q0", "q1", "k0", "k1", "scores", "v0", "v1", "pT", "ctx", "out"],
    "heads1 scalar": ["q0", "q1", "exp", "v0", "v1", "pT", "ctx"],
    "heads1 vector": ["dv", "k_bias", "k0", "k1", "max", "bw", "shifted", "sum", "rc", "p", "pb", "pT"],
    "heads1 gpsimd": [],
    "close1 tensor": ["bwT", "pbT", "acc"],
    "close1 scalar": [],
    "close1 vector": ["bw", "pb"],
    "close1 gpsimd": [],
    "norm2 tensor": ["n_turned"],
    "norm2 scalar": ["n_hT"],
    "norm2 vector": ["n_stats", "n_mv", "n_eps", "n_xn"],
    "norm2 gpsimd": ["n_rstd"],
    "heads2 tensor": ["q0", "q1", "k0", "k1", "scores", "v0", "v1", "pT", "ctx", "out"],
    "heads2 scalar": ["q0", "q1", "exp", "v0", "v1", "pT", "ctx"],
    "heads2 vector": ["dv", "k_bias", "k0", "k1", "max", "bw", "shifted", "sum", "rc", "p", "pb", "pT"],
    "heads2 gpsimd": [],
    "close2 tensor": ["bwT", "pbT", "acc"],
    "close2 scalar": [],
    "close2 vector": ["bw", "pb"],
    "close2 gpsimd": [],
    "norm3 tensor": ["n_turned"],
    "norm3 scalar": ["n_hT"],
    "norm3 vector": ["n_stats", "n_mv", "n_eps", "n_xn"],
    "norm3 gpsimd": ["n_rstd"],
    "mlp2 tensor": ["fc1_0", "fc1_1", "fc2"],
    "mlp2 scalar": ["gelu0", "gelu1"],
    "mlp2 vector": [],
    "mlp2 gpsimd": [],
    "rwkv tensor": [
        "a_turned", "lora", "mixes", "td1", "rkvg", "td2", "vrep", "o", "ogT", "yT", "wo", "f_turned", "kk",
        "rr", "ffn"
    ],
    "rwkv scalar": ["a_hT", "lora", "td1", "rkv", "g", "ew", "w", "yT", "f_hT", "relu", "kk", "rr"],
    "rwkv vector": [
        "a_stats", "a_mv", "a_eps", "a_xn", "a_sx", "a_mul", "mix", "xm1", "xm2", "xm", "gate", "s0", "av",
        "scan", "rs", "cv", "og", "gsum", "gmean", "cen", "sq", "gsq", "gvar", "y1", "y2", "y3", "y", "x1",
        "f_stats", "f_mv", "f_eps", "f_xn", "f_sx", "f_mul", "mk", "mr1", "mr", "rf", "out"
    ],
    "rwkv gpsimd": ["a_rstd", "rs", "grstd", "f_rstd"],
}


class Steps:

    def __init__(self, sems, names):
        self.sems, self.names, self.seen = sems, names, [0] * len(sems)

    def did(self, name, u):
        assert name == self.names[self.seen[u] % len(self.names)], (name, self.names)
        self.seen[u] += 1
        return self.sems[u], 1

    def at(self, name, u, r):
        return self.sems[u], self.names.index(name) + 1 + r * len(self.names)


class Phase:
    def __init__(self, new_sem, name, orders):
        def steps(engine):
            return Steps([new_sem(f"{name}_{engine}_{u}") for u in range(STREAMS)], orders[f"{name} {engine}"])

        self.pe, self.act, self.vec, self.pool = (steps(e) for e in ("tensor", "scalar", "vector", "gpsimd"))


class Memory:
    pass


def bc(ap, axis, shape):
    return ap.unsqueeze(axis).to_broadcast(shape)




def norm_vec(vec, ph, m, u, r, src, tag, dst=None, stat=0, own=True, reader=None):
    V, G = ph.vec, ph.pool
    st, mv, rs = m.stats[u], m.mv[u], m.rstd[u]
    if own:
        vec.drain()
    vec.bn_stats(st[:, :], src).then_inc(*V.did(tag + "_stats", u))
    vec.drain()
    vec.bn_aggr(mv[:, stat, :], st[:, :]).then_inc(*V.did(tag + "_mv", u))
    vec.wait_ge(*V.at(tag + "_mv", u, r))
    vec.tensor_scalar(rs[:, stat:stat + 1], mv[:, stat, 1:2], EPS, None, ALU.add).then_inc(*V.did(tag + "_eps", u))
    if reader:
        vec.wait_ge(*reader)
    vec.wait_ge(*G.at(tag + "_rstd", u, r))
    vec.tensor_scalar(dst if dst is not None else m.xn[u][:, :], src, mv[:, stat, 0:1], m.rstd2[u][:, stat:stat + 1],
                      ALU.subtract, ALU.mult).then_inc(*V.did(tag + "_xn", u))


def norm_pool(pool, ph, m, u, r, tag, stat=0):
    pool.wait_ge(*ph.vec.at(tag + "_eps", u, r))
    pool.tensor_tensor(m.rstd2[u][:, stat:stat + 1], m.rstd[u][:, stat:stat + 1], m.col("pow"), ALU.pow)\
        .then_inc(*ph.pool.did(tag + "_rstd", u))


def turn_tensor(pe, ph, m, u, r, tag, out, src=None):
    src = (src or m.xn)[u]
    for k in range(KD):
        last = pe.transpose(out[:, k * P:(k + 1) * P], src[:, k * P:(k + 1) * P], m.ident[:, :])
    last.then_inc(*ph.pe.did(tag + "_turned", u))


def turn_act(act, ph, m, u, r, tag, src, dst, scale, shift):
    act.wait_ge(*ph.pe.at(tag + "_turned", u, r))
    for k in range(KD):
        last = act.activation(dst(k), src[:, k * P:(k + 1) * P], ACT.Identity,
                              bias=m.col(shift, k), scale=m.col(scale, k))
    last.then_inc(*ph.act.did(tag + "_hT", u))




ATTN0 = ("self", "cross")


def attn0_tensor(pe, ph, m):
    T, A, V, G = ph.pe, ph.act, ph.vec, ph.pool
    pe.wait_ge(m.s_const, 16 * m.n_const)
    pe.wait_ge(m.s_w0, 80)
    with pe.Fori(0, ROUNDS) as r:
        for kind in ATTN0:
            wq = m.wqkv0[:, :, 0:D] if kind == "self" else m.wq0[:, :, :]
            wk = m.wqkv0[:, :, D:2 * D] if kind == "self" else m.wkv0[:, :, 0:D]
            wv = m.wqkv0[:, :, 2 * D:3 * D] if kind == "self" else m.wkv0[:, :, D:2 * D]
            wo = m.wao0 if kind == "self" else m.wco0
            for u in range(STREAMS):
                pe.wait_ge(*V.at(kind + "_xn", u, r))
                if kind == "self":
                    pe.wait_ge(*G.at("enc", u, r))
                turn_tensor(pe, ph, m, u, r, kind, m.ps[u][:, 3, :])
            for u in range(STREAMS):
                kv = m.hT_s[u] if kind == "self" else m.encT_t[u]
                pe.wait_ge(*A.at(kind + "_hT", u, r))
                for n, (w, x) in enumerate(((wq, m.hT_s[u]), (wk, kv))):
                    for f in range(KD):
                        for k in range(KD):
                            last = pe.matmul(m.ps[u][:, 2 * n, f * P:(f + 1) * P],
                                             w[:, k, f * P:(f + 1) * P], x[:, k, :], start=k == 0, stop=k == KD - 1)
                last.then_inc(*T.did(kind + "_qk", u))
                for b in range(2):
                    for h in range(2):
                        for k in range(KD):
                            last = pe.matmul(m.ps[u][h * S:(h + 1) * S, 1, b * D:(b + 1) * D],
                                             kv[:, k, b * S:(b + 1) * S], wv[:, k, :], start=k == 0, stop=k == KD - 1)
                last.then_inc(*T.did(kind + "_v", u))
            for u in range(STREAMS):
                pe.wait_ge(*A.at(kind + "_q", u, r))
                pe.wait_ge(*V.at(kind + "_k", u, r))
                for f in range(KD):
                    for b in range(2):
                        last = pe.matmul(m.ps[u][b * S:(b + 1) * S, 2 + f, :], m.qT0[u][:, f, b * S:(b + 1) * S],
                                         m.kdiag[u][:, f, b, :, :], start=True, stop=True)
                last.then_inc(*T.did(kind + "_scores", u))
            for u in range(STREAMS):
                pe.wait_ge(*V.at(kind + "_p", u, r))
                pe.wait_ge(*A.at(kind + "_v", u, r))
                for j in range(NH0 // 2):
                    last = pe.transpose(m.ps[u][:, j // 4, (j % 4) * P:(j % 4 + 1) * P],
                                        m.p0[u][:, 2 * j * S:(2 * j + 2) * S], m.ident[:, :])
                    if j % 4 == 3:
                        last.then_inc(*T.did(f"{kind}_pT{j // 4}", u))
            for u in range(STREAMS):
                pe.wait_ge(*A.at(kind + "_pT", u, r))
                pe.wait_ge(*V.at(kind + "_pT", u, r))
                for b in range(2):
                    for f in range(KD):
                        for j in range(4):
                            last = pe.matmul(m.ps[u][:, 2, f * P + b * S:f * P + (b + 1) * S],
                                             m.vdiag[u][:, b, f, j * P:(j + 1) * P],
                                             m.pT0[u][:, 4 * f + j, b * S:(b + 1) * S], start=j == 0, stop=j == 3)
                last.then_inc(*T.did(kind + "_ctx", u))
            for u in range(STREAMS):
                pe.wait_ge(*A.at(kind + "_ctx", u, r))
                pe.matmul(m.ps[u][:, 3, 0:D], m.ones[0:1, :], m.row("b_ao" if kind == "self" else "b_co")[0:1, :],
                          start=True, stop=False)
                for k in range(KD):
                    last = pe.matmul(m.ps[u][:, 3, 0:D], m.cT0[u][:, k, :], wo[:, k, :],
                                     start=False, stop=k == KD - 1)
                last.then_inc(*T.did(kind + "_out", u))
        for u in range(STREAMS):
            pe.wait_ge(*V.at("mlp_xn", u, r))
            turn_tensor(pe, ph, m, u, r, "mlp", m.ps[u][:, 0, :], m.xn_last)


def attn0_scalar(act, ph, m):
    T, A, V, G = ph.pe, ph.act, ph.vec, ph.pool
    act.wait_ge(m.s_const, 16 * m.n_const)
    act.wait_ge(m.s_zero, 1)
    with act.Fori(0, ROUNDS) as r:
        for kind in ATTN0:
            for u in range(STREAMS):
                turn_act(act, ph, m, u, r, kind, m.ps[u][:, 3, :], lambda k: m.hT_s[u][:, k, :],
                         "ln1_s" if kind == "self" else "ln2_s", "ln1_b" if kind == "self" else "ln2_b")
            for u in range(STREAMS):
                act.wait_ge(*T.at(kind + "_qk", u, r))
                for f in range(KD):
                    last = act.activation(m.qT0[u][:, f, :], m.ps[u][:, 0, f * P:(f + 1) * P], ACT.Identity,
                                          bias=m.col("bq_" + kind, f))
                last.then_inc(*A.did(kind + "_q", u))
                act.wait_ge(*T.at(kind + "_v", u, r))
                for b in range(2):
                    for h in range(2):
                        half = slice(h * S, (h + 1) * S)
                        to = m.vdiag[u][half, b, :, :].rearrange("p f (j c) -> p f j c", c=DIAG)
                        last = act.activation(to[:, :, :, h * HD0:(h + 1) * HD0],
                                              m.ps[u][half, 1, b * D:(b + 1) * D].rearrange(
                                                  "p (f j h e) -> p f j h e", f=KD, h=2, e=HD0)[:, :, :, h, :],
                                              ACT.Copy)
                last.then_inc(*A.did(kind + "_v", u))
            for u in range(STREAMS):
                act.wait_ge(*V.at(kind + "_shifted", u, r))
                act.activation(m.p0[u][:, :], m.p0[u][:, :], ACT.Exp).then_inc(*A.did(kind + "_exp", u))
            for u in range(STREAMS):
                act.wait_ge(*T.at(kind + "_pT0", u, r))
                act.activation(m.pT0[u][:, 0:4, :], m.ps[u][:, 0, :], ACT.Copy).then_inc(*A.did(kind + "_pT", u))
            for u in range(STREAMS):
                act.wait_ge(*T.at(kind + "_ctx", u, r))
                for f in range(KD):
                    last = act.activation(m.cT0[u][:, f, :], m.ps[u][:, 2, f * P:(f + 1) * P], ACT.Identity,
                                          bias=m.col("bv_" + kind, f))
                last.then_inc(*A.did(kind + "_ctx", u))
        for u in range(STREAMS):
            turn_act(act, ph, m, u, r, "mlp", m.ps[u][:, 0, :], lambda k: m.hT_of(k, u, r), "ln3_s", "ln3_b")


def attn0_vector(vec, ph, m):
    T, A, V, G = ph.pe, ph.act, ph.vec, ph.pool
    vec.wait_ge(m.s_const, 16 * m.n_const)
    vec.wait_ge(m.s_mask, 48)
    vec.tensor_scalar(m.mask_add["self"][:, :], m.mask_self[:, :], MASKED, -MASKED, ALU.mult, ALU.add)
    vec.tensor_scalar(m.mask_add["cross"][:, :, :], m.mask_cross[:, :, :], MASKED, -MASKED, ALU.mult, ALU.add)
    vec.tensor_scalar(m.mask_mul["self"][:, :], m.mask_self[:, :], HD0 ** -0.5, None, ALU.mult)
    vec.tensor_scalar(m.mask_mul["cross"][:, :, :], m.mask_cross[:, :, :], HD0 ** -0.5, None, ALU.mult)\
        .then_inc(m.s_masks, 1)
    for u in range(STREAMS):
        last = vec.memset(m.vdiag[u][:, :, :, :], 0.0)
    last.then_inc(m.s_zero, 1)
    vec.wait_ge(m.s_masks, 1)
    vec.wait_ge(m.s_x, 16)
    with vec.Fori(0, ROUNDS) as r:
        for kind in ATTN0:
            for u in range(STREAMS):
                norm_vec(vec, ph, m, u, r, m.x_of(u, r), kind)
            for u in range(STREAMS):
                vec.wait_ge(*T.at(kind + "_qk", u, r))
                for f in range(KD):
                    for b in range(2):
                        keys = m.ps[u][:, 2, f * P + b * S:f * P + (b + 1) * S]
                        last = vec.scalar_tensor_tensor(
                            out=m.kdiag[u][:, f, b, :, :], in0=bc(keys, 1, [P, HB, S]),
                            scalar=m.col("bk_" + kind, f), in1=bc(m.headmask[:, :], 2, [P, HB, S]),
                            op0=ALU.add, op1=ALU.mult)
                last.then_inc(*V.did(kind + "_k", u))
            for u in range(STREAMS):
                vec.wait_ge(*T.at(kind + "_scores", u, r))
                s = m.ps[u][:, 2:4, :].rearrange("p g (h t) -> p (g h) t", t=S)
                p = m.p0[u][:, :].rearrange("p (h t) -> p h t", t=S)
                mul, add = ((x[:, :] if kind == "self" else x[:, m.tile(u, r), :])
                            for x in (m.mask_mul[kind], m.mask_add[kind]))
                wide = [P, NH0, S]
                vec.tensor_tensor(p, s, bc(mul, 1, wide), ALU.mult).then_inc(*V.did(kind + "_mul", u))
                vec.wait_ge(*V.at(kind + "_mul", u, r))
                vec.tensor_tensor(p, p, bc(add, 1, wide), ALU.add).then_inc(*V.did(kind + "_masked", u))
                vec.wait_ge(*V.at(kind + "_masked", u, r))
                vec.tensor_reduce(m.mx[u][:, 0:NH0], p, AX, ALU.max).then_inc(*V.did(kind + "_max", u))
                vec.wait_ge(*V.at(kind + "_max", u, r))
                vec.tensor_tensor(p, p, bc(m.mx[u][:, 0:NH0], 2, wide), ALU.subtract)\
                    .then_inc(*V.did(kind + "_shifted", u))
            for u in range(STREAMS):
                p = m.p0[u][:, :].rearrange("p (h t) -> p h t", t=S)
                vec.wait_ge(*A.at(kind + "_exp", u, r))
                vec.tensor_reduce(m.sm[u][:, 0:NH0], p, AX, ALU.add).then_inc(*V.did(kind + "_psum", u))
                vec.wait_ge(*V.at(kind + "_psum", u, r))
                vec.reciprocal(m.rc[u][:, 0:NH0], m.sm[u][:, 0:NH0]).then_inc(*V.did(kind + "_rc", u))
                vec.wait_ge(*V.at(kind + "_rc", u, r))
                vec.tensor_tensor(p, p, bc(m.rc[u][:, 0:NH0], 2, [P, NH0, S]), ALU.mult)\
                    .then_inc(*V.did(kind + "_p", u))
            for u in range(STREAMS):
                vec.wait_ge(*T.at(kind + "_pT1", u, r))
                vec.tensor_copy(m.pT0[u][:, 4:8, :], m.ps[u][:, 1, :].rearrange("p (j q) -> p j q", q=P))\
                    .then_inc(*V.did(kind + "_pT", u))
            for u in range(STREAMS):
                vec.wait_ge(*T.at(kind + "_out", u, r))
                vec.tensor_tensor(m.x_of(u, r), m.ps[u][:, 3, 0:D], m.x_of(u, r), ALU.add)\
                    .then_inc(*V.did(kind + "_sum", u))
        for u in range(STREAMS):
            norm_vec(vec, ph, m, u, r, m.x_of(u, r), "mlp", dst=m.xn_last[u][:, :])


def attn0_gpsimd(pool, ph, m):
    pool.wait_ge(m.s_const, 16 * m.n_const)
    pool.wait_ge(m.s_enc, 16)
    with pool.Fori(0, ROUNDS) as r:
        for u in range(STREAMS):
            pool.wait_ge(*ph.vec.at("self_stats", u, r))
            pool.wait_ge(m.s_enc, 16)
            pool.tensor_copy(m.encT_t[u][:, :, :], m.encT_of(u, r)).then_inc(*ph.pool.did("enc", u))
            norm_pool(pool, ph, m, u, r, "self")
        for kind in ATTN0:
            if kind == "cross":
                for u in range(STREAMS):
                    norm_pool(pool, ph, m, u, r, kind)
        for u in range(STREAMS):
            norm_pool(pool, ph, m, u, r, "mlp")




def start_acc(pe, m, row):
    for u in range(STREAMS):
        for c in range(2):
            pe.matmul(m.ps[u][:, 2 + c, :], m.ones[0:1, :], bc(m.row(row)[0:1, :], 1, [1, 2, D]),
                      start=True, stop=True)


def stream_in(sp, m, ph, pack_a, pack_b, width, rounds, free_a, free_b, before):
    for sem, value in before:
        sp.wait_ge(sem, value)
    for u in range(STREAMS):
        sp.dma_start(m.wa[u][:, 0:width], pack_a[u]).then_inc(m.s_wa[u], 16)
        sp.dma_start(m.wb[u][:, :], pack_b[u]).then_inc(m.s_wb[u], 16)
    with sp.Fori(0, rounds - 1) as r:
        for u in range(STREAMS):
            for steps, name in free_a:
                sp.wait_ge(*steps.at(name, u, r))
            sp.wait_ge(m.s_wa[u], 16)
            sp.dma_start(m.wa[u][:, 0:width], pack_a[2 * r + 2 + u]).then_inc(m.s_wa[u], 16)
        for u in range(STREAMS):
            for steps, name in free_b:
                sp.wait_ge(*steps.at(name, u, r))
            sp.wait_ge(m.s_wb[u], 16)
            sp.dma_start(m.wb[u][:, :], pack_b[2 * r + 2 + u]).then_inc(m.s_wb[u], 16)




def mlp_tensor(pe, ph, m, row, loads, before):
    T, A = ph.pe, ph.act
    for sem, value in before:
        pe.wait_ge(sem, value)
    start_acc(pe, m, row)
    with pe.Fori(0, F // P // 2) as r:
        for u in range(STREAMS):
            pe.wait_ge(m.s_wa[u], 16 * (loads + 1) + r * 16)
            for c in range(2):
                for k in range(KD):
                    last = pe.matmul(m.ps[u][:, c, :], m.wa[u][:, k * P:(k + 1) * P], m.hT[:, k, c * 512:(c + 1) * 512],
                                     start=k == 0, stop=k == KD - 1)
                last.then_inc(*T.did(f"fc1_{c}", u))
        for u in range(STREAMS):
            pe.wait_ge(*A.at("gelu1", u, r))
            pe.wait_ge(m.s_wb[u], 16 * (loads + 1) + r * 16)
            for t in range(TILES):
                last = pe.matmul(m.acc(t), m.g[u][:, t * P:(t + 1) * P], m.wb[u][:, :],
                                 start=False, stop=False, skip_group_check=True)
            last.then_inc(*T.did("fc2", u))


def mlp_scalar(act, ph, m, gelu):
    with act.Fori(0, F // P // 2) as r:
        for u in range(STREAMS):
            for c in range(2):
                act.wait_ge(*ph.pe.at(f"fc1_{c}", u, r))
                act.activation(m.g[u][:, c * 512:(c + 1) * 512], m.ps[u][:, c, :], gelu,
                               bias=m.wa[u][:, KD * P:KD * P + 1]).then_inc(*ph.act.did(f"gelu{c}", u))


def add_acc_vector(vec, m, sem, before):
    for s, value in before:
        vec.wait_ge(s, value)
    for u in range(STREAMS):
        xs = m.x[:, :, :].rearrange("p (r u) d -> p r u d", u=2)[:, :, u, :]
        vec.tensor_tensor(xs, m.ps[u][:, 2:4, :].rearrange("p c (r d) -> p (c r) d", d=D), xs, ALU.add)\
            .then_inc(sem, 1)




def norm_all(eng, which, ph, m, scale, shift, before):
    for sem, value in before:
        eng.wait_ge(sem, value)

    def round_of(r, reader):
        for u in range(STREAMS):
            if which == "vector":
                norm_vec(eng, ph, m, u, r, m.x_of(u, r), "n", reader=reader and ph.act.at("n_hT", u, r - 1))
            elif which == "gpsimd":
                norm_pool(eng, ph, m, u, r, "n")
            elif which == "tensor":
                eng.wait_ge(*ph.vec.at("n_xn", u, r))
                turn_tensor(eng, ph, m, u, r, "n", m.ps[u][:, 1, :])
            else:
                turn_act(eng, ph, m, u, r, "n", m.ps[u][:, 1, :], lambda k: m.hT_of(k, u, r), scale, shift)

    round_of(0, False)
    with eng.Fori(1, ROUNDS) as r:
        round_of(r, True)




def heads_tensor(pe, ph, m, row, loads, before):
    T, A, V = ph.pe, ph.act, ph.vec
    for sem, value in before:
        pe.wait_ge(sem, value)
    start_acc(pe, m, row)
    with pe.Fori(0, NH2 // 2) as r:
        for u in range(STREAMS):
            pe.wait_ge(m.s_wa[u], 16 * (loads + 1) + r * 16)
            for n, x in enumerate((m.hT, m.encT)):
                for c in range(2):
                    if n:
                        pe.wait_ge(*A.at(f"q{c}", u, r))
                    for k in range(KD):
                        last = pe.matmul(m.ps[u][:, c, :], m.wa[u][:, (KD * n + k) * P:(KD * n + k + 1) * P],
                                         x[:, k, c * 512:(c + 1) * 512], start=k == 0, stop=k == KD - 1)
                    last.then_inc(*T.did(f"{'qk'[n]}{c}", u))
        for u in range(STREAMS):
            pe.wait_ge(*V.at("k1", u, r))
            for t in range(TILES):
                for b in range(2):
                    last = pe.matmul(m.ps[u][b * S:(b + 1) * S, t // 4, (t % 4) * T2:(t % 4 + 1) * T2],
                                     m.qT[u][:, t * P + b * S:t * P + (b + 1) * S], m.kT[u][:, t, b, :],
                                     start=True, stop=True)
            pe.wait_ge(m.s_wb[u], 16 * (loads + 1) + r * 16)
            for f in range(KD):
                last = pe.matmul(m.ps[u][:, 1, 300 + f:301 + f], m.wb[u][:, f * P:(f + 1) * P], m.dv[u][:, :],
                                 start=True, stop=True)
            last.then_inc(*T.did("scores", u))
        for u in range(STREAMS):
            pe.wait_ge(*V.at("shifted", u, r))
            for t in range(TILES):
                for k in range(KD):
                    last = pe.matmul(m.ps[u][:, t // 4, (t % 4) * P:(t % 4 + 1) * P], m.encT[:, k, t * P:(t + 1) * P],
                                     m.wa[u][:, (2 * KD + k) * P:(2 * KD + k + 1) * P],
                                     start=k == 0, stop=k == KD - 1)
                if t % 4 == 3:
                    last.then_inc(*T.did(f"v{t // 4}", u))
        for u in range(STREAMS):
            pe.wait_ge(*V.at("p", u, r))
            pe.wait_ge(*A.at("v0", u, r))
            for j in range(TILES // 2):
                last = pe.transpose(m.ps[u][:, 0, j * P:(j + 1) * P], m.pn[u][:, 2 * j:2 * j + 2, :], m.ident[:, :])
            last.then_inc(*T.did("pT", u))
        for u in range(STREAMS):
            pe.wait_ge(*A.at("pT", u, r))
            pe.wait_ge(*V.at("pT", u, r))
            for b in range(2):
                for t in range(TILES):
                    last = pe.matmul(m.ps[u][:, b, t * S:(t + 1) * S], m.v[u][b * S:(b + 1) * S, t, :],
                                     m.pT[u][b * S:(b + 1) * S, t, :], start=True, stop=True)
            last.then_inc(*T.did("ctx", u))
        for u in range(STREAMS):
            pe.wait_ge(*A.at("ctx", u, r))
            for t in range(TILES):
                last = pe.matmul(m.acc(t), m.cT[u][:, t, :, :], m.wb[u][:, :],
                                 start=False, stop=False, skip_group_check=True)
            last.then_inc(*T.did("out", u))


def heads_scalar(act, ph, m):
    T, A, V = ph.pe, ph.act, ph.vec
    with act.Fori(0, NH2 // 2) as r:
        for u in range(STREAMS):
            for c in range(2):
                act.wait_ge(*T.at(f"q{c}", u, r))
                act.activation(m.qT[u][:, c * 512:(c + 1) * 512], m.ps[u][:, c, :], ACT.Identity,
                               bias=m.head_col(u, 0)).then_inc(*A.did(f"q{c}", u))
        for u in range(STREAMS):
            act.wait_ge(*V.at("shifted", u, r))
            act.activation(m.p[u][:, :, :], m.p[u][:, :, :], ACT.Exp, scale=HD2 ** -0.5).then_inc(*A.did("exp", u))
        for u in range(STREAMS):
            for c in range(2):
                act.wait_ge(*T.at(f"v{c}", u, r))
                act.activation(m.v[u][:, 4 * c:4 * c + 4, :], m.ps[u][:, c, :], ACT.Copy)\
                    .then_inc(*A.did(f"v{c}", u))
        for u in range(STREAMS):
            act.wait_ge(*T.at("pT", u, r))
            turn_probs(lambda o, i: act.activation(o, i, ACT.Copy), m, u, 0).then_inc(*A.did("pT", u))
        for u in range(STREAMS):
            act.wait_ge(*T.at("ctx", u, r))
            for b in range(2):
                last = act.activation(m.cT[u][:, :, b, :], m.ps[u][:, b, :].rearrange("p (t q) -> p t q", q=S),
                                      ACT.Identity, bias=m.head_col(u, 2))
            last.then_inc(*A.did("ctx", u))


def turn_probs(copy, m, u, odd):
    src = m.ps[u][:, 0, :].rearrange("p (j b q) -> p j b q", b=2, q=S)
    for b in range(2):
        dst = m.pT[u][b * S:(b + 1) * S, :, :].rearrange("p (j o) q -> p j o q", o=2)
        last = copy(dst[:, :, odd, :], src[odd * S:(odd + 1) * S, :, b, :])
    return last


def heads_vector(vec, ph, m, loads):
    T, A, V = ph.pe, ph.act, ph.vec
    with vec.Fori(0, NH2 // 2) as r:
        for u in range(STREAMS):
            vec.wait_ge(m.s_wa[u], 16 * (loads + 1) + r * 16)
            vec.tensor_tensor(m.dv[u][:, :], m.head_col(u, 4), m.head_col(u, 2), ALU.subtract)\
                .then_inc(*V.did("dv", u))
            for c in range(2):
                vec.wait_ge(*T.at(f"k{c}", u, r))
                if c == 0:
                    vec.tensor_copy(m.kT[u][:, :, :, S], bc(m.head_col(u, 3), 1, [P, TILES, 2])).then_inc(
                        *V.did("k_bias", u))
                vec.tensor_scalar(m.kT[u][:, 4 * c:4 * c + 4, :, 0:S],
                                  m.ps[u][:, c, :].rearrange("p (t b k) -> p t b k", b=2, k=S),
                                  m.head_col(u, 1), None, ALU.add).then_inc(*V.did(f"k{c}", u))
        for u in range(STREAMS):
            s = m.ps[u][:, 0:2, 0:4 * T2].rearrange("p c (t k) -> p c t k", k=T2)
            p = m.p[u][:, :, :].rearrange("p (c t) k -> p c t k", c=2)
            mx = m.mx[u][:, 0:TILES].rearrange("p (c t) -> p c t", c=2)
            vec.wait_ge(*T.at("scores", u, r))
            vec.tensor_reduce(mx, s, AX, ALU.max).then_inc(*V.did("max", u))
            vec.tensor_scalar(m.bwT[:, :, bass.ds(2 * r + u, 1)], bc(m.ps[u][:, 1, 300:302], 2, [P, 2, 1]),
                              1.0, None, ALU.mult).then_inc(*V.did("bw", u))
            vec.wait_ge(*V.at("max", u, r))
            vec.tensor_tensor(p, s, bc(mx, 3, [P, 2, 4, T2]), ALU.subtract).then_inc(*V.did("shifted", u))
        for u in range(STREAMS):
            p = m.p[u][:, :, :]
            vec.wait_ge(*A.at("exp", u, r))
            vec.tensor_reduce(m.sm[u][:, 0:TILES], p, AX, ALU.add).then_inc(*V.did("sum", u))
            vec.wait_ge(*V.at("sum", u, r))
            vec.reciprocal(m.rc[u][:, 0:TILES], m.sm[u][:, 0:TILES]).then_inc(*V.did("rc", u))
            vec.wait_ge(*V.at("rc", u, r))
            vec.tensor_tensor(m.pn[u][:, :, :], p[:, :, 0:S], bc(m.rc[u][:, 0:TILES], 2, [P, TILES, S]), ALU.mult)\
                .then_inc(*V.did("p", u))
            vec.tensor_tensor(m.pb[:, :, bass.ds(2 * r + u, 1)], p[:, :, S:T2],
                              m.rc[u][:, 0:TILES].unsqueeze(2), ALU.mult).then_inc(*V.did("pb", u))
        for u in range(STREAMS):
            vec.wait_ge(*T.at("pT", u, r))
            turn_probs(vec.tensor_copy, m, u, 1).then_inc(*V.did("pT", u))


def bias_token_tensor(pe, ph, cl, m):
    V = ph.vec
    for u in range(STREAMS):
        pe.wait_ge(*V.at("pT", u, NH2 // 2 - 1))
    for f in range(KD):
        last = pe.transpose(m.ps[0][0:NH2, 0, f * P:(f + 1) * P], m.bwT[:, f, :], m.ident[:, :])
    last.then_inc(*cl.pe.did("bwT", 0))
    for t in range(TILES):
        last = pe.transpose(m.ps[1][0:NH2, t // 4, (t % 4) * P:(t % 4 + 1) * P], m.pb[:, t, :], m.ident[:, :])
    last.then_inc(*cl.pe.did("pbT", 0))
    pe.wait_ge(*cl.vec.at("bw", 0, 0))
    pe.wait_ge(*cl.vec.at("pb", 0, 0))
    for t in range(TILES):
        last = pe.matmul(m.acc(t), m.pbT[:, t * P:(t + 1) * P], m.bw[:, :], start=False, stop=False,
                         skip_group_check=True)
    last.then_inc(*cl.pe.did("acc", 0))


def bias_token_vector(vec, cl, m):
    vec.wait_ge(*cl.pe.at("bwT", 0, 0))
    vec.tensor_copy(m.bw[:, :], m.ps[0][0:NH2, 0, 0:D]).then_inc(*cl.vec.did("bw", 0))
    vec.wait_ge(*cl.pe.at("pbT", 0, 0))
    vec.tensor_copy(m.pbT[:, :], m.ps[1][0:NH2, 0:2, :].rearrange("p c n -> p (c n)")).then_inc(*cl.vec.did("pb", 0))




def inorm_tensor(pe, ph, m, before):
    T, A, V, G = ph.pe, ph.act, ph.vec, ph.pool
    for sem, value in before:
        pe.wait_ge(sem, value)
    with pe.Fori(0, ROUNDS) as r:
        for u in range(STREAMS):
            pe.wait_ge(*V.at("c_xn", u, r))
            pe.wait_ge(*G.at("copy", u, r))
            for n, x in enumerate((m.xn[u], m.cn[u])):
                last = pe.matmul(m.ps[u][:, 0, n * D:(n + 1) * D], m.w1x1[:, n, :], x[:, :], start=True, stop=True)
            for c in range(2):
                last = pe.matmul(m.ps[u][:, 1, c * P:(c + 1) * P], m.ctx_t[u][:, c * P:(c + 1) * P], m.w1x1[:, 2, :],
                                 start=True, stop=True)
            last.then_inc(*T.did("mmm", u))
        for u in range(STREAMS):
            pe.wait_ge(*A.at("mm", u, r))
            for b in range(2):
                half = slice(b * S, (b + 1) * S)
                for c in range(2):
                    last = pe.matmul(m.ps[u][:, 2 + b, c * D:(c + 1) * D], m.mnm[u][half, c * P:(c + 1) * P],
                                     m.mnm[u][half, D:2 * D], start=True, stop=True)
            last.then_inc(*T.did("scores", u))
        for u in range(STREAMS):
            pe.wait_ge(*V.at("p", u, r))
            pe.wait_ge(*A.at("ml", u, r))
            for b in range(2):
                for s in range(2):
                    for c in range(2):
                        last = pe.transpose(m.ps[u][:, b, s * D + c * P:s * D + (c + 1) * P],
                                            m.p1[u][:, 2 * b + c, s * P:(s + 1) * P], m.ident[:, :])
                last.then_inc(*T.did(f"pT{b}", u))
        for u in range(STREAMS):
            for b in range(2):
                pe.wait_ge(*(A, V)[b].at("pT", u, r))
                for s in range(2):
                    last = pe.matmul(m.ps[u][b * S:(b + 1) * S, 2, 0:D], m.mlT[u][:, s, b * S:(b + 1) * S],
                                     m.p1T[u][:, b, s * D:(s + 1) * D], start=s == 0, stop=s == 1)
            last.then_inc(*T.did("mo", u))
        for u in range(STREAMS):
            pe.wait_ge(*A.at("mo", u, r))
            pe.matmul(m.ps[u][:, 3, 0:D], m.w1x1[:, 3, :], m.mo[u][:, :], start=True, stop=True)\
                .then_inc(*T.did("out", u))
        for u in range(STREAMS):
            pe.wait_ge(*V.at("n_xn", u, r))
            turn_tensor(pe, ph, m, u, r, "n", m.ps[u][:, 3, :], m.xn_last)


def inorm_scalar(act, ph, m):
    T, A, V, G = ph.pe, ph.act, ph.vec, ph.pool
    with act.Fori(0, ROUNDS) as r:
        for u in range(STREAMS):
            act.wait_ge(*T.at("mmm", u, r))
            for n, bias in enumerate(("bn", "bm")):
                last = act.activation(m.mnm[u][:, n * D:(n + 1) * D], m.ps[u][:, 0, n * D:(n + 1) * D], ACT.Identity,
                                      bias=m.col(bias))
            last.then_inc(*A.did("mm", u))
            act.activation(m.mlT[u][:, :, :], m.ps[u][:, 1, 0:2 * P], ACT.Copy).then_inc(*A.did("ml", u))
        for u in range(STREAMS):
            act.wait_ge(*V.at("neg", u, r))
            for n in range(4):
                last = act.activation(m.p1[u][:, n, :], m.ps[u][:, 2 + n // 2, (n % 2) * D:(n % 2 + 1) * D], ACT.Exp,
                                      bias=m.mx[u][:, n:n + 1], accum_out=m.sm[u][:, n:n + 1])
            last.then_inc(*A.did("exp", u))
        for u in range(STREAMS):
            act.wait_ge(*T.at("pT0", u, r))
            act.activation(m.p1T[u][:, 0, :], m.ps[u][:, 0, :], ACT.Copy).then_inc(*A.did("pT", u))
        for u in range(STREAMS):
            act.wait_ge(*T.at("mo", u, r))
            act.activation(m.mo[u][:, :], m.ps[u][:, 2, 0:D], ACT.Identity, bias=m.col("bl"))\
                .then_inc(*A.did("mo", u))
        for u in range(STREAMS):
            turn_act(act, ph, m, u, r, "n", m.ps[u][:, 3, :], lambda k: m.hT_of(k, u, r), "w1_s", "w1_b")


def inorm_vector(vec, ph, m, before):
    T, A, V, G = ph.pe, ph.act, ph.vec, ph.pool
    for sem, value in before:
        vec.wait_ge(sem, value)
    with vec.Fori(0, ROUNDS) as r:
        for u in range(STREAMS):
            norm_vec(vec, ph, m, u, r, m.x_of(u, r), "x")
            vec.wait_ge(*G.at("copy", u, r))
            norm_vec(vec, ph, m, u, r, m.ctx_t[u][:, :], "c", dst=m.cn[u][:, :], stat=1, own=False)
        for u in range(STREAMS):
            s = m.ps[u][:, 2:4, :].rearrange("p b (c s) -> p (b c) s", c=2)
            vec.wait_ge(*T.at("scores", u, r))
            vec.tensor_reduce(m.rc[u][:, 0:4], s, AX, ALU.max).then_inc(*V.did("max", u))
            vec.wait_ge(*V.at("max", u, r))
            vec.tensor_scalar(m.mx[u][:, 0:4], m.rc[u][:, 0:4], -1.0, None, ALU.mult).then_inc(*V.did("neg", u))
        for u in range(STREAMS):
            vec.wait_ge(*A.at("exp", u, r))
            vec.reciprocal(m.rc[u][:, 0:4], m.sm[u][:, 0:4]).then_inc(*V.did("rc", u))
            vec.wait_ge(*V.at("rc", u, r))
            vec.tensor_tensor(m.p1[u][:, :, :], m.p1[u][:, :, :], bc(m.rc[u][:, 0:4], 2, [P, 4, D]), ALU.mult)\
                .then_inc(*V.did("p", u))
        for u in range(STREAMS):
            vec.wait_ge(*T.at("pT1", u, r))
            vec.tensor_copy(m.p1T[u][:, 1, :], m.ps[u][:, 1, :]).then_inc(*V.did("pT", u))
        for u in range(STREAMS):
            vec.wait_ge(*T.at("out", u, r))
            vec.scalar_tensor_tensor(out=m.x_of(u, r), in0=m.ps[u][:, 3, 0:D], scalar=m.col("bo"), in1=m.x_of(u, r),
                                     op0=ALU.add, op1=ALU.add).then_inc(*V.did("sum", u))
        for u in range(STREAMS):
            norm_vec(vec, ph, m, u, r, m.x_of(u, r), "n", dst=m.xn_last[u][:, :])


def inorm_gpsimd(pool, ph, m, before):
    for sem, value in before:
        pool.wait_ge(sem, value)
    with pool.Fori(0, ROUNDS) as r:
        for u in range(STREAMS):
            pool.wait_ge(*ph.vec.at("x_stats", u, r))
            pool.wait_ge(m.s_enc, 16)
            pool.tensor_copy(m.ctx_t[u][:, :], m.ctx_of(u, r)).then_inc(*ph.pool.did("copy", u))
            norm_pool(pool, ph, m, u, r, "x")
            norm_pool(pool, ph, m, u, r, "c", stat=1)
        for u in range(STREAMS):
            norm_pool(pool, ph, m, u, r, "n")




MIX_K, MIX_W, MIX_V, MIX_R, MIX_G = range(ND)
W_R, W_K, W_V, W_G, W_O, W_FK, W_FR, W_FV = range(8)


def rwkv_tensor(pe, ph, m, before):
    T, A, V, G = ph.pe, ph.act, ph.vec, ph.pool
    for sem, value in before:
        pe.wait_ge(sem, value)

    def product(out, lhsT, rhs):
        for k in range(KD):
            last = pe.matmul(out, lhsT(k), rhs(k), start=k == 0, stop=k == KD - 1)
        return last

    with pe.Fori(0, ROUNDS) as r:
        for u in range(STREAMS):
            pe.wait_ge(*V.at("a_xn", u, r))
            turn_tensor(pe, ph, m, u, r, "a", m.ps[u][:, 0, :])
        for u in range(STREAMS):
            pe.wait_ge(*V.at("mix", u, r))
            product(m.ps[u][:, 0, 0:P], lambda k: m.maa_w1[:, k, 0:P], lambda k: m.mix[u][:, k, :])
            product(m.ps[u][0:DM, 0, P:2 * P], lambda k: m.maa_w1[:, k, P:ND * DM], lambda k: m.mix[u][:, k, :])\
                .then_inc(*T.did("lora", u))
        for u in range(STREAMS):
            pe.wait_ge(*A.at("lora", u, r))
            for f in range(ND):
                for e in range(KD):
                    n = KD * f + e
                    out = m.ps[u][:, 1 + n // 4, (n % 4) * P:(n % 4 + 1) * P]
                    if f < 4:
                        pe.matmul(out, m.maa_w2[:, f, e * P:(e + 1) * P], m.xx[u][:, 0:P], start=True, stop=True)
                    else:
                        last = pe.matmul(out, m.maa_w2l[:, e * P:(e + 1) * P], m.xx[u][0:DM, P:2 * P],
                                         start=True, stop=True)
            last.then_inc(*T.did("mixes", u))
        for u in range(STREAMS):
            pe.wait_ge(*V.at("xm", u, r))
            xm = lambda f, k: m.xm[u][:, KD * f + k, :]
            product(m.ps[u][0:DD, 0, 0:P], lambda k: m.td_w1[:, k, :], lambda k: xm(MIX_W, k))\
                .then_inc(*T.did("td1", u))
            for n, (w, f) in enumerate(((W_R, MIX_R), (W_K, MIX_K), (W_V, MIX_V))):
                for e in range(KD):
                    last = product(m.ps[u][:, 1 + n // 2, (n % 2) * D + e * P:(n % 2) * D + (e + 1) * P],
                                   lambda k: m.wr[:, w, k, e * P:(e + 1) * P], lambda k: xm(f, k))
            product(m.ps[u][:, 2, D:2 * D], lambda k: xm(MIX_G, k), lambda k: m.wr[:, W_G, k, :])\
                .then_inc(*T.did("rkvg", u))
            pe.wait_ge(*A.at("td1", u, r))
            for e in range(KD):
                last = pe.matmul(m.ps[u][:, 3, e * P:(e + 1) * P], m.td_w2[:, e * P:(e + 1) * P], m.td[u][:, :],
                                 start=True, stop=True)
            last.then_inc(*T.did("td2", u))
        for u in range(STREAMS):
            pe.wait_ge(*A.at("ew", u, r))
            pe.wait_ge(*V.at("gate", u, r))
            for j in range(HS):
                last = pe.matmul(m.ps[u][:, j // 2, (j % 2) * D:(j % 2 + 1) * D], m.sel[:, j, :], m.rkv[u][:, 2, :],
                                 start=True, stop=True)
            last.then_inc(*T.did("vrep", u))
        for u in range(STREAMS):
            pe.wait_ge(*V.at("rs", u, r))
            pe.wait_ge(*G.at("rs", u, r))
            for j in range(HS):
                pe.matmul(m.ps[u][:, 0, 0:D], m.gather[:, j, :], m.sc[u][:, j, :], start=j == 0, stop=j == HS - 1)
            pe.matmul(m.ps[u][:, 1, 0:D], m.headsum[:, :], m.ruk[u][:, :], start=True, stop=True)\
                .then_inc(*T.did("o", u))
        for u in range(STREAMS):
            pe.wait_ge(*V.at("og", u, r))
            for e in range(KD):
                last = pe.transpose(m.ps[u][:, 2, e * P:(e + 1) * P], m.og[u][:, e * P:(e + 1) * P], m.ident[:, :])
            last.then_inc(*T.did("ogT", u))
        for u in range(STREAMS):
            pe.wait_ge(*V.at("y", u, r))
            for e in range(KD):
                last = pe.transpose(m.ps[u][:, 3, e * P:(e + 1) * P], m.tok[u][:, e * P:(e + 1) * P], m.ident[:, :])
            last.then_inc(*T.did("yT", u))
        for u in range(STREAMS):
            pe.wait_ge(*A.at("yT", u, r))
            product(m.ps[u][:, 0, 0:D], lambda k: m.yT[u][:, k, :], lambda k: m.wr[:, W_O, k, :])\
                .then_inc(*T.did("wo", u))
        for u in range(STREAMS):
            pe.wait_ge(*V.at("f_xn", u, r))
            turn_tensor(pe, ph, m, u, r, "f", m.ps[u][:, 1, :])
        for u in range(STREAMS):
            pe.wait_ge(*V.at("mk", u, r))
            for e in range(KD):
                last = product(m.ps[u][:, 2, e * P:(e + 1) * P], lambda k: m.wr[:, W_FK, k, e * P:(e + 1) * P],
                               lambda k: m.mk[u][:, k, :])
            last.then_inc(*T.did("kk", u))
            pe.wait_ge(*V.at("mr", u, r))
            product(m.ps[u][:, 3, 0:D], lambda k: m.mr[u][:, k, :], lambda k: m.wr[:, W_FR, k, :])\
                .then_inc(*T.did("rr", u))
        for u in range(STREAMS):
            pe.wait_ge(*A.at("kk", u, r))
            product(m.ps[u][:, 0, 0:D], lambda k: m.kk[u][:, k * P:(k + 1) * P], lambda k: m.wr[:, W_FV, k, :])\
                .then_inc(*T.did("ffn", u))


def rwkv_scalar(act, ph, m):
    T, A, V, G = ph.pe, ph.act, ph.vec, ph.pool
    act.wait_ge(m.s_zero, 2)
    with act.Fori(0, ROUNDS) as r:
        for u in range(STREAMS):
            turn_act(act, ph, m, u, r, "a", m.ps[u][:, 0, :], lambda k: m.xa[u][:, k, :], "r1_w", "r1_b")
        for u in range(STREAMS):
            act.wait_ge(*T.at("lora", u, r))
            act.activation(m.xx[u][:, 0:P], m.ps[u][:, 0, 0:P], ACT.Tanh)
            act.activation(m.xx[u][0:DM, P:2 * P], m.ps[u][0:DM, 0, P:2 * P], ACT.Tanh).then_inc(*A.did("lora", u))
        for u in range(STREAMS):
            act.wait_ge(*T.at("td1", u, r))
            act.activation(m.td[u][:, :], m.ps[u][0:DD, 0, 0:P], ACT.Tanh).then_inc(*A.did("td1", u))
            act.wait_ge(*T.at("rkvg", u, r))
            act.activation(m.rkv[u][:, :, :], m.ps[u][:, 1:3, :].rearrange("p c n -> p (c n)")[:, 0:3 * D], ACT.Copy)\
                .then_inc(*A.did("rkv", u))
            act.activation(m.th[u][:, :], m.ps[u][:, 2, D:2 * D], ACT.Tanh, scale=0.5).then_inc(*A.did("g", u))
            act.wait_ge(*T.at("td2", u, r))
            for e in range(KD):
                last = act.activation(m.ew[u][:, e * P:(e + 1) * P], m.ps[u][:, 3, e * P:(e + 1) * P], ACT.Exp,
                                      bias=m.col("decay", e))
            last.then_inc(*A.did("ew", u))
            act.wait_ge(*A.at("ew", u, r))
            act.activation(m.wS[u][:, :, 1:S], m.ew[u][:, :].rearrange("p (n s) -> p n s", s=S)[:, :, 0:S - 1],
                           ACT.Exp, scale=-1.0).then_inc(*A.did("w", u))
        for u in range(STREAMS):
            act.wait_ge(*T.at("yT", u, r))
            act.activation(m.yT[u][:, :, :], m.ps[u][:, 3, 0:D], ACT.Copy).then_inc(*A.did("yT", u))
        for u in range(STREAMS):
            turn_act(act, ph, m, u, r, "f", m.ps[u][:, 1, :], lambda k: m.xa[u][:, k, :], "r2_w", "r2_b")
        for u in range(STREAMS):
            act.wait_ge(*T.at("kk", u, r))
            act.activation(m.kr[u][:, :], m.ps[u][:, 2, 0:D], ACT.Relu).then_inc(*A.did("relu", u))
            act.wait_ge(*A.at("relu", u, r))
            act.activation(m.kk[u][:, :], m.kr[u][:, :], ACT.Square).then_inc(*A.did("kk", u))
            act.wait_ge(*T.at("rr", u, r))
            act.activation(m.th[u][:, :], m.ps[u][:, 3, 0:D], ACT.Tanh, scale=0.5).then_inc(*A.did("rr", u))


def rwkv_shift(vec, V, m, u, r, tag, state):
    xa = m.xa[u][:, :, :].rearrange("p k (b s) -> p k b s", b=2)
    sx = m.sx[u][:, :, :].rearrange("p k (b s) -> p k b s", b=2)
    first = m.encT_of(u, r).rearrange("p k (b s) -> p k b s", b=2)[:, :, :, state:state + 1]
    vec.tensor_tensor(sx[:, :, :, 1:S], xa[:, :, :, 0:S - 1], xa[:, :, :, 1:S], ALU.subtract)
    vec.tensor_tensor(sx[:, :, :, 0:1], first, xa[:, :, :, 0:1], ALU.subtract).then_inc(*V.did(tag + "_sx", u))


def rwkv_mix(vec, V, m, u, r, tag, dst, factor):
    vec.wait_ge(*V.at(tag + "_sx", u, r))
    vec.tensor_tensor(dst[:, :, :], m.sx[u][:, :, :], bc(factor, 2, [P, KD, P]), ALU.mult)\
        .then_inc(*V.did(f"{tag}_mul", u))
    vec.wait_ge(*V.at(f"{tag}_mul", u, r))
    return vec.tensor_tensor(dst[:, :, :], dst[:, :, :], m.xa[u][:, :, :], ALU.add)


def rwkv_vector(vec, ph, m, before):
    T, A, V, G = ph.pe, ph.act, ph.vec, ph.pool
    for sem, value in before:
        vec.wait_ge(sem, value)
    for u in range(STREAMS):
        vec.memset(m.wS[u][:, :, 0:1], 0.0)
    vec.tensor_scalar(m.gn_w[:, :], m.row("gn_w"), 0.5, None, ALU.mult)
    vec.tensor_scalar(m.gn_b[:, :], m.row("gn_b"), 0.5, None, ALU.mult).then_inc(m.s_zero, 1)
    vec.wait_ge(m.s_zero, 2)
    with vec.Fori(0, ROUNDS) as r:
        for u in range(STREAMS):
            norm_vec(vec, ph, m, u, r, m.x_of(u, r), "a")
        for u in range(STREAMS):
            vec.wait_ge(*A.at("a_hT", u, r))
            rwkv_shift(vec, V, m, u, r, "a", 1)
            rwkv_mix(vec, V, m, u, r, "a", m.mix[u], m.cols("maa_x")).then_inc(*V.did("mix", u))
        for u in range(STREAMS):
            vec.wait_ge(*T.at("mixes", u, r))
            xm = m.xm[u][:, :, :]
            wide = m.xm[u][:, :, :].rearrange("p (f k) t -> p f (k t)", k=KD)
            flat = lambda x: bc(x[u][:, :, :].rearrange("p k t -> p (k t)"), 1, [P, ND, D])
            vec.tensor_tensor(xm, m.ps[u][:, 1:4, :].rearrange("p c (n t) -> p (c n) t", t=P)[:, 0:ND * KD, :],
                              bc(m.cols("maa_stack"), 2, [P, ND * KD, P]), ALU.add).then_inc(*V.did("xm1", u))
            vec.wait_ge(*V.at("xm1", u, r))
            vec.tensor_tensor(wide, wide, flat(m.sx), ALU.mult).then_inc(*V.did("xm2", u))
            vec.wait_ge(*V.at("xm2", u, r))
            vec.tensor_tensor(wide, wide, flat(m.xa), ALU.add).then_inc(*V.did("xm", u))
        for u in range(STREAMS):
            vec.wait_ge(*A.at("rkv", u, r))
            for e in range(KD):
                part = slice(e * P, (e + 1) * P)
                vec.scalar_tensor_tensor(out=m.ruk[u][:, part], in0=m.rkv[u][:, 0, part], scalar=m.col("u", e),
                                         in1=m.rkv[u][:, 1, part], op0=ALU.mult, op1=ALU.mult)
            vec.wait_ge(*A.at("g", u, r))
            vec.scalar_tensor_tensor(out=m.gate[u][:, :], in0=m.th[u][:, :], scalar=1.0, in1=m.ps[u][:, 2, D:2 * D],
                                     op0=ALU.add, op1=ALU.mult).then_inc(*V.did("gate", u))
            vec.tensor_scalar(m.av[u][:, :, :, 0:1], m.s0[:, m.tile(u, r), :].rearrange(
                "p (j n o) -> p j n o", n=4, o=1), 1.0, None, ALU.mult).then_inc(*V.did("s0", u))
        for u in range(STREAMS):
            vec.wait_ge(*T.at("vrep", u, r))
            keys = m.rkv[u][:, 1, :].rearrange("p (n s) -> p n s", s=S)[:, :, 0:S - 1]
            vals = m.ps[u][:, :, :].rearrange("p c (j n s) -> p (c j) n s", j=2, s=S)[:, :, :, 0:S - 1]
            vec.tensor_tensor(m.av[u][:, :, :, 1:S], vals, bc(keys, 1, [P, HS, 4, S - 1]), ALU.mult)\
                .then_inc(*V.did("av", u))
            vec.wait_ge(*V.at("av", u, r))
            vec.wait_ge(*A.at("w", u, r))
            for j in range(HS):
                last = vec.tensor_tensor_scan(m.sc[u][:, j, :], m.wS[u][:, :, :].rearrange("p n s -> p (n s)"),
                                              m.av[u][:, j, :, :].rearrange("p n s -> p (n s)"), 0.0,
                                              ALU.mult, ALU.add)
            last.then_inc(*V.did("scan", u))
            vec.wait_ge(*V.at("scan", u, r))
            vec.tensor_tensor(m.sc[u][:, 0:m.vj, :], m.sc[u][:, 0:m.vj, :],
                              bc(m.rkv[u][:, 0, :], 1, [P, m.vj, D]), ALU.mult).then_inc(*V.did("rs", u))
        for u in range(STREAMS):
            vec.wait_ge(*T.at("o", u, r))
            vec.tensor_tensor(m.og[u][:, :], m.ps[u][:, 1, 0:D], m.rkv[u][:, 2, :], ALU.mult)\
                .then_inc(*V.did("cv", u))
            vec.wait_ge(*V.at("cv", u, r))
            vec.tensor_tensor(m.og[u][:, :], m.ps[u][:, 0, 0:D], m.og[u][:, :], ALU.add).then_inc(*V.did("og", u))
        for u in range(STREAMS):
            head = lambda x: x.rearrange("p (h j) -> p h j", j=HS)
            tok, n = m.tok[u][:, :], D // HS
            vec.wait_ge(*T.at("ogT", u, r))
            vec.tensor_reduce(m.mx[u][:, 0:n], head(m.ps[u][:, 2, 0:D]), AX, ALU.add).then_inc(*V.did("gsum", u))
            vec.wait_ge(*V.at("gsum", u, r))
            vec.tensor_scalar(m.mx[u][:, 0:n], m.mx[u][:, 0:n], 1.0 / HS, None, ALU.mult).then_inc(*V.did("gmean", u))
            vec.wait_ge(*V.at("gmean", u, r))
            vec.tensor_tensor(head(tok), head(m.ps[u][:, 2, 0:D]), bc(m.mx[u][:, 0:n], 2, [P, n, HS]), ALU.subtract)\
                .then_inc(*V.did("cen", u))
            vec.wait_ge(*V.at("cen", u, r))
            vec.tensor_tensor(m.sq[u][:, :], tok, tok, ALU.mult).then_inc(*V.did("sq", u))
            vec.wait_ge(*V.at("sq", u, r))
            vec.tensor_reduce(m.sm[u][:, 0:n], head(m.sq[u][:, :]), AX, ALU.add).then_inc(*V.did("gsq", u))
            vec.wait_ge(*V.at("gsq", u, r))
            vec.tensor_scalar(m.sm[u][:, 0:n], m.sm[u][:, 0:n], 1.0 / HS, EPS, ALU.mult, ALU.add)\
                .then_inc(*V.did("gvar", u))
        for u in range(STREAMS):
            tok, n = m.tok[u][:, :], D // HS
            vec.wait_ge(*G.at("grstd", u, r))
            vec.tensor_tensor(head(tok), head(tok), bc(m.rc[u][:, 0:n], 2, [P, n, HS]), ALU.mult)\
                .then_inc(*V.did("y1", u))
            vec.wait_ge(*V.at("y1", u, r))
            vec.tensor_tensor(tok, tok, m.gn_w[:, :], ALU.mult).then_inc(*V.did("y2", u))
            vec.wait_ge(*V.at("y2", u, r))
            vec.tensor_tensor(tok, tok, m.gn_b[:, :], ALU.add).then_inc(*V.did("y3", u))
            vec.wait_ge(*V.at("y3", u, r))
            vec.tensor_tensor(tok, tok, m.gate[u][:, :], ALU.mult).then_inc(*V.did("y", u))
        for u in range(STREAMS):
            vec.wait_ge(*T.at("wo", u, r))
            vec.tensor_tensor(m.x_of(u, r), m.ps[u][:, 0, 0:D], m.x_of(u, r), ALU.add).then_inc(*V.did("x1", u))
            norm_vec(vec, ph, m, u, r, m.x_of(u, r), "f")
        for u in range(STREAMS):
            vec.wait_ge(*A.at("f_hT", u, r))
            rwkv_shift(vec, V, m, u, r, "f", 0)
            rwkv_mix(vec, V, m, u, r, "f", m.mk[u], m.cols("ffn_k")).then_inc(*V.did("mk", u))
            vec.tensor_tensor(m.mr[u][:, :, :], m.sx[u][:, :, :], bc(m.cols("ffn_r"), 2, [P, KD, P]), ALU.mult)\
                .then_inc(*V.did("mr1", u))
            vec.wait_ge(*V.at("mr1", u, r))
            vec.tensor_tensor(m.mr[u][:, :, :], m.mr[u][:, :, :], m.xa[u][:, :, :], ALU.add).then_inc(*V.did("mr", u))
        for u in range(STREAMS):
            vec.wait_ge(*A.at("rr", u, r))
            vec.wait_ge(*T.at("ffn", u, r))
            vec.scalar_tensor_tensor(out=m.tok[u][:, :], in0=m.th[u][:, :], scalar=1.0, in1=m.ps[u][:, 0, 0:D],
                                     op0=ALU.add, op1=ALU.mult).then_inc(*V.did("rf", u))
            vec.wait_ge(*V.at("rf", u, r))
            vec.scalar_tensor_tensor(out=m.x_of(u, r), in0=m.tok[u][:, :], scalar=0.5, in1=m.x_of(u, r),
                                     op0=ALU.mult, op1=ALU.add).then_inc(*V.did("out", u))


def rwkv_gpsimd(pool, ph, m):
    V, G = ph.vec, ph.pool
    with pool.Fori(0, ROUNDS) as r:
        for u in range(STREAMS):
            norm_pool(pool, ph, m, u, r, "a")
        for u in range(STREAMS):
            pool.wait_ge(*V.at("scan", u, r))
            pool.tensor_tensor(m.sc[u][:, m.vj:HS, :], m.sc[u][:, m.vj:HS, :],
                               bc(m.rkv[u][:, 0, :], 1, [P, HS - m.vj, D]), ALU.mult).then_inc(*G.did("rs", u))
        for u in range(STREAMS):
            pool.wait_ge(*V.at("gvar", u, r))
            n = D // HS
            pool.tensor_tensor(m.rc[u][:, 0:n], m.sm[u][:, 0:n], m.col("pow").to_broadcast([P, n]), ALU.pow)\
                .then_inc(*G.did("grstd", u))
        for u in range(STREAMS):
            norm_pool(pool, ph, m, u, r, "f")




def build(nc, dram, out, orders=STEPS, stop_after=99):
    m = Memory()
    with ExitStack() as ctx:
        n_sb = [0]

        def sb(shape):
            n_sb[0] += 1
            return ctx.enter_context(nc.sbuf_tensor(f"sb{n_sb[0]}", shape, F32))

        def pair(shape):
            return [sb(shape) for _ in range(STREAMS)]

        def sem(name):
            return ctx.enter_context(nc.semaphore(name))

        m.x, m.ctx = sb([P, TILES, D]), sb([P, TILES, D])
        m.encT, m.hT = sb([P, KD, B * S]), sb([P, KD, B * S])
        m.ident, m.headmask, m.sel, m.gather, m.headsum = (
            sb([P, P]), sb([P, HB]), sb([P, HS, P]), sb([P, HS, P]), sb([P, P]))
        m.colbuf, m.rowbuf, m.ones = sb([P, NCOL]), sb([P, len(ROWS), D]), sb([1, P])
        m.w1x1 = sb([P, 4, P])
        m.wqkv0, m.wao0, m.wq0, m.wkv0, m.wco0 = (sb([P, KD, n * D]) for n in (3, 1, 1, 2, 1))
        m.mask_self, m.mask_cross = sb([P, S]), sb([P, TILES, S])
        m.mask_mul = {"self": sb([P, S]), "cross": sb([P, TILES, S])}
        m.mask_add = {"self": sb([P, S]), "cross": sb([P, TILES, S])}
        m.wr = sb([P, 8, KD, D])
        m.maa_w1, m.maa_w2, m.maa_w2l = sb([P, KD, ND * DM]), sb([P, 4, D]), sb([DM, D])
        m.td_w1, m.td_w2, m.s0 = sb([P, KD, DD]), sb([DD, D]), sb([P, TILES, HS * 4])
        m.gn_w, m.gn_b = sb([P, D]), sb([P, D])
        m.vj = 5
        m.wa, m.wb = pair([P, PACK_A]), pair([P, D])
        m.stats, m.mv, m.rstd, m.rstd2 = pair([P, 6]), pair([P, 2, 2]), pair([P, 2]), pair([P, 2])
        m.mx, m.sm, m.rc, m.dv = pair([P, 32]), pair([P, 32]), pair([P, 32]), pair([P, 1])
        m.xn, m.xn_last = pair([P, D]), pair([P, D])
        m.pb, m.bwT, m.bw, m.pbT = sb([P, TILES, NH2]), sb([P, KD, NH2]), sb([NH2, D]), sb([NH2, B * S])

        area = pair([P, 7936])

        def cut(u, at, shape, rows=P):
            n = 1
            for s in shape:
                n *= s
            ap = area[u][0:rows, at[0]:at[0] + n]
            at[0] += n
            assert at[0] <= 7936, at
            if len(shape) == 1:
                return ap
            names = "abcde"[:len(shape)]
            return ap.rearrange(f"p ({' '.join(names)}) -> p {' '.join(names)}",
                                **{c: s for c, s in zip(names[1:], shape[1:])})

        def cuts(shape, at, rows=P):
            start = at[0]
            both = []
            for u in range(STREAMS):
                at[0] = start
                both.append(cut(u, at, shape, rows))
            return both

        at = [0]
        m.hT_s = cuts([KD, P], at)
        m.encT_t, m.qT0, m.cT0 = cuts([KD, P], at), cuts([KD, P], at), cuts([KD, P], at)
        m.kdiag = cuts([KD, 2, HB, S], at)
        m.vdiag = cuts([2, KD, 4 * DIAG], at)
        m.p0 = cuts([NH0 * S], at)
        m.pT0 = cuts([NH0 // 2, P], at)
        at = [0]
        m.g = cuts([B * S], at)
        at = [0]
        m.cn, m.ctx_t, m.mnm, m.mlT = cuts([D], at), cuts([D], at), cuts([2 * D], at), cuts([2, P], at)
        m.p1, m.p1T, m.mo = cuts([4, D], at), cuts([2, 2 * D], at), cuts([D], at)
        at = [0]
        m.qT, m.kT, m.v = cuts([B * S], at), cuts([TILES, 2, T2], at), cuts([TILES, P], at)
        m.p, m.pT, m.cT = cuts([TILES, T2], at), cuts([TILES, S], at), cuts([TILES, 2, S], at)
        m.pn = cuts([TILES, S], at)
        at = [0]
        m.xa, m.sx, m.mix, m.xm = cuts([KD, P], at), cuts([KD, P], at), cuts([KD, P], at), cuts([ND * KD, P], at)
        m.xx, m.td, m.ew, m.wS = cuts([2 * P], at), cuts([P], at, DD), cuts([D], at), cuts([4, S], at)
        m.rkv, m.ruk, m.th, m.gate = cuts([3, D], at), cuts([D], at), cuts([D], at), cuts([D], at)
        m.av = cuts([HS, 4, S], at)
        end = at[0]
        at[0] = end
        m.tok = cuts([D], at)
        m.sc = None
        at2 = [0]
        sc = pair([P, HS, D])
        m.sc = sc
        m.og = [x[:, 2:4, :].rearrange("p a b -> p (a b)")[:, 0:D] for x in m.xm]
        m.sq = [x[:, 4:6, :].rearrange("p a b -> p (a b)") for x in m.xm]
        m.yT = [x[:, 6:8, :] for x in m.xm]
        m.mk = m.mix
        m.mr = [x[:, 8:10, :] for x in m.xm]
        m.kr = m.xx
        m.kk = [x[:, 0:2, :].rearrange("p a b -> p (a b)") for x in m.xm]

        m.ps = [ctx.enter_context(nc.psum_tensor(f"ps{u}", [P, 4, 512], F32)) for u in range(STREAMS)]

        m.tile = lambda u, r: 2 * r + u
        m.x_of = lambda u, r: m.x[:, 2 * r + u, :]
        m.ctx_of = lambda u, r: m.ctx[:, 2 * r + u, :]
        m.encT_of = lambda u, r: m.encT[:, :, bass.ds((2 * r + u) * P, P)]
        m.hT_of = lambda k, u, r: m.hT[:, k, bass.ds((2 * r + u) * P, P)]
        m.acc = lambda t: m.ps[t % 2][:, 2 + t // 4, (t // 2 % 2) * D:(t // 2 % 2 + 1) * D]
        m.col = lambda name, k=0: m.colbuf[:, COL[name] + k:COL[name] + k + 1]
        m.cols = lambda name: m.colbuf[:, COL[name]:COL[name] + dict(COLS)[name]]
        m.row = lambda name: m.rowbuf[:, ROWS.index(name), :]
        m.head_col = lambda u, n: m.wa[u][:, 3 * KD * P + n:3 * KD * P + n + 1]

        m.s_const, m.s_x, m.s_enc, m.s_w0, m.s_mask, m.s_wr, m.s_ctx, m.s_row = (
            sem(n) for n in ("const_in", "x_in", "encT_in", "w0_in", "mask_in", "rwkv_in", "ctx_in", "rows_in"))
        m.s_zero, m.s_masks, m.s_acc, m.s_pad, m.s_out = (
            sem(n) for n in ("zeroed", "masks", "acc_added", "padded", "out_stored"))
        m.s_wa = [sem(f"wa_in_{u}") for u in range(STREAMS)]
        m.s_wb = [sem(f"wb_in_{u}") for u in range(STREAMS)]
        m.n_const = 5

        names = ("attn0", "mlp0", "inorm", "heads1", "close1", "norm2", "heads2", "close2", "norm3", "mlp2", "rwkv")
        ph = {n: Phase(sem, n, orders) for n in names}
        last = NH2 // 2 - 1
        end_of = lambda steps, name, rounds: [steps.at(name, u, rounds - 1) for u in range(STREAMS)]

        block = ctx.enter_context(nc.Block())

        @block.sync
        def _(sp):
            sp.dma_start(m.x[:, :, :], dram["x"].rearrange("t p d -> p t d")).then_inc(m.s_x, 16)
            sp.dma_start(m.encT[:, :, :], dram["encT"]).then_inc(m.s_enc, 16)
            for t, name in ((m.ident, "ident"), (m.headmask, "headmask"), (m.colbuf, "cols")):
                sp.dma_start(t[:, :], dram[name]).then_inc(m.s_const, 16)
            sp.dma_start(m.rowbuf[:, :, :], dram["rows"].partition_broadcast(P)).then_inc(m.s_const, 16)
            sp.dma_start(m.ones[:, :], dram["ones"]).then_inc(m.s_const, 16)
            for half in (slice(0, S), slice(S, P)):
                sp.dma_start(m.mask_self[half, :], dram["mask_self"]).then_inc(m.s_mask, 16)
            sp.dma_start(m.mask_cross[:, :, :], dram["mask_cross"].rearrange("t p s -> p t s")).then_inc(m.s_mask, 16)
            sp.dma_start(m.wqkv0[:, :, :], dram["w_qkv"]).then_inc(m.s_w0, 16)
            sp.dma_start(m.wq0[:, :, :], dram["w_q"]).then_inc(m.s_w0, 16)
            sp.dma_start(m.wkv0[:, :, :], dram["w_kv"]).then_inc(m.s_w0, 16)
            sp.dma_start(m.wao0[:, :, :], dram["w_ao"]).then_inc(m.s_w0, 16)
            sp.dma_start(m.wco0[:, :, :], dram["w_co"]).then_inc(m.s_w0, 16)
            stream_in(sp, m, ph["mlp0"], dram["mlp0_a"], dram["mlp0_b"], MLP_A, F // P // 2,
                      [(ph["mlp0"].act, "gelu1")], [(ph["mlp0"].pe, "fc2")], [])
            sp.dma_start(m.ctx[:, :, :], dram["ctx"].rearrange("t p d -> p t d")).then_inc(m.s_ctx, 16)
            sp.wait_ge(m.s_pad, 1)
            for b in range(2):
                half = slice(b * S, (b + 1) * S)
                sp.dma_start(m.w1x1[half, :, half], dram["w1x1"]).then_inc(m.s_ctx, 16)
            for f in range(4):
                sp.dma_start(m.maa_w2[f * DM:(f + 1) * DM, f, :], dram["maa_w2"][f]).then_inc(m.s_wr, 16)
            sp.dma_start(m.maa_w2l[:, :], dram["maa_w2"][4]).then_inc(m.s_wr, 16)
            for t, name in ((m.wr, "w_r"), (m.maa_w1, "maa_w1"), (m.td_w1, "td_w1"), (m.td_w2, "td_w2"), (m.s0, "s0"),
                            (m.sel, "sel"), (m.gather, "gather"), (m.headsum, "headsum")):
                sp.dma_start(t[:], dram[name]).then_inc(m.s_wr, 16)
            if stop_after >= 3:
                stream_in(sp, m, ph["heads1"], dram["heads1_a"], dram["heads1_b"], PACK_A, NH2 // 2,
                          [(ph["heads1"].pe, "v1"), (ph["heads1"].act, "ctx")], [(ph["heads1"].pe, "out")],
                          end_of(ph["mlp0"].pe, "fc2", F // P // 2))
            if stop_after >= 4:
                stream_in(sp, m, ph["heads2"], dram["heads2_a"], dram["heads2_b"], PACK_A, NH2 // 2,
                          [(ph["heads2"].pe, "v1"), (ph["heads2"].act, "ctx")], [(ph["heads2"].pe, "out")],
                          end_of(ph["heads1"].pe, "out", NH2 // 2))
            if stop_after >= 5:
                stream_in(sp, m, ph["mlp2"], dram["mlp2_a"], dram["mlp2_b"], MLP_A, F // P // 2,
                          [(ph["mlp2"].act, "gelu1")], [(ph["mlp2"].pe, "fc2")],
                          end_of(ph["heads2"].pe, "out", NH2 // 2))
            if stop_after >= 6:
                with sp.Fori(0, ROUNDS) as r:
                    for u in range(STREAMS):
                        sp.wait_ge(*ph["rwkv"].vec.at("out", u, r))
                        sp.wait_ge(m.s_x, 16)
                        sp.dma_start(out[2 * r + u], m.x_of(u, r)).then_inc(m.s_out, 16)
                sp.wait_ge(m.s_out, 16 * TILES)
            else:
                if stop_after == 2:
                    for s, v in end_of(ph["inorm"].vec, "sum", ROUNDS):
                        sp.wait_ge(s, v)
                else:
                    sp.wait_ge(m.s_acc, {1: 2, 3: 4, 4: 6, 5: 8}[stop_after])
                sp.dma_start(out.rearrange("t p d -> p t d"), m.x[:, :, :]).then_inc(m.s_out, 16)
                sp.wait_ge(m.s_out, 16)

        @block.gpsimd
        def _(pool):
            pool.memset(m.w1x1[:, :, :], 0.0)
            pool.memset(m.maa_w2[:, :, :], 0.0).then_inc(m.s_pad, 1)
            attn0_gpsimd(pool, ph["attn0"], m)
            if stop_after >= 2:
                inorm_gpsimd(pool, ph["inorm"], m, [(m.s_ctx, 48)])
            if stop_after >= 4:
                norm_all(pool, "gpsimd", ph["norm2"], m, None, None, [])
            if stop_after >= 5:
                norm_all(pool, "gpsimd", ph["norm3"], m, None, None, [])
            if stop_after >= 6:
                rwkv_gpsimd(pool, ph["rwkv"], m)

        @block.scalar
        def _(act):
            attn0_scalar(act, ph["attn0"], m)
            mlp_scalar(act, ph["mlp0"], m, ACT.Gelu_apprx_tanh)
            if stop_after >= 2:
                inorm_scalar(act, ph["inorm"], m)
            if stop_after >= 3:
                heads_scalar(act, ph["heads1"], m)
            if stop_after >= 4:
                norm_all(act, "scalar", ph["norm2"], m, "w2_s", "w2_b", [])
                heads_scalar(act, ph["heads2"], m)
            if stop_after >= 5:
                norm_all(act, "scalar", ph["norm3"], m, "wm_s", "wm_b", [])
                mlp_scalar(act, ph["mlp2"], m, ACT.Gelu)
            if stop_after >= 6:
                rwkv_scalar(act, ph["rwkv"], m)

        @block.vector
        def _(vec):
            attn0_vector(vec, ph["attn0"], m)
            add_acc_vector(vec, m, m.s_acc, end_of(ph["mlp0"].pe, "fc2", F // P // 2))
            if stop_after >= 2:
                inorm_vector(vec, ph["inorm"], m, [(m.s_acc, 2)])
            if stop_after >= 3:
                heads_vector(vec, ph["heads1"], m, 4)
                bias_token_vector(vec, ph["close1"], m)
                add_acc_vector(vec, m, m.s_acc, [ph["close1"].pe.at("acc", 0, 0)])
            if stop_after >= 4:
                norm_all(vec, "vector", ph["norm2"], m, None, None, [(m.s_acc, 4)])
                heads_vector(vec, ph["heads2"], m, 12)
                bias_token_vector(vec, ph["close2"], m)
                add_acc_vector(vec, m, m.s_acc, [ph["close2"].pe.at("acc", 0, 0)])
            if stop_after >= 5:
                norm_all(vec, "vector", ph["norm3"], m, None, None, [(m.s_acc, 6)])
                add_acc_vector(vec, m, m.s_acc, end_of(ph["mlp2"].pe, "fc2", F // P // 2))
            if stop_after >= 6:
                rwkv_vector(vec, ph["rwkv"], m, [(m.s_acc, 8)])

        @block.tensor
        def _(pe):
            attn0_tensor(pe, ph["attn0"], m)
            mlp_tensor(pe, ph["mlp0"], m, "b2", 0, end_of(ph["attn0"].act, "mlp_hT", ROUNDS))
            if stop_after >= 2:
                inorm_tensor(pe, ph["inorm"], m, [(m.s_acc, 2), (m.s_ctx, 48)])
            if stop_after >= 3:
                heads_tensor(pe, ph["heads1"], m, "bo1", 4, end_of(ph["inorm"].act, "n_hT", ROUNDS))
                bias_token_tensor(pe, ph["heads1"], ph["close1"], m)
            if stop_after >= 4:
                norm_all(pe, "tensor", ph["norm2"], m, None, None, [])
                heads_tensor(pe, ph["heads2"], m, "bo2", 12, end_of(ph["norm2"].act, "n_hT", ROUNDS))
                bias_token_tensor(pe, ph["heads2"], ph["close2"], m)
            if stop_after >= 5:
                norm_all(pe, "tensor", ph["norm3"], m, None, None, [])
                mlp_tensor(pe, ph["mlp2"], m, "b_fc2", 20, end_of(ph["norm3"].act, "n_hT", ROUNDS))
            if stop_after >= 6:
                rwkv_tensor(pe, ph["rwkv"], m, [(m.s_acc, 8), (m.s_wr, 16 * 13)])


def lay_out(inputs):
    import numpy as np

    a = {k: np.asarray(v) for k, v in inputs.items()}
    L0, L1, L2, L3 = (lambda n, i=i: a[f"L{i}_xattn_{n}"] for i in range(4))
    block = lambda w: np.ascontiguousarray(w.reshape(-1, P, w.shape[-1]).transpose(1, 0, 2))
    col = lambda v: v.reshape(-1, P).T
    twice = lambda v: np.concatenate([v, v]).reshape(P, 1)
    qkv, kv = L0("b_qkv"), L0("b_kv")
    cols = [L0("ln1_s"), L0("ln1_b"), qkv[:D], qkv[D:2 * D], qkv[2 * D:], L0("ln2_s"), L0("ln2_b"), L0("b_q"),
            kv[:D], kv[D:], L0("ln3_s"), L0("ln3_b")]
    cols = [col(v) for v in cols] + [twice(L1(n)) for n in ("bn", "bm", "bl", "bo")]
    cols += [col(L2(n)) for n in ("ln1_scale", "ln1_offset", "ln2_scale", "ln2_offset", "ln_mlp_scale",
                                  "ln_mlp_offset")]
    cols += [col(L3(n).reshape(-1)) for n in ("ln1_w", "ln1_b", "ln2_w", "ln2_b", "maa_x", "maa_stack", "time_decay",
                                              "u", "ffn_maa_k", "ffn_maa_r")]
    cols += [np.full((P, 1), -0.5, np.float32)]
    rows = [L0("b_ao"), L0("b_co"), L0("b2"), L2("bo1"), L2("bo2"), L2("b_fc2"), L3("gn_w"), L3("gn_b")]

    def heads(i):
        w = [L2(f"w{n}{i}").reshape(KD, P, NH2, HD2).transpose(2, 1, 0, 3).reshape(NH2, P, KD * HD2) for n in "qkv"]
        c = [L2(n).reshape(NH2, HD2, 1) for n in (f"bq{i}", f"bk{i}", f"bv{i}", f"bias_k{i}", f"bias_v{i}")]
        return np.ascontiguousarray(np.concatenate(w + c, axis=2)), L2(f"wo{i}").reshape(NH2, HD2, D)

    def mlp(w1, b1, w2):
        w = w1.reshape(KD, P, F // P, P).transpose(2, 1, 0, 3).reshape(F // P, P, KD * P)
        return np.ascontiguousarray(np.concatenate([w, b1.reshape(F // P, P, 1)], axis=2)), w2.reshape(F // P, P, D)

    ctx = a["ctx_2048"]
    p, n = np.arange(P)[:, None], np.arange(P)[None, :]
    same = p // HS == n // HS
    got = {
        "x": a["x"].reshape(TILES, P, D), "ctx": ctx.reshape(TILES, P, D),
        "encT": np.ascontiguousarray(ctx.reshape(B * S, KD, P).transpose(2, 1, 0)),
        "ident": np.eye(P, dtype=np.float32),
        "headmask": (np.arange(P)[:, None] // HD0 == np.arange(HB)[None, :]).astype(np.float32),
        "cols": np.ascontiguousarray(np.concatenate(cols, axis=1)), "rows": np.stack(rows),
        "ones": np.ones((1, P), np.float32),
        "mask_self": a["mask_1x1xSxS2_fc1"].reshape(S, S), "mask_cross": a["mask_Bx1xSxS2_ff1"].reshape(TILES, P, S),
        "w_qkv": block(L0("w_qkv")), "w_ao": block(L0("w_ao")), "w_q": block(L0("w_q")), "w_kv": block(L0("w_kv")),
        "w_co": block(L0("w_co")),
        "w1x1": np.ascontiguousarray(np.stack([L1(n) for n in ("Wn", "Wm", "Wl", "Wo")]).transpose(2, 0, 1)),
        "maa_w2": L3("maa_w2"), "maa_w1": block(L3("maa_w1")), "td_w1": block(L3("td_w1")), "td_w2": L3("td_w2"),
        "w_r": np.ascontiguousarray(np.stack([L3(n) for n in ("Wr", "Wk", "Wv", "Wg", "Wo", "Wfk", "Wfr", "Wfv")])
                                    .transpose(2, 0, 1).reshape(KD, P, 8, D).transpose(1, 2, 0, 3)),
        "s0": np.ascontiguousarray(ctx[:, 2:2 + HS, :].reshape(TILES, 2, KD, P, HS).transpose(3, 0, 4, 2, 1)
                                   .reshape(P, TILES, HS * 4)),
        "sel": np.stack([same & (p % HS == j) for j in range(HS)], axis=1).astype(np.float32),
        "gather": np.stack([same & (n % HS == j) for j in range(HS)], axis=1).astype(np.float32),
        "headsum": same.astype(np.float32),
    }
    got["mlp0_a"], got["mlp0_b"] = mlp(L0("w1"), L0("b1"), L0("w2"))
    got["mlp2_a"], got["mlp2_b"] = mlp(L2("w_fc1"), L2("b_fc1"), L2("w_fc2"))
    for i in (1, 2):
        got[f"heads{i}_a"], got[f"heads{i}_b"] = heads(i)
    return {k: np.ascontiguousarray(v) for k, v in got.items()}


def kernel(**inputs):
    import concourse.bacc as bacc
    from concourse.bass_utils import run_bass_kernel_spmd

    arrays = lay_out(inputs)
    nc = bacc.Bacc("TRN2", target_bir_lowering=False, num_devices=1)
    dram = {k: nc.dram_tensor(f"in_{k}", v.shape, F32, kind="ExternalInput").ap() for k, v in arrays.items()}
    out = nc.dram_tensor("out_x", (TILES, P, D), F32, kind="ExternalOutput").ap()
    build(nc, dram, out)
    result = run_bass_kernel_spmd(nc, [{f"in_{k}": v for k, v in arrays.items()}], core_ids=[0])
    return result.results[0]["out_x"].reshape(B, S, D)
```

```python
from contextlib import ExitStack

import concourse.bass as bass
from concourse import mybir

F32 = mybir.dt.float32
ALU = mybir.AluOpType
ACT = mybir.ActivationFunctionType
AX = mybir.AxisListType.X

P = 128
B, S, D = 16, 64, 256
TILES = B * S // P
KD = D // P
STREAMS = 2
ROUNDS = TILES // STREAMS
EPS = 1e-5
MASKED = 10000.0

NH0, HD0 = 16, 16
HB = P // HD0
NH2, HD2 = 16, 128
T2 = S + 1
F = 1024
HS = 8
DM, ND = 32, 5
DD = 64

COLS = [("ln1_s", 2), ("ln1_b", 2), ("bq_self", 2), ("bk_self", 2), ("bv_self", 2), ("ln2_s", 2), ("ln2_b", 2),
        ("bq_cross", 2), ("bk_cross", 2), ("bv_cross", 2), ("ln3_s", 2), ("ln3_b", 2),
        ("bn", 1), ("bm", 1), ("bl", 1), ("bo", 1),
        ("w1_s", 2), ("w1_b", 2), ("w2_s", 2), ("w2_b", 2), ("wm_s", 2), ("wm_b", 2),
        ("r1_w", 2), ("r1_b", 2), ("r2_w", 2), ("r2_b", 2), ("maa_x", 2), ("maa_stack", 10), ("decay", 2),
        ("u", 2), ("ffn_k", 2), ("ffn_r", 2), ("pow", 1)]
COL = {}
for _name, _n in COLS:
    COL[_name] = sum(n for m, n in COLS if m in COL)
NCOL = sum(n for _, n in COLS)
ROWS = ["b_ao", "b_co", "b2", "bo1", "bo2", "b_fc2", "gn_w", "gn_b"]
PACK_A = 3 * KD * P + 5
MLP_A = KD * P + 1


STEPS = {
    "attn0_in tensor": [],
    "attn0_in scalar": [],
    "attn0_in vector": ["self_stats", "self_mv", "self_eps", "self_xn"],
    "attn0_in gpsimd": ["self_rstd", "enc"],
    "attn0 tensor": [
        "self_turned", "self_q", "self_k0", "self_k1", "self_v", "self_scores0", "self_scores1", "self_pT0",
        "self_pT1", "self_ctx", "self_out", "cross_k0", "cross_k1", "cross_turned", "cross_q", "cross_v",
        "cross_scores0", "cross_scores1", "cross_pT0", "cross_pT1", "cross_ctx", "cross_out"
    ],
    "attn0 scalar": [
        "self_hT", "self_q", "self_k1", "self_v", "self_exp0", "self_exp1", "self_pT0", "self_pT1",
        "self_ctx", "cross_k1", "cross_hT", "cross_q", "cross_v", "cross_exp0", "cross_exp1", "cross_pT0",
        "cross_pT1", "cross_ctx"
    ],
    "attn0 vector": [
        "self_k0", "self_mul0", "self_masked0", "self_max0", "self_shifted0", "self_mul1", "self_masked1",
        "self_max1", "self_shifted1", "self_psum0", "self_rc0", "self_p0", "self_psum1", "self_rc1",
        "self_p1", "self_sum", "cross_stats", "cross_mv", "cross_eps", "cross_xn", "cross_k0", "cross_mul0",
        "cross_masked0", "cross_max0", "cross_shifted0", "cross_mul1", "cross_masked1", "cross_max1",
        "cross_shifted1", "cross_psum0", "cross_rc0", "cross_p0", "cross_psum1", "cross_rc1", "cross_p1",
        "cross_sum", "mlp_stats", "mlp_mv", "mlp_eps", "mlp_xn"
    ],
    "attn0 gpsimd": ["cross_rstd", "mlp_rstd"],
    "attn0_rows tensor": ["mlp_turned"],
    "attn0_rows scalar": ["mlp_hT"],
    "attn0_rows vector": [],
    "attn0_rows gpsimd": [],
    "mlp0 tensor": ["fc1_0", "fc1_1", "fc2"],
    "mlp0 scalar": ["gelu0", "gelu1"],
    "mlp0 vector": [],
    "mlp0 gpsimd": [],
    "inorm tensor": ["mmm", "scores", "pT0", "pT1", "mo", "out", "n_turned"],
    "inorm scalar": ["mm", "ml", "exp", "pT", "mo", "n_hT"],
    "inorm vector": [
        "x_stats", "c_stats", "x_mv", "c_mv", "x_eps", "c_eps", "x_xn", "c_xn", "max", "neg", "rc", "p", "pT",
        "sum", "n_stats", "n_mv", "n_eps", "n_xn"
    ],
    "inorm gpsimd": ["x_rstd", "c_rstd", "copy", "n_rstd"],
    "heads1 tensor": ["q0", "q1", "k0", "k1", "scores", "v0", "v1", "pT", "ctx", "out"],
    "heads1 scalar": ["q0", "q1", "exp", "v0", "v1", "pT", "ctx"],
    "heads1 vector": ["dv", "k_bias", "k0", "k1", "max", "bw", "shifted", "sum", "rc", "p", "pb", "pT"],
    "heads1 gpsimd": [],
    "close1 tensor": ["bwT", "pbT", "acc"],
    "close1 scalar": [],
    "close1 vector": ["bw", "pb"],
    "close1 gpsimd": [],
    "norm2 tensor": ["n_turned"],
    "norm2 scalar": ["n_hT"],
    "norm2 vector": ["n_stats", "n_mv", "n_eps", "n_xn"],
    "norm2 gpsimd": ["n_rstd"],
    "heads2 tensor": ["q0", "q1", "k0", "k1", "scores", "v0", "v1", "pT", "ctx", "out"],
    "heads2 scalar": ["q0", "q1", "exp", "v0", "v1", "pT", "ctx"],
    "heads2 vector": ["dv", "k_bias", "k0", "k1", "max", "bw", "shifted", "sum", "rc", "p", "pb", "pT"],
    "heads2 gpsimd": [],
    "close2 tensor": ["bwT", "pbT", "acc"],
    "close2 scalar": [],
    "close2 vector": ["bw", "pb"],
    "close2 gpsimd": [],
    "norm3 tensor": ["n_turned"],
    "norm3 scalar": ["n_hT"],
    "norm3 vector": ["n_stats", "n_mv", "n_eps", "n_xn"],
    "norm3 gpsimd": ["n_rstd"],
    "mlp2 tensor": ["fc1_0", "fc1_1", "fc2"],
    "mlp2 scalar": ["gelu0", "gelu1"],
    "mlp2 vector": [],
    "mlp2 gpsimd": [],
    "rwkv tensor": [
        "a_turned", "lora", "mixes", "td1", "rkvg", "td2", "vrep", "o", "ogT", "yT", "wo", "f_turned", "kk",
        "rr", "ffn"
    ],
    "rwkv scalar": ["a_hT", "lora", "td1", "rkv", "g", "ew", "w", "gstd", "yT", "f_hT", "relu", "kk", "rr"],
    "rwkv vector": [
        "a_stats", "a_mv", "a_eps", "a_xn", "a_sx", "a_mul", "mix", "xm1", "xm2", "xm", "gate", "gates", "s0",
        "av", "scan", "rs", "cv", "og", "gsum", "cen", "sq", "gsq", "gvar", "grstd", "y1", "y2", "y", "x1",
        "f_stats", "f_mv", "f_eps", "f_xn", "f_sx", "f_mul", "mk", "mr1", "mr", "rf", "out"
    ],
    "rwkv gpsimd": ["a_rstd", "rs", "f_rstd"],
}


class Steps:

    def __init__(self, sems, names):
        self.sems, self.names, self.seen = sems, names, [0] * len(sems)

    def did(self, name, u):
        assert name == self.names[self.seen[u] % len(self.names)], (name, self.names)
        self.seen[u] += 1
        return self.sems[u], 1

    def at(self, name, u, r):
        return self.sems[u], self.names.index(name) + 1 + r * len(self.names)


class Phase:
    def __init__(self, new_sem, name, orders):
        def steps(engine):
            return Steps([new_sem(f"{name}_{engine}_{u}") for u in range(STREAMS)], orders[f"{name} {engine}"])

        self.pe, self.act, self.vec, self.pool = (steps(e) for e in ("tensor", "scalar", "vector", "gpsimd"))


class Memory:
    pass


def bc(ap, axis, shape):
    return ap.unsqueeze(axis).to_broadcast(shape)




def norm_vec(vec, ph, m, r, rows, reader=False):
    V, G = ph.vec, ph.pool
    vec.drain()
    for u, src, tag, dst, at in rows:
        vec.bn_stats(m.stats[u][:, at, :], src).then_inc(*V.did(tag + "_stats", u))
    vec.drain()
    for u, src, tag, dst, at in rows:
        vec.bn_aggr(m.mv[u][:, at, :], m.stats[u][:, at, :]).then_inc(*V.did(tag + "_mv", u))
    for u, src, tag, dst, at in rows:
        vec.wait_ge(*V.at(tag + "_mv", u, r))
        vec.tensor_scalar(m.rstd[u][:, at:at + 1], m.mv[u][:, at, 1:2], EPS, None, ALU.add)\
            .then_inc(*V.did(tag + "_eps", u))
    for u, src, tag, dst, at in rows:
        if reader:
            vec.wait_ge(*ph.act.at("n_hT", u, r - 1))
        vec.wait_ge(*G.at(tag + "_rstd", u, r))
        vec.tensor_scalar(dst, src, m.mv[u][:, at, 0:1], m.rstd2[u][:, at:at + 1], ALU.subtract, ALU.mult)\
            .then_inc(*V.did(tag + "_xn", u))


def norm_pool(pool, ph, m, u, r, tag, stat=0):
    pool.wait_ge(*ph.vec.at(tag + "_eps", u, r))
    pool.tensor_tensor(m.rstd2[u][:, stat:stat + 1], m.rstd[u][:, stat:stat + 1], m.col("pow"), ALU.pow)\
        .then_inc(*ph.pool.did(tag + "_rstd", u))


def turn_tensor(pe, ph, m, u, r, tag, out, src=None):
    src = (src or m.xn)[u]
    for k in range(KD):
        last = pe.transpose(out[:, k * P:(k + 1) * P], src[:, k * P:(k + 1) * P], m.ident[:, :])
    last.then_inc(*ph.pe.did(tag + "_turned", u))


def turn_act(act, ph, m, u, r, tag, src, dst, scale, shift):
    act.wait_ge(*ph.pe.at(tag + "_turned", u, r))
    for k in range(KD):
        last = act.activation(dst(k), src[:, k * P:(k + 1) * P], ACT.Identity,
                              bias=m.col(shift, k), scale=m.col(scale, k))
    last.then_inc(*ph.act.did(tag + "_hT", u))




ATTN0 = ("self", "cross")
WARM = 4


def later(r):
    return not isinstance(r, int)


def nothing(*stage):
    pass


def attn0_rounds(eng, enter=nothing, front=nothing, turn=nothing, scores=nothing, back=nothing, late=nothing,
                 keys=nothing, mlp_rows=nothing):
    def step(a, b, new=None):
        front(*a)
        if b:
            turn(*b)
        scores(*a)
        if new:
            enter(*new)
        if b:
            back(*b)
        late(*a, 0)
        if b and b[1] == "self":
            keys(b[0], "cross", b[2])
        late(*a, 1)

    def rest(r):
        step((1, "self", r), (0, "self", r))
        step((0, "cross", r), (1, "self", r))

    enter(0, 0)
    enter(1, 0)
    step((0, "self", 0), None)
    rest(0)
    with eng.Fori(1, ROUNDS) as r:
        step((1, "cross", r - 1), (0, "cross", r - 1), (0, r))
        step((0, "self", r), (1, "cross", r - 1), (1, r))
        rest(r)
    end = ROUNDS - 1
    step((1, "cross", end), (0, "cross", end))
    turn(1, "cross", end)
    back(1, "cross", end)
    for u in range(STREAMS):
        mlp_rows(u, end)


def keep_warm(pe, bank, x, n):
    for _ in range(n):
        pe.matmul(bank, x[:, 0:P], x, start=True, stop=True)


def attn0_tensor(pe, ph, ph_in, ph_rows, m):
    T, A, V, G = ph.pe, ph.act, ph.vec, ph.pool
    weights = {"self": (m.wqkv0[:, :, 0:D], m.wqkv0[:, :, D:2 * D], m.wqkv0[:, :, 2 * D:3 * D], m.wao0, "b_ao"),
               "cross": (m.wq0[:, :, :], m.wkv0[:, :, 0:D], m.wkv0[:, :, D:2 * D], m.wco0, "b_co")}

    def mlp_rows(u, r):
        pe.wait_ge(*V.at("mlp_xn", u, r))
        turn_tensor(pe, ph_rows, m, u, r, "mlp", m.ps[u][:, 0, :], m.xn_last)

    def turned(out, w, f, x):
        for k in range(KD):
            last = pe.matmul(out, w[:, k, f * P:(f + 1) * P], x[:, k, :], start=k == 0, stop=k == KD - 1)
        return last

    def keys(u, kind, r):
        if kind == "cross":
            pe.wait_ge(*ph_in.pool.at("enc", u, r))
        for f in range(KD):
            turned(m.ps[u][:, 2 + f, 0:P], weights[kind][1], f, m.hT_s[u] if kind == "self" else m.encT_t[u])\
                .then_inc(*T.did(f"{kind}_k{f}", u))
        if kind == "cross":
            keep_warm(pe, m.ps[u][:, 0, :], m.wqkv0[:, 0, 0:512], WARM)

    def front(u, kind, r):
        wq, wk, wv, wo, bias = weights[kind]
        x = m.hT_s[u] if kind == "self" else m.encT_t[u]
        pe.wait_ge(*(ph_in.vec if kind == "self" else V).at(kind + "_xn", u, r))
        turn_tensor(pe, ph, m, u, r, kind, m.ps[u][:, 0, :])
        pe.wait_ge(*A.at(kind + "_hT", u, r))
        if kind == "self" and later(r):
            pe.wait_ge(*V.at("cross_sum", u, r - 1))
        for f in range(KD):
            last = turned(m.ps[u][:, 1, f * P:(f + 1) * P], wq, f, m.hT_s[u])
        last.then_inc(*T.did(kind + "_q", u))
        if kind == "self":
            if later(r):
                mlp_rows(u, r - 1)
            keys(u, kind, r)
        pe.wait_ge(*V.at(kind + "_k0", u, r))
        for k in range(KD):
            last = pe.matmul(m.ps[u][:, 2, D:2 * D], x[:, k, :], wv[:, k, :], start=k == 0, stop=k == KD - 1)
        last.then_inc(*T.did(kind + "_v", u))

    def scores(u, kind, r):
        pe.wait_ge(*A.at(kind + "_q", u, r))
        if kind == "self" and later(r):
            pe.wait_ge(*ph_rows.act.at("mlp_hT", u, r - 1))
        for f in range(KD):
            if f == 1:
                pe.wait_ge(*A.at(kind + "_k1", u, r))
            for b in range(2):
                last = pe.matmul(m.ps[u][b * S:(b + 1) * S, f, :], m.qT0[u][:, f, b * S:(b + 1) * S],
                                 m.kdiag[u][:, f, b, :, :], start=True, stop=True)
            last.then_inc(*T.did(f"{kind}_scores{f}", u))

    def turn(u, kind, r):
        pe.wait_ge(*A.at(kind + "_v", u, r))
        for f in range(KD):
            pe.wait_ge(*V.at(f"{kind}_p{f}", u, r))
            for j in range(4):
                n = 4 * f + j
                last = pe.transpose(m.ps[u][:, 2 + f, j * P:(j + 1) * P], m.p0[u][:, 2 * n * S:(2 * n + 2) * S],
                                    m.ident[:, :])
            last.then_inc(*T.did(f"{kind}_pT{f}", u))

    def back(u, kind, r):
        wq, wk, wv, wo, bias = weights[kind]
        pe.wait_ge(m.s_w0, 80)
        for f in range(KD):
            pe.wait_ge(*A.at(f"{kind}_pT{f}", u, r))
            for j in range(4):
                for b in range(2):
                    last = pe.matmul(m.ps[u][j * 2 * HD0:(j + 1) * 2 * HD0, 0, f * P + b * S:f * P + (b + 1) * S],
                                     m.vdiag[u][:, b, 4 * f + j, :], m.pT0[u][:, 4 * f + j, b * S:(b + 1) * S],
                                     start=True, stop=True)
        last.then_inc(*T.did(kind + "_ctx", u))
        pe.matmul(m.ps[u][:, 1, D:2 * D], m.ones[0:1, :], m.row(bias)[0:1, :], start=True, stop=False)
        pe.wait_ge(*A.at(kind + "_ctx", u, r))
        for k in range(KD):
            last = pe.matmul(m.ps[u][:, 1, D:2 * D], m.cT0[u][:, k, :], wo[:, k, :], start=False, stop=k == KD - 1)
        last.then_inc(*T.did(kind + "_out", u))
        if kind == "cross":
            keep_warm(pe, m.ps[u][:, 0, :], m.wqkv0[:, 0, 0:512], WARM)

    pe.wait_ge(m.s_zero, 1)
    keep_warm(pe, m.ps[0][:, 0, :], m.vdiag[0][:, :, :, :].rearrange("p b n c -> p (b n c)"), 10)
    pe.wait_ge(m.s_const, 16 * m.n_const)
    pe.wait_ge(m.s_wqkv, 16)
    attn0_rounds(pe, front=front, turn=turn, scores=scores, back=back, keys=keys, mlp_rows=mlp_rows)


def attn0_scalar(act, ph, ph_rows, m):
    T, A, V, G = ph.pe, ph.act, ph.vec, ph.pool

    def mlp_rows(u, r):
        turn_act(act, ph_rows, m, u, r, "mlp", m.ps[u][:, 0, :], lambda k: m.hT_of(k, u, r), "ln3_s", "ln3_b")

    def keys(u, kind, r):
        act.wait_ge(*T.at(kind + "_k1", u, r))
        k = m.ps[u][:, 3, 0:P].rearrange("p (b s) -> p b s", b=2)
        for h in range(HB):
            last = act.activation(m.kdiag[u][:, 1, :, h, :], k, ACT.Identity, scale=m.headmask[:, h:h + 1],
                                  bias=m.kmask[kind][:, h:h + 1])
        last.then_inc(*A.did(kind + "_k1", u))

    def front(u, kind, r):
        turn_act(act, ph, m, u, r, kind, m.ps[u][:, 0, :], lambda k: m.hT_s[u][:, k, :],
                 "ln1_s" if kind == "self" else "ln2_s", "ln1_b" if kind == "self" else "ln2_b")
        act.wait_ge(*T.at(kind + "_q", u, r))
        for f in range(KD):
            last = act.activation(m.qT0[u][:, f, :], m.ps[u][:, 1, f * P:(f + 1) * P], ACT.Identity,
                                  bias=m.col("bq_" + kind, f))
        last.then_inc(*A.did(kind + "_q", u))
        if kind == "self":
            if later(r):
                mlp_rows(u, r - 1)
            keys(u, kind, r)
        act.wait_ge(*T.at(kind + "_v", u, r))
        for b in range(2):
            for o in range(2):
                last = act.activation(m.vdiag[u][o * S:(o + 1) * S, b, :, o * HD0:(o + 1) * HD0],
                                      m.ps[u][b * S:(b + 1) * S, 2, D:2 * D].rearrange(
                                          "p (n o e) -> p n o e", o=2, e=HD0)[:, :, o, :], ACT.Copy)
        last.then_inc(*A.did(kind + "_v", u))

    def late(u, kind, r, f):
        act.wait_ge(*V.at(f"{kind}_shifted{f}", u, r))
        p = m.p0[u][:, f * 512:(f + 1) * 512]
        act.activation(p, p, ACT.Exp).then_inc(*A.did(f"{kind}_exp{f}", u))

    def turn(u, kind, r):
        for b in range(2):
            act.wait_ge(*T.at(f"{kind}_pT{b}", u, r))
            act.activation(m.pT0[u][:, 4 * b:4 * b + 4, :], m.ps[u][:, 2 + b, :], ACT.Copy)\
                .then_inc(*A.did(f"{kind}_pT{b}", u))

    def back(u, kind, r):
        act.wait_ge(*T.at(kind + "_ctx", u, r))
        for f in range(KD):
            last = act.activation(m.cT0[u][:, f, :], m.ps[u][:, 0, f * P:(f + 1) * P], ACT.Identity,
                                  bias=m.col("bv_" + kind, f))
        last.then_inc(*A.did(kind + "_ctx", u))

    act.wait_ge(m.s_const, 16 * m.n_const)
    act.wait_ge(m.s_masks, 1)
    act.wait_ge(m.s_zero, 1)
    attn0_rounds(act, front=front, turn=turn, back=back, late=late, keys=keys, mlp_rows=mlp_rows)


def attn0_vector(vec, ph, ph_in, m):
    T, A, V, G = ph.pe, ph.act, ph.vec, ph.pool
    half = [P, HB, S]

    def norm(u, kind, r, ph=ph):
        norm_vec(vec, ph, m, r, [(u, m.x_of(u, r), kind, (m.xn_last if kind == "mlp" else m.xn)[u][:, :], 0)])

    def probs(u, b):
        return m.p0[u][:, b * 512:(b + 1) * 512].rearrange("p (n t) -> p n t", t=S)

    def enter(u, r):
        norm(u, "self", r, ph_in)

    def keys(u, kind, r):
        vec.wait_ge(*T.at(kind + "_k0", u, r))
        for b in range(2):
            last = vec.scalar_tensor_tensor(
                out=m.kdiag[u][:, 0, b, :, :], in0=bc(m.ps[u][:, 2, b * S:(b + 1) * S], 1, half),
                scalar=m.col("bk_" + kind, 0), in1=bc(m.headmask[:, :], 2, half), op0=ALU.add, op1=ALU.mult)
        last.then_inc(*V.did(kind + "_k0", u))

    def front(u, kind, r):
        if kind == "self":
            keys(u, kind, r)

    def scores(u, kind, r):
        for b in range(2):
            s = m.ps[u][:, b, :].rearrange("p (n t) -> p n t", t=S)
            mul, add = (bc(x[kind] if kind == "self" else x[kind][:, m.tile(u, r), :], 1, half)
                        for x in (m.mask_mul, m.mask_add))
            mx = m.mx[u][:, b * HB:(b + 1) * HB]
            vec.wait_ge(*T.at(f"{kind}_scores{b}", u, r))
            vec.tensor_tensor(probs(u, b), s, mul, ALU.mult).then_inc(*V.did(f"{kind}_mul{b}", u))
            vec.wait_ge(*V.at(f"{kind}_mul{b}", u, r))
            vec.tensor_tensor(probs(u, b), probs(u, b), add, ALU.add).then_inc(*V.did(f"{kind}_masked{b}", u))
            vec.wait_ge(*V.at(f"{kind}_masked{b}", u, r))
            vec.tensor_reduce(mx, probs(u, b), AX, ALU.max).then_inc(*V.did(f"{kind}_max{b}", u))
            vec.wait_ge(*V.at(f"{kind}_max{b}", u, r))
            vec.tensor_tensor(probs(u, b), probs(u, b), bc(mx, 2, half), ALU.subtract)\
                .then_inc(*V.did(f"{kind}_shifted{b}", u))

    def late(u, kind, r, f):
        sums, rc = (x[u][:, f * HB:(f + 1) * HB] for x in (m.sm, m.rc))
        vec.wait_ge(*A.at(f"{kind}_exp{f}", u, r))
        vec.tensor_reduce(sums, probs(u, f), AX, ALU.add).then_inc(*V.did(f"{kind}_psum{f}", u))
        vec.wait_ge(*V.at(f"{kind}_psum{f}", u, r))
        vec.reciprocal(rc, sums).then_inc(*V.did(f"{kind}_rc{f}", u))
        vec.wait_ge(*V.at(f"{kind}_rc{f}", u, r))
        vec.tensor_tensor(probs(u, f), probs(u, f), bc(rc, 2, half), ALU.mult).then_inc(*V.did(f"{kind}_p{f}", u))

    def back(u, kind, r):
        vec.wait_ge(*T.at(kind + "_out", u, r))
        vec.tensor_tensor(m.x_of(u, r), m.ps[u][:, 1, D:2 * D], m.x_of(u, r), ALU.add)\
            .then_inc(*V.did(kind + "_sum", u))
        norm(u, "cross" if kind == "self" else "mlp", r)

    vec.wait_ge(m.s_const, 16 * m.n_const)
    vec.wait_ge(m.s_mask, 48)
    for kind in ATTN0:
        vec.tensor_scalar(m.mask_add[kind], m.mask_mul[kind], MASKED, -MASKED, ALU.mult, ALU.add)
        vec.tensor_scalar(m.mask_mul[kind], m.mask_mul[kind], HD0 ** -0.5, None, ALU.mult)
        last = vec.tensor_scalar(m.kmask[kind][:, :], m.headmask[:, :], m.col("bk_" + kind, 1), None, ALU.mult)
    last.then_inc(m.s_masks, 1)
    vec.wait_ge(m.s_masks, 1)
    vec.wait_ge(m.s_x, 16)
    attn0_rounds(vec, enter=enter, front=front, scores=scores, back=back, late=late,
                 keys=keys)


def attn0_gpsimd(pool, ph, ph_in, m):

    def enter(u, r):
        norm_pool(pool, ph_in, m, u, r, "self")
        pool.tensor_copy(m.encT_t[u][:, :, :], m.encT_of(u, r)).then_inc(*ph_in.pool.did("enc", u))

    def back(u, kind, r):
        norm_pool(pool, ph, m, u, r, "cross" if kind == "self" else "mlp")

    pool.wait_ge(m.s_const, 16 * m.n_const)
    pool.wait_ge(m.s_enc, 16)
    attn0_rounds(pool, enter=enter, back=back)




def start_acc(pe, m, row):
    for u in range(STREAMS):
        for c in range(2):
            pe.matmul(m.ps[u][:, 2 + c, :], m.ones[0:1, :], bc(m.row(row)[0:1, :], 1, [1, 2, D]),
                      start=True, stop=True)


def stream_in(sp, m, ph, pack_a, pack_b, width, rounds, free_a, free_b, before):
    for sem, value in before:
        sp.wait_ge(sem, value)
    for u in range(STREAMS):
        sp.dma_start(m.wa[u][:, 0:width], pack_a[u]).then_inc(m.s_wa[u], 16)
        sp.dma_start(m.wb[u][:, :], pack_b[u]).then_inc(m.s_wb[u], 16)
    with sp.Fori(0, rounds - 1) as r:
        for u in range(STREAMS):
            for steps, name in free_a:
                sp.wait_ge(*steps.at(name, u, r))
            sp.wait_ge(m.s_wa[u], 16)
            sp.dma_start(m.wa[u][:, 0:width], pack_a[2 * r + 2 + u]).then_inc(m.s_wa[u], 16)
        for u in range(STREAMS):
            for steps, name in free_b:
                sp.wait_ge(*steps.at(name, u, r))
            sp.wait_ge(m.s_wb[u], 16)
            sp.dma_start(m.wb[u][:, :], pack_b[2 * r + 2 + u]).then_inc(m.s_wb[u], 16)




def mlp_tensor(pe, ph, m, row, loads, before):
    T, A = ph.pe, ph.act
    for sem, value in before:
        pe.wait_ge(sem, value)
    start_acc(pe, m, row)
    with pe.Fori(0, F // P // 2) as r:
        for u in range(STREAMS):
            pe.wait_ge(m.s_wa[u], 16 * (loads + 1) + r * 16)
            for c in range(2):
                for k in range(KD):
                    last = pe.matmul(m.ps[u][:, c, :], m.wa[u][:, k * P:(k + 1) * P], m.hT[:, k, c * 512:(c + 1) * 512],
                                     start=k == 0, stop=k == KD - 1)
                last.then_inc(*T.did(f"fc1_{c}", u))
        for u in range(STREAMS):
            pe.wait_ge(*A.at("gelu1", u, r))
            pe.wait_ge(m.s_wb[u], 16 * (loads + 1) + r * 16)
            for t in range(TILES):
                last = pe.matmul(m.acc(t), m.g[u][:, t * P:(t + 1) * P], m.wb[u][:, :],
                                 start=False, stop=False, skip_group_check=True)
            last.then_inc(*T.did("fc2", u))


def mlp_scalar(act, ph, m, gelu):
    with act.Fori(0, F // P // 2) as r:
        for u in range(STREAMS):
            for c in range(2):
                act.wait_ge(*ph.pe.at(f"fc1_{c}", u, r))
                act.activation(m.g[u][:, c * 512:(c + 1) * 512], m.ps[u][:, c, :], gelu,
                               bias=m.wa[u][:, KD * P:KD * P + 1]).then_inc(*ph.act.did(f"gelu{c}", u))


def add_acc_vector(vec, m, sem, before):
    for s, value in before:
        vec.wait_ge(s, value)
    for u in range(STREAMS):
        xs = m.x[:, :, :].rearrange("p (r u) d -> p r u d", u=2)[:, :, u, :]
        vec.tensor_tensor(xs, m.ps[u][:, 2:4, :].rearrange("p c (r d) -> p (c r) d", d=D), xs, ALU.add)\
            .then_inc(sem, 1)




def norm_all(eng, which, ph, m, scale, shift, before):
    for sem, value in before:
        eng.wait_ge(sem, value)

    def round_of(r, reader):
        if which == "vector":
            norm_vec(eng, ph, m, r, [(u, m.x_of(u, r), "n", m.xn[u][:, :], 0) for u in range(STREAMS)], reader)
        for u in range(STREAMS):
            if which == "gpsimd":
                norm_pool(eng, ph, m, u, r, "n")
            elif which == "tensor":
                eng.wait_ge(*ph.vec.at("n_xn", u, r))
                turn_tensor(eng, ph, m, u, r, "n", m.ps[u][:, 1, :])
            elif which == "scalar":
                turn_act(eng, ph, m, u, r, "n", m.ps[u][:, 1, :], lambda k: m.hT_of(k, u, r), scale, shift)

    round_of(0, False)
    with eng.Fori(1, ROUNDS) as r:
        round_of(r, True)




def heads_tensor(pe, ph, m, row, loads, before):
    T, A, V = ph.pe, ph.act, ph.vec
    for sem, value in before:
        pe.wait_ge(sem, value)
    start_acc(pe, m, row)
    with pe.Fori(0, NH2 // 2) as r:
        for u in range(STREAMS):
            pe.wait_ge(m.s_wa[u], 16 * (loads + 1) + r * 16)
            for n, x in enumerate((m.hT, m.encT)):
                for c in range(2):
                    if n:
                        pe.wait_ge(*A.at(f"q{c}", u, r))
                    for k in range(KD):
                        last = pe.matmul(m.ps[u][:, c, :], m.wa[u][:, (KD * n + k) * P:(KD * n + k + 1) * P],
                                         x[:, k, c * 512:(c + 1) * 512], start=k == 0, stop=k == KD - 1)
                    last.then_inc(*T.did(f"{'qk'[n]}{c}", u))
        for u in range(STREAMS):
            pe.wait_ge(*V.at("k1", u, r))
            for t in range(TILES):
                for b in range(2):
                    last = pe.matmul(m.ps[u][b * S:(b + 1) * S, t // 4, (t % 4) * T2:(t % 4 + 1) * T2],
                                     m.qT[u][:, t * P + b * S:t * P + (b + 1) * S], m.kT[u][:, t, b, :],
                                     start=True, stop=True)
            pe.wait_ge(m.s_wb[u], 16 * (loads + 1) + r * 16)
            for f in range(KD):
                last = pe.matmul(m.ps[u][:, 1, 300 + f:301 + f], m.wb[u][:, f * P:(f + 1) * P], m.dv[u][:, :],
                                 start=True, stop=True)
            last.then_inc(*T.did("scores", u))
        for u in range(STREAMS):
            pe.wait_ge(*V.at("shifted", u, r))
            for t in range(TILES):
                for k in range(KD):
                    last = pe.matmul(m.ps[u][:, t // 4, (t % 4) * P:(t % 4 + 1) * P], m.encT[:, k, t * P:(t + 1) * P],
                                     m.wa[u][:, (2 * KD + k) * P:(2 * KD + k + 1) * P],
                                     start=k == 0, stop=k == KD - 1)
                if t % 4 == 3:
                    last.then_inc(*T.did(f"v{t // 4}", u))
        for u in range(STREAMS):
            pe.wait_ge(*V.at("p", u, r))
            pe.wait_ge(*A.at("v0", u, r))
            for j in range(TILES // 2):
                last = pe.transpose(m.ps[u][:, 0, j * P:(j + 1) * P], m.pn[u][:, 2 * j:2 * j + 2, :], m.ident[:, :])
            last.then_inc(*T.did("pT", u))
        for u in range(STREAMS):
            pe.wait_ge(*A.at("pT", u, r))
            pe.wait_ge(*V.at("pT", u, r))
            for t in range(TILES):
                last = pe.matmul(m.ps[u][:, t // 4, (t % 4) * P:(t % 4 + 1) * P], m.v[u][:, t, :],
                                 m.pT[u][:, t, :, :], start=True, stop=True)
            last.then_inc(*T.did("ctx", u))
        for u in range(STREAMS):
            pe.wait_ge(*A.at("ctx", u, r))
            for t in range(TILES):
                last = pe.matmul(m.acc(t), m.cT[u][:, t, :], m.wb[u][:, :],
                                 start=False, stop=False, skip_group_check=True)
            last.then_inc(*T.did("out", u))


def heads_scalar(act, ph, m):
    T, A, V = ph.pe, ph.act, ph.vec
    with act.Fori(0, NH2 // 2) as r:
        for u in range(STREAMS):
            for c in range(2):
                act.wait_ge(*T.at(f"q{c}", u, r))
                act.activation(m.qT[u][:, c * 512:(c + 1) * 512], m.ps[u][:, c, :], ACT.Identity,
                               bias=m.head_col(u, 0)).then_inc(*A.did(f"q{c}", u))
        for u in range(STREAMS):
            act.wait_ge(*V.at("shifted", u, r))
            act.activation(m.p[u][:, :, :], m.p[u][:, :, :], ACT.Exp, scale=HD2 ** -0.5).then_inc(*A.did("exp", u))
        for u in range(STREAMS):
            for c in range(2):
                act.wait_ge(*T.at(f"v{c}", u, r))
                act.activation(m.v[u][:, 4 * c:4 * c + 4, :], m.ps[u][:, c, :], ACT.Copy)\
                    .then_inc(*A.did(f"v{c}", u))
        for u in range(STREAMS):
            act.wait_ge(*T.at("pT", u, r))
            turn_probs(lambda o, i: act.activation(o, i, ACT.Copy), m, u, 0).then_inc(*A.did("pT", u))
        for u in range(STREAMS):
            act.wait_ge(*T.at("ctx", u, r))
            for c in range(2):
                last = act.activation(m.cT[u][:, 4 * c:4 * c + 4, :], m.ps[u][:, c, :], ACT.Identity,
                                      bias=m.head_col(u, 2))
            last.then_inc(*A.did("ctx", u))


def turn_probs(copy, m, u, odd):
    src = m.ps[u][:, 0, :].rearrange("p (j b q) -> p j b q", b=2, q=S)
    for b in range(2):
        dst = m.pT[u][b * S:(b + 1) * S, :, b, :].rearrange("p (j o) q -> p j o q", o=2)
        last = copy(dst[:, :, odd, :], src[odd * S:(odd + 1) * S, :, b, :])
    return last


def heads_vector(vec, ph, m, loads):
    T, A, V = ph.pe, ph.act, ph.vec
    for u in range(STREAMS):
        vec.memset(m.pT[u][:, :, :, :], 0.0).then_inc(m.s_pT, 1)
    with vec.Fori(0, NH2 // 2) as r:
        for u in range(STREAMS):
            vec.wait_ge(m.s_wa[u], 16 * (loads + 1) + r * 16)
            vec.tensor_tensor(m.dv[u][:, :], m.head_col(u, 4), m.head_col(u, 2), ALU.subtract)\
                .then_inc(*V.did("dv", u))
            for c in range(2):
                vec.wait_ge(*T.at(f"k{c}", u, r))
                if c == 0:
                    vec.tensor_copy(m.kT[u][:, :, :, S], bc(m.head_col(u, 3), 1, [P, TILES, 2])).then_inc(
                        *V.did("k_bias", u))
                vec.tensor_scalar(m.kT[u][:, 4 * c:4 * c + 4, :, 0:S],
                                  m.ps[u][:, c, :].rearrange("p (t b k) -> p t b k", b=2, k=S),
                                  m.head_col(u, 1), None, ALU.add).then_inc(*V.did(f"k{c}", u))
        for u in range(STREAMS):
            s = m.ps[u][:, 0:2, 0:4 * T2].rearrange("p c (t k) -> p c t k", k=T2)
            p = m.p[u][:, :, :].rearrange("p (c t) k -> p c t k", c=2)
            mx = m.mx[u][:, 0:TILES].rearrange("p (c t) -> p c t", c=2)
            vec.wait_ge(*T.at("scores", u, r))
            vec.tensor_reduce(mx, s, AX, ALU.max).then_inc(*V.did("max", u))
            vec.tensor_scalar(m.bwT[:, :, bass.ds(2 * r + u, 1)], bc(m.ps[u][:, 1, 300:302], 2, [P, 2, 1]),
                              1.0, None, ALU.mult).then_inc(*V.did("bw", u))
            vec.wait_ge(*V.at("max", u, r))
            vec.tensor_tensor(p, s, bc(mx, 3, [P, 2, 4, T2]), ALU.subtract).then_inc(*V.did("shifted", u))
        for u in range(STREAMS):
            p = m.p[u][:, :, :]
            vec.wait_ge(*A.at("exp", u, r))
            vec.tensor_reduce(m.sm[u][:, 0:TILES], p, AX, ALU.add).then_inc(*V.did("sum", u))
            vec.wait_ge(*V.at("sum", u, r))
            vec.reciprocal(m.rc[u][:, 0:TILES], m.sm[u][:, 0:TILES]).then_inc(*V.did("rc", u))
            vec.wait_ge(*V.at("rc", u, r))
            vec.tensor_tensor(m.pn[u][:, :, :], p[:, :, 0:S], bc(m.rc[u][:, 0:TILES], 2, [P, TILES, S]), ALU.mult)\
                .then_inc(*V.did("p", u))
            vec.tensor_tensor(m.pb[:, :, bass.ds(2 * r + u, 1)], p[:, :, S:T2],
                              m.rc[u][:, 0:TILES].unsqueeze(2), ALU.mult).then_inc(*V.did("pb", u))
        for u in range(STREAMS):
            vec.wait_ge(*T.at("pT", u, r))
            turn_probs(vec.tensor_copy, m, u, 1).then_inc(*V.did("pT", u))


def bias_token_tensor(pe, ph, cl, m):
    V = ph.vec
    for u in range(STREAMS):
        pe.wait_ge(*V.at("pT", u, NH2 // 2 - 1))
    for f in range(KD):
        last = pe.transpose(m.ps[0][0:NH2, 0, f * P:(f + 1) * P], m.bwT[:, f, :], m.ident[:, :])
    last.then_inc(*cl.pe.did("bwT", 0))
    for t in range(TILES):
        last = pe.transpose(m.ps[1][0:NH2, t // 4, (t % 4) * P:(t % 4 + 1) * P], m.pb[:, t, :], m.ident[:, :])
    last.then_inc(*cl.pe.did("pbT", 0))
    pe.wait_ge(*cl.vec.at("bw", 0, 0))
    pe.wait_ge(*cl.vec.at("pb", 0, 0))
    for t in range(TILES):
        last = pe.matmul(m.acc(t), m.pbT[:, t * P:(t + 1) * P], m.bw[:, :], start=False, stop=False,
                         skip_group_check=True)
    last.then_inc(*cl.pe.did("acc", 0))


def bias_token_vector(vec, cl, m):
    vec.wait_ge(*cl.pe.at("bwT", 0, 0))
    vec.tensor_copy(m.bw[:, :], m.ps[0][0:NH2, 0, 0:D]).then_inc(*cl.vec.did("bw", 0))
    vec.wait_ge(*cl.pe.at("pbT", 0, 0))
    vec.tensor_copy(m.pbT[:, :], m.ps[1][0:NH2, 0:2, :].rearrange("p c n -> p (c n)")).then_inc(*cl.vec.did("pb", 0))




def inorm_tensor(pe, ph, m, before):
    T, A, V, G = ph.pe, ph.act, ph.vec, ph.pool
    for sem, value in before:
        pe.wait_ge(sem, value)
    with pe.Fori(0, ROUNDS) as r:
        for u in range(STREAMS):
            pe.wait_ge(*V.at("c_xn", u, r))
            pe.wait_ge(*G.at("copy", u, r))
            for n, x in enumerate((m.xn[u], m.cn[u])):
                last = pe.matmul(m.ps[u][:, 0, n * D:(n + 1) * D], m.w1x1[:, n, :], x[:, :], start=True, stop=True)
            for c in range(2):
                last = pe.matmul(m.ps[u][:, 1, c * P:(c + 1) * P], m.ctx_t[u][:, c * P:(c + 1) * P], m.w1x1[:, 2, :],
                                 start=True, stop=True)
            last.then_inc(*T.did("mmm", u))
        for u in range(STREAMS):
            pe.wait_ge(*A.at("mm", u, r))
            for b in range(2):
                half = slice(b * S, (b + 1) * S)
                for c in range(2):
                    last = pe.matmul(m.ps[u][:, 2 + b, c * D:(c + 1) * D], m.mnm[u][half, c * P:(c + 1) * P],
                                     m.mnm[u][half, D:2 * D], start=True, stop=True)
            last.then_inc(*T.did("scores", u))
        for u in range(STREAMS):
            pe.wait_ge(*V.at("p", u, r))
            pe.wait_ge(*A.at("ml", u, r))
            for b in range(2):
                for s in range(2):
                    for c in range(2):
                        last = pe.transpose(m.ps[u][:, b, s * D + c * P:s * D + (c + 1) * P],
                                            m.p1[u][:, 2 * b + c, s * P:(s + 1) * P], m.ident[:, :])
                last.then_inc(*T.did(f"pT{b}", u))
        for u in range(STREAMS):
            for b in range(2):
                pe.wait_ge(*(A, V)[b].at("pT", u, r))
                for s in range(2):
                    last = pe.matmul(m.ps[u][b * S:(b + 1) * S, 2, 0:D], m.mlT[u][:, s, b * S:(b + 1) * S],
                                     m.p1T[u][:, b, s * D:(s + 1) * D], start=s == 0, stop=s == 1)
            last.then_inc(*T.did("mo", u))
        for u in range(STREAMS):
            pe.wait_ge(*A.at("mo", u, r))
            pe.matmul(m.ps[u][:, 3, 0:D], m.w1x1[:, 3, :], m.mo[u][:, :], start=True, stop=True)\
                .then_inc(*T.did("out", u))
        for u in range(STREAMS):
            pe.wait_ge(*V.at("n_xn", u, r))
            turn_tensor(pe, ph, m, u, r, "n", m.ps[u][:, 3, :], m.xn_last)


def inorm_scalar(act, ph, m):
    T, A, V, G = ph.pe, ph.act, ph.vec, ph.pool
    with act.Fori(0, ROUNDS) as r:
        for u in range(STREAMS):
            act.wait_ge(*T.at("mmm", u, r))
            for n, bias in enumerate(("bn", "bm")):
                last = act.activation(m.mnm[u][:, n * D:(n + 1) * D], m.ps[u][:, 0, n * D:(n + 1) * D], ACT.Identity,
                                      bias=m.col(bias))
            last.then_inc(*A.did("mm", u))
            act.activation(m.mlT[u][:, :, :], m.ps[u][:, 1, 0:2 * P], ACT.Copy).then_inc(*A.did("ml", u))
        for u in range(STREAMS):
            act.wait_ge(*V.at("neg", u, r))
            for n in range(4):
                last = act.activation(m.p1[u][:, n, :], m.ps[u][:, 2 + n // 2, (n % 2) * D:(n % 2 + 1) * D], ACT.Exp,
                                      bias=m.mx[u][:, n:n + 1], accum_out=m.sm[u][:, n:n + 1])
            last.then_inc(*A.did("exp", u))
        for u in range(STREAMS):
            act.wait_ge(*T.at("pT0", u, r))
            act.activation(m.p1T[u][:, 0, :], m.ps[u][:, 0, :], ACT.Copy).then_inc(*A.did("pT", u))
        for u in range(STREAMS):
            act.wait_ge(*T.at("mo", u, r))
            act.activation(m.mo[u][:, :], m.ps[u][:, 2, 0:D], ACT.Identity, bias=m.col("bl"))\
                .then_inc(*A.did("mo", u))
        for u in range(STREAMS):
            turn_act(act, ph, m, u, r, "n", m.ps[u][:, 3, :], lambda k: m.hT_of(k, u, r), "w1_s", "w1_b")


def inorm_vector(vec, ph, m, before):
    T, A, V, G = ph.pe, ph.act, ph.vec, ph.pool
    for sem, value in before:
        vec.wait_ge(sem, value)
    with vec.Fori(0, ROUNDS) as r:
        norm_vec(vec, ph, m, r, [row for u in range(STREAMS) for row in (
            (u, m.x_of(u, r), "x", m.xn[u][:, :], 0), (u, m.ctx_of(u, r), "c", m.cn[u][:, :], 1))])
        for u in range(STREAMS):
            s = m.ps[u][:, 2:4, :].rearrange("p b (c s) -> p (b c) s", c=2)
            vec.wait_ge(*T.at("scores", u, r))
            vec.tensor_reduce(m.rc[u][:, 0:4], s, AX, ALU.max).then_inc(*V.did("max", u))
            vec.wait_ge(*V.at("max", u, r))
            vec.tensor_scalar(m.mx[u][:, 0:4], m.rc[u][:, 0:4], -1.0, None, ALU.mult).then_inc(*V.did("neg", u))
        for u in range(STREAMS):
            vec.wait_ge(*A.at("exp", u, r))
            vec.reciprocal(m.rc[u][:, 0:4], m.sm[u][:, 0:4]).then_inc(*V.did("rc", u))
            vec.wait_ge(*V.at("rc", u, r))
            vec.tensor_tensor(m.p1[u][:, :, :], m.p1[u][:, :, :], bc(m.rc[u][:, 0:4], 2, [P, 4, D]), ALU.mult)\
                .then_inc(*V.did("p", u))
        for u in range(STREAMS):
            vec.wait_ge(*T.at("pT1", u, r))
            vec.tensor_copy(m.p1T[u][:, 1, :], m.ps[u][:, 1, :]).then_inc(*V.did("pT", u))
        for u in range(STREAMS):
            vec.wait_ge(*T.at("out", u, r))
            vec.scalar_tensor_tensor(out=m.x_of(u, r), in0=m.ps[u][:, 3, 0:D], scalar=m.col("bo"), in1=m.x_of(u, r),
                                     op0=ALU.add, op1=ALU.add).then_inc(*V.did("sum", u))
        norm_vec(vec, ph, m, r, [(u, m.x_of(u, r), "n", m.xn_last[u][:, :], 0) for u in range(STREAMS)])


def inorm_gpsimd(pool, ph, m, before):
    for sem, value in before:
        pool.wait_ge(sem, value)
    with pool.Fori(0, ROUNDS) as r:
        for u in range(STREAMS):
            norm_pool(pool, ph, m, u, r, "x")
            norm_pool(pool, ph, m, u, r, "c", stat=1)
        for u in range(STREAMS):
            pool.tensor_copy(m.ctx_t[u][:, :], m.ctx_of(u, r)).then_inc(*ph.pool.did("copy", u))
        for u in range(STREAMS):
            norm_pool(pool, ph, m, u, r, "n")




MIX_K, MIX_W, MIX_V, MIX_R, MIX_G = range(ND)
W_R, W_K, W_V, W_G, W_O, W_FK, W_FR, W_FV = range(8)


def rwkv_rounds(eng, norm=nothing, rows=nothing, mixed=nothing, lora=nothing, mixes=nothing, project=nothing,
                spread=nothing, scan=nothing, gather=nothing, heads=nothing, gated=nothing, attended=nothing,
                norm_out=nothing, shifted=nothing, ffn=nothing, close=nothing):
    def both(r, *stages):
        for stage in stages:
            for u in range(STREAMS):
                stage(u, r)

    with eng.Fori(0, ROUNDS) as r:
        norm(r)
        both(r, rows, mixed, lora, mixes, project, spread, scan)
        gather(0, r)
        heads(0, r)
        gather(1, r)
        gated(0, r)
        heads(1, r)
        gated(1, r)
        both(r, attended)
        norm_out(r)
        both(r, shifted, ffn, close)


def rwkv_tensor(pe, ph, m, before):
    T, A, V, G = ph.pe, ph.act, ph.vec, ph.pool

    def product(out, lhsT, rhs):
        for k in range(KD):
            last = pe.matmul(out, lhsT(k), rhs(k), start=k == 0, stop=k == KD - 1)
        return last

    def rows(u, r):
        pe.wait_ge(*V.at("a_xn", u, r))
        turn_tensor(pe, ph, m, u, r, "a", m.ps[u][:, 0, :])

    def lora(u, r):
        pe.wait_ge(*V.at("mix", u, r))
        product(m.ps[u][:, 0, 0:P], lambda k: m.maa_w1[:, k, 0:P], lambda k: m.mix[u][:, k, :])
        product(m.ps[u][0:DM, 0, P:2 * P], lambda k: m.maa_w1[:, k, P:ND * DM], lambda k: m.mix[u][:, k, :])\
            .then_inc(*T.did("lora", u))
        pe.wait_ge(*A.at("lora", u, r))
        for f in range(ND):
            for e in range(KD):
                n = KD * f + e
                out = m.ps[u][:, 1 + n // 4, (n % 4) * P:(n % 4 + 1) * P]
                if f < 4:
                    pe.matmul(out, m.maa_w2[:, f, e * P:(e + 1) * P], m.xx[u][:, 0:P], start=True, stop=True)
                else:
                    last = pe.matmul(out, m.maa_w2l[:, e * P:(e + 1) * P], m.xx[u][0:DM, P:2 * P],
                                     start=True, stop=True)
        last.then_inc(*T.did("mixes", u))

    def project(u, r):
        pe.wait_ge(*V.at("xm", u, r))
        xm = lambda f, k: m.xm[u][:, KD * f + k, :]
        product(m.ps[u][0:DD, 0, 0:P], lambda k: m.td_w1[:, k, :], lambda k: xm(MIX_W, k)).then_inc(*T.did("td1", u))
        for n, (w, f) in enumerate(((W_R, MIX_R), (W_K, MIX_K), (W_V, MIX_V))):
            for e in range(KD):
                last = product(m.ps[u][:, 1 + n // 2, (n % 2) * D + e * P:(n % 2) * D + (e + 1) * P],
                               lambda k: m.wr[:, w, k, e * P:(e + 1) * P], lambda k: xm(f, k))
        product(m.ps[u][:, 2, D:2 * D], lambda k: xm(MIX_G, k), lambda k: m.wr[:, W_G, k, :])\
            .then_inc(*T.did("rkvg", u))
        pe.wait_ge(*A.at("td1", u, r))
        for e in range(KD):
            last = pe.matmul(m.ps[u][:, 3, e * P:(e + 1) * P], m.td_w2[:, e * P:(e + 1) * P], m.td[u][:, :],
                             start=True, stop=True)
        last.then_inc(*T.did("td2", u))

    def spread(u, r):
        pe.wait_ge(*A.at("ew", u, r))
        pe.wait_ge(*V.at("gate", u, r))
        for j in range(HS):
            last = pe.matmul(m.ps[u][:, j // 2, (j % 2) * D:(j % 2 + 1) * D], m.sel[:, j, :], m.rkv[u][:, 2, :],
                             start=True, stop=True)
        last.then_inc(*T.did("vrep", u))

    def gather(u, r):
        pe.wait_ge(*V.at("rs", u, r))
        pe.wait_ge(*G.at("rs", u, r))
        for j in range(HS):
            pe.matmul(m.ps[u][:, 0, 0:D], m.gather[:, j, :], m.sc[u][:, j, :], start=j == 0, stop=j == HS - 1)
        pe.matmul(m.ps[u][:, 1, 0:D], m.headsum[:, :], m.ruk[u][:, :], start=True, stop=True).then_inc(*T.did("o", u))

    def heads(u, r):
        pe.wait_ge(*V.at("og", u, r))
        for e in range(KD):
            last = pe.transpose(m.ps[u][:, 2, e * P:(e + 1) * P], m.og[u][:, e * P:(e + 1) * P], m.ident[:, :])
        last.then_inc(*T.did("ogT", u))

    def attended(u, r):
        pe.wait_ge(*V.at("y", u, r))
        for e in range(KD):
            last = pe.transpose(m.ps[u][:, 3, e * P:(e + 1) * P], m.tok[u][:, e * P:(e + 1) * P], m.ident[:, :])
        last.then_inc(*T.did("yT", u))
        pe.wait_ge(*A.at("yT", u, r))
        product(m.ps[u][:, 0, 0:D], lambda k: m.yT[u][:, k, :], lambda k: m.wr[:, W_O, k, :])\
            .then_inc(*T.did("wo", u))

    def shifted(u, r):
        pe.wait_ge(*V.at("f_xn", u, r))
        turn_tensor(pe, ph, m, u, r, "f", m.ps[u][:, 1, :])

    def ffn(u, r):
        pe.wait_ge(*V.at("mk", u, r))
        for e in range(KD):
            last = product(m.ps[u][:, 2, e * P:(e + 1) * P], lambda k: m.wr[:, W_FK, k, e * P:(e + 1) * P],
                           lambda k: m.mk[u][:, k, :])
        last.then_inc(*T.did("kk", u))
        pe.wait_ge(*V.at("mr", u, r))
        product(m.ps[u][:, 3, 0:D], lambda k: m.mr[u][:, k, :], lambda k: m.wr[:, W_FR, k, :])\
            .then_inc(*T.did("rr", u))

    def close(u, r):
        pe.wait_ge(*A.at("kk", u, r))
        product(m.ps[u][:, 0, 0:D], lambda k: m.kk[u][:, k * P:(k + 1) * P], lambda k: m.wr[:, W_FV, k, :])\
            .then_inc(*T.did("ffn", u))

    for sem, value in before:
        pe.wait_ge(sem, value)
    rwkv_rounds(pe, gather=gather, rows=rows, heads=heads, lora=lora, attended=attended, project=project,
                shifted=shifted, ffn=ffn, spread=spread, close=close)


def rwkv_scalar(act, ph, m):
    T, A, V, G = ph.pe, ph.act, ph.vec, ph.pool

    def rows(u, r):
        turn_act(act, ph, m, u, r, "a", m.ps[u][:, 0, :], lambda k: m.xa[u][:, k, :], "r1_w", "r1_b")

    def lora(u, r):
        act.wait_ge(*T.at("lora", u, r))
        act.activation(m.xx[u][:, 0:P], m.ps[u][:, 0, 0:P], ACT.Tanh)
        act.activation(m.xx[u][0:DM, P:2 * P], m.ps[u][0:DM, 0, P:2 * P], ACT.Tanh).then_inc(*A.did("lora", u))

    def project(u, r):
        act.wait_ge(*T.at("td1", u, r))
        act.activation(m.td[u][:, :], m.ps[u][0:DD, 0, 0:P], ACT.Tanh).then_inc(*A.did("td1", u))
        act.wait_ge(*T.at("rkvg", u, r))
        act.activation(m.rkv[u][:, :, :], m.ps[u][:, 1:3, :].rearrange("p c n -> p (c n)")[:, 0:3 * D], ACT.Copy)\
            .then_inc(*A.did("rkv", u))
        act.activation(m.th[u][:, :], m.ps[u][:, 2, D:2 * D], ACT.Tanh, scale=0.5).then_inc(*A.did("g", u))
        act.wait_ge(*T.at("td2", u, r))
        for e in range(KD):
            last = act.activation(m.ew[u][:, e * P:(e + 1) * P], m.ps[u][:, 3, e * P:(e + 1) * P], ACT.Exp,
                                  bias=m.col("decay", e))
        last.then_inc(*A.did("ew", u))
        act.wait_ge(*A.at("ew", u, r))
        act.activation(m.wS[u][:, :, 1:S], m.ew[u][:, :].rearrange("p (n s) -> p n s", s=S)[:, :, 0:S - 1],
                       ACT.Exp, scale=-1.0).then_inc(*A.did("w", u))

    def heads(u, r):
        act.wait_ge(*V.at("gvar", u, r))
        n = D // HS
        act.activation(m.sm[u][:, 0:n], m.sm[u][:, 0:n], ACT.Sqrt).then_inc(*A.did("gstd", u))

    def attended(u, r):
        act.wait_ge(*T.at("yT", u, r))
        act.activation(m.yT[u][:, :, :], m.ps[u][:, 3, 0:D], ACT.Copy).then_inc(*A.did("yT", u))

    def shifted(u, r):
        turn_act(act, ph, m, u, r, "f", m.ps[u][:, 1, :], lambda k: m.xa[u][:, k, :], "r2_w", "r2_b")

    def ffn(u, r):
        act.wait_ge(*T.at("kk", u, r))
        act.activation(m.kr[u][:, :], m.ps[u][:, 2, 0:D], ACT.Relu).then_inc(*A.did("relu", u))
        act.wait_ge(*A.at("relu", u, r))
        act.activation(m.kk[u][:, :], m.kr[u][:, :], ACT.Square).then_inc(*A.did("kk", u))
        act.wait_ge(*T.at("rr", u, r))
        act.activation(m.th[u][:, :], m.ps[u][:, 3, 0:D], ACT.Tanh, scale=0.5).then_inc(*A.did("rr", u))

    act.wait_ge(m.s_gn, 1)
    rwkv_rounds(act, rows=rows, lora=lora, project=project, heads=heads, attended=attended, shifted=shifted, ffn=ffn)


def rwkv_shift(vec, V, m, u, r, tag, state):
    xa = m.xa[u][:, :, :].rearrange("p k (b s) -> p k b s", b=2)
    sx = m.sx[u][:, :, :].rearrange("p k (b s) -> p k b s", b=2)
    first = m.encT_of(u, r).rearrange("p k (b s) -> p k b s", b=2)[:, :, :, state:state + 1]
    vec.tensor_tensor(sx[:, :, :, 1:S], xa[:, :, :, 0:S - 1], xa[:, :, :, 1:S], ALU.subtract)
    vec.tensor_tensor(sx[:, :, :, 0:1], first, xa[:, :, :, 0:1], ALU.subtract).then_inc(*V.did(tag + "_sx", u))


def rwkv_mix(vec, V, m, u, r, tag, dst, factor):
    vec.wait_ge(*V.at(tag + "_sx", u, r))
    vec.tensor_tensor(dst[:, :, :], m.sx[u][:, :, :], bc(factor, 2, [P, KD, P]), ALU.mult)\
        .then_inc(*V.did(f"{tag}_mul", u))
    vec.wait_ge(*V.at(f"{tag}_mul", u, r))
    return vec.tensor_tensor(dst[:, :, :], dst[:, :, :], m.xa[u][:, :, :], ALU.add)


def rwkv_vector(vec, ph, m, before):
    T, A, V, G = ph.pe, ph.act, ph.vec, ph.pool
    n = D // HS
    head = lambda x: x.rearrange("p (h j) -> p h j", j=HS)

    def norm(r, tag="a"):
        norm_vec(vec, ph, m, r, [(u, m.x_of(u, r), tag, m.xn[u][:, :], 0) for u in range(STREAMS)])

    def norm_out(r):
        norm(r, "f")

    def mixed(u, r):
        vec.wait_ge(*A.at("a_hT", u, r))
        rwkv_shift(vec, V, m, u, r, "a", 1)
        rwkv_mix(vec, V, m, u, r, "a", m.mix[u], m.cols("maa_x")).then_inc(*V.did("mix", u))

    def mixes(u, r):
        vec.wait_ge(*T.at("mixes", u, r))
        xm = m.xm[u][:, :, :]
        wide = m.xm[u][:, :, :].rearrange("p (f k) t -> p f (k t)", k=KD)
        flat = lambda x: bc(x[u][:, :, :].rearrange("p k t -> p (k t)"), 1, [P, ND, D])
        vec.tensor_tensor(xm, m.ps[u][:, 1:4, :].rearrange("p c (n t) -> p (c n) t", t=P)[:, 0:ND * KD, :],
                          bc(m.cols("maa_stack"), 2, [P, ND * KD, P]), ALU.add).then_inc(*V.did("xm1", u))
        vec.wait_ge(*V.at("xm1", u, r))
        vec.tensor_tensor(wide, wide, flat(m.sx), ALU.mult).then_inc(*V.did("xm2", u))
        vec.wait_ge(*V.at("xm2", u, r))
        vec.tensor_tensor(wide, wide, flat(m.xa), ALU.add).then_inc(*V.did("xm", u))

    def project(u, r):
        vec.wait_ge(*A.at("rkv", u, r))
        for e in range(KD):
            part = slice(e * P, (e + 1) * P)
            vec.scalar_tensor_tensor(out=m.ruk[u][:, part], in0=m.rkv[u][:, 0, part], scalar=m.col("u", e),
                                     in1=m.rkv[u][:, 1, part], op0=ALU.mult, op1=ALU.mult)
        vec.wait_ge(*A.at("g", u, r))
        vec.scalar_tensor_tensor(out=m.gate[u][:, :], in0=m.th[u][:, :], scalar=1.0, in1=m.ps[u][:, 2, D:2 * D],
                                 op0=ALU.add, op1=ALU.mult).then_inc(*V.did("gate", u))
        vec.wait_ge(*V.at("gate", u, r))
        vec.tensor_tensor(m.gate_b[u][:, :], m.gate[u][:, :], m.row("gn_b"), ALU.mult)
        vec.tensor_tensor(m.gate[u][:, :], m.gate[u][:, :], m.row("gn_w"), ALU.mult).then_inc(*V.did("gates", u))
        vec.tensor_scalar(m.av[u][:, :, :, 0:1], m.s0[:, m.tile(u, r), :].rearrange(
            "p (j n o) -> p j n o", n=4, o=1), 1.0, None, ALU.mult).then_inc(*V.did("s0", u))

    def scan(u, r):
        vec.wait_ge(*T.at("vrep", u, r))
        keys = m.rkv[u][:, 1, :].rearrange("p (n s) -> p n s", s=S)[:, :, 0:S - 1]
        vals = m.ps[u][:, :, :].rearrange("p c (j n s) -> p (c j) n s", j=2, s=S)[:, :, :, 0:S - 1]
        vec.tensor_tensor(m.av[u][:, :, :, 1:S], vals, bc(keys, 1, [P, HS, 4, S - 1]), ALU.mult)\
            .then_inc(*V.did("av", u))
        vec.wait_ge(*V.at("av", u, r))
        vec.wait_ge(*A.at("w", u, r))
        for j in range(HS):
            last = vec.tensor_tensor_scan(m.sc[u][:, j, :], m.wS[u][:, :, :].rearrange("p n s -> p (n s)"),
                                          m.av[u][:, j, :, :].rearrange("p n s -> p (n s)"), 0.0,
                                          ALU.mult, ALU.add)
        last.then_inc(*V.did("scan", u))
        vec.wait_ge(*V.at("scan", u, r))
        vec.tensor_tensor(m.sc[u][:, 0:m.vj, :], m.sc[u][:, 0:m.vj, :],
                          bc(m.rkv[u][:, 0, :], 1, [P, m.vj, D]), ALU.mult).then_inc(*V.did("rs", u))

    def gather(u, r):
        vec.wait_ge(*T.at("o", u, r))
        vec.tensor_tensor(m.og[u][:, :], m.ps[u][:, 1, 0:D], m.rkv[u][:, 2, :], ALU.mult).then_inc(*V.did("cv", u))
        vec.wait_ge(*V.at("cv", u, r))
        vec.tensor_tensor(m.og[u][:, :], m.ps[u][:, 0, 0:D], m.og[u][:, :], ALU.add).then_inc(*V.did("og", u))

    def heads(u, r):
        tok = m.tok[u][:, :]
        vec.wait_ge(*T.at("ogT", u, r))
        vec.tensor_reduce(m.mx[u][:, 0:n], head(m.ps[u][:, 2, 0:D]), AX, ALU.add).then_inc(*V.did("gsum", u))
        vec.wait_ge(*V.at("gsum", u, r))
        vec.scalar_tensor_tensor(out=head(tok), in0=bc(m.mx[u][:, 0:n], 2, [P, n, HS]), scalar=-1.0 / HS,
                                 in1=head(m.ps[u][:, 2, 0:D]), op0=ALU.mult, op1=ALU.add).then_inc(*V.did("cen", u))
        vec.wait_ge(*V.at("cen", u, r))
        vec.tensor_tensor(m.sq[u][:, :], tok, tok, ALU.mult).then_inc(*V.did("sq", u))
        vec.wait_ge(*V.at("sq", u, r))
        vec.tensor_reduce(m.sm[u][:, 0:n], head(m.sq[u][:, :]), AX, ALU.add).then_inc(*V.did("gsq", u))
        vec.wait_ge(*V.at("gsq", u, r))
        vec.tensor_scalar(m.sm[u][:, 0:n], m.sm[u][:, 0:n], 1.0 / HS, EPS, ALU.mult, ALU.add)\
            .then_inc(*V.did("gvar", u))

    def gated(u, r):
        tok = m.tok[u][:, :]
        vec.wait_ge(*A.at("gstd", u, r))
        vec.reciprocal(m.rc[u][:, 0:n], m.sm[u][:, 0:n]).then_inc(*V.did("grstd", u))
        vec.wait_ge(*V.at("grstd", u, r))
        vec.tensor_tensor(head(tok), head(tok), bc(m.rc[u][:, 0:n], 2, [P, n, HS]), ALU.mult)\
            .then_inc(*V.did("y1", u))
        vec.wait_ge(*V.at("y1", u, r))
        vec.tensor_tensor(tok, tok, m.gate[u][:, :], ALU.mult).then_inc(*V.did("y2", u))
        vec.wait_ge(*V.at("y2", u, r))
        vec.tensor_tensor(tok, tok, m.gate_b[u][:, :], ALU.add).then_inc(*V.did("y", u))

    def attended(u, r):
        vec.wait_ge(*T.at("wo", u, r))
        vec.tensor_tensor(m.x_of(u, r), m.ps[u][:, 0, 0:D], m.x_of(u, r), ALU.add).then_inc(*V.did("x1", u))

    def shifted(u, r):
        vec.wait_ge(*A.at("f_hT", u, r))
        rwkv_shift(vec, V, m, u, r, "f", 0)
        rwkv_mix(vec, V, m, u, r, "f", m.mk[u], m.cols("ffn_k")).then_inc(*V.did("mk", u))
        vec.tensor_tensor(m.mr[u][:, :, :], m.sx[u][:, :, :], bc(m.cols("ffn_r"), 2, [P, KD, P]), ALU.mult)\
            .then_inc(*V.did("mr1", u))
        vec.wait_ge(*V.at("mr1", u, r))
        vec.tensor_tensor(m.mr[u][:, :, :], m.mr[u][:, :, :], m.xa[u][:, :, :], ALU.add).then_inc(*V.did("mr", u))

    def close(u, r):
        vec.wait_ge(*A.at("rr", u, r))
        vec.wait_ge(*T.at("ffn", u, r))
        vec.scalar_tensor_tensor(out=m.tok[u][:, :], in0=m.th[u][:, :], scalar=1.0, in1=m.ps[u][:, 0, 0:D],
                                 op0=ALU.add, op1=ALU.mult).then_inc(*V.did("rf", u))
        vec.wait_ge(*V.at("rf", u, r))
        vec.scalar_tensor_tensor(out=m.x_of(u, r), in0=m.tok[u][:, :], scalar=0.5, in1=m.x_of(u, r),
                                 op0=ALU.mult, op1=ALU.add).then_inc(*V.did("out", u))

    for sem, value in before:
        vec.wait_ge(sem, value)
    for u in range(STREAMS):
        vec.memset(m.wS[u][:, :, 0:1], 0.0)
    vec.tensor_scalar(m.row("gn_w"), m.row("gn_w"), 0.5, None, ALU.mult)
    vec.tensor_scalar(m.row("gn_b"), m.row("gn_b"), 0.5, None, ALU.mult).then_inc(m.s_gn, 1)
    vec.wait_ge(m.s_gn, 1)
    rwkv_rounds(vec, norm=norm, gather=gather, heads=heads, mixed=mixed, gated=gated, mixes=mixes,
                attended=attended, norm_out=norm_out, project=project, shifted=shifted, close=close, scan=scan)


def rwkv_gpsimd(pool, ph, m):
    V, G = ph.vec, ph.pool

    def norm(r, tag="a"):
        for u in range(STREAMS):
            norm_pool(pool, ph, m, u, r, tag)

    def norm_out(r):
        norm(r, "f")

    def scan(u, r):
        pool.wait_ge(*V.at("scan", u, r))
        pool.tensor_tensor(m.sc[u][:, m.vj:HS, :], m.sc[u][:, m.vj:HS, :],
                           bc(m.rkv[u][:, 0, :], 1, [P, HS - m.vj, D]), ALU.mult).then_inc(*G.did("rs", u))

    rwkv_rounds(pool, norm=norm, scan=scan, norm_out=norm_out)




def build(nc, dram, out, orders=STEPS, stop_after=99):
    m = Memory()
    with ExitStack() as ctx:
        n_sb = [0]

        def sb(shape):
            n_sb[0] += 1
            return ctx.enter_context(nc.sbuf_tensor(f"sb{n_sb[0]}", shape, F32))

        def pair(shape):
            return [sb(shape) for _ in range(STREAMS)]

        def sem(name):
            return ctx.enter_context(nc.semaphore(name))

        m.x, m.ctx = sb([P, TILES, D]), sb([P, TILES, D])
        m.encT, m.hT = sb([P, KD, B * S]), sb([P, KD, B * S])
        m.ident, m.headmask, m.sel, m.gather, m.headsum = (
            sb([P, P]), sb([P, HB]), sb([P, HS, P]), sb([P, HS, P]), sb([P, P]))
        m.colbuf, m.rowbuf, m.ones = sb([P, NCOL]), sb([P, len(ROWS), D]), sb([1, P])
        m.w1x1 = sb([P, 4, P])
        m.wqkv0, m.wao0, m.wq0, m.wkv0, m.wco0 = (sb([P, KD, n * D]) for n in (3, 1, 1, 2, 1))
        m.mask_mul, m.mask_add = (
            {"self": sb([P, S])[:, :], "cross": sb([P, TILES, S])[:, :, :]} for _ in range(2))
        m.kmask = {kind: sb([P, HB]) for kind in ATTN0}
        m.wr = sb([P, 8, KD, D])
        m.maa_w1, m.maa_w2, m.maa_w2l = sb([P, KD, ND * DM]), sb([P, 4, D]), sb([DM, D])
        m.td_w1, m.td_w2, m.s0 = sb([P, KD, DD]), sb([DD, D]), sb([P, TILES, HS * 4])
        m.vj = 5
        m.wa, m.wb = pair([P, PACK_A]), pair([P, D])
        m.stats, m.mv, m.rstd, m.rstd2 = pair([P, 2, 6]), pair([P, 2, 2]), pair([P, 2]), pair([P, 2])
        m.mx, m.sm, m.rc, m.dv = pair([P, 32]), pair([P, 32]), pair([P, 32]), pair([P, 1])
        m.xn, m.xn_last = pair([P, D]), pair([P, D])
        m.pb, m.bwT, m.bw, m.pbT = sb([P, TILES, NH2]), sb([P, KD, NH2]), sb([NH2, D]), sb([NH2, B * S])

        AREA = 9088
        area = pair([P, AREA])

        def cut(u, at, shape, rows=P):
            n = 1
            for s in shape:
                n *= s
            ap = area[u][0:rows, at[0]:at[0] + n]
            at[0] += n
            assert at[0] <= AREA, at
            if len(shape) == 1:
                return ap
            names = "abcde"[:len(shape)]
            return ap.rearrange(f"p ({' '.join(names)}) -> p {' '.join(names)}",
                                **{c: s for c, s in zip(names[1:], shape[1:])})

        def cuts(shape, at, rows=P):
            start = at[0]
            both = []
            for u in range(STREAMS):
                at[0] = start
                both.append(cut(u, at, shape, rows))
            return both

        at = [0]
        m.hT_s = cuts([KD, P], at)
        m.encT_t, m.cT0 = cuts([KD, P], at), cuts([KD, P], at)
        m.kdiag = cuts([KD, 2, HB, S], at)
        m.vdiag, m.qT0 = cuts([2, NH0 // 2, 2 * HD0], at), cuts([KD, P], at)
        m.p0 = cuts([NH0 * S], at)
        m.pT0 = cuts([NH0 // 2, P], at)
        at = [0]
        m.g = cuts([B * S], at)
        at = [0]
        m.cn, m.ctx_t, m.mnm, m.mlT = cuts([D], at), cuts([D], at), cuts([2 * D], at), cuts([2, P], at)
        m.p1, m.p1T, m.mo = cuts([4, D], at), cuts([2, 2 * D], at), cuts([D], at)
        at = [0]
        m.qT, m.kT, m.v = cuts([B * S], at), cuts([TILES, 2, T2], at), cuts([TILES, P], at)
        m.p, m.pT, m.cT = cuts([TILES, T2], at), cuts([TILES, 2, S], at), cuts([TILES, P], at)
        m.pn = cuts([TILES, S], at)
        at = [0]
        m.xa, m.sx, m.mix, m.xm = cuts([KD, P], at), cuts([KD, P], at), cuts([KD, P], at), cuts([ND * KD, P], at)
        m.xx, m.td, m.ew, m.wS = cuts([2 * P], at), cuts([P], at, DD), cuts([D], at), cuts([4, S], at)
        m.rkv, m.ruk, m.th, m.gate = cuts([3, D], at), cuts([D], at), cuts([D], at), cuts([D], at)
        m.av = cuts([HS, 4, S], at)
        m.gate_b, m.tok, m.sc = cuts([D], at), cuts([D], at), cuts([HS, D], at)
        m.og = [x[:, 2:4, :].rearrange("p a b -> p (a b)")[:, 0:D] for x in m.xm]
        m.sq = [x[:, 4:6, :].rearrange("p a b -> p (a b)") for x in m.xm]
        m.yT = [x[:, 6:8, :] for x in m.xm]
        m.mk = m.mix
        m.mr = [x[:, 8:10, :] for x in m.xm]
        m.kr = m.xx
        m.kk = [x[:, 0:2, :].rearrange("p a b -> p (a b)") for x in m.xm]

        m.ps = [ctx.enter_context(nc.psum_tensor(f"ps{u}", [P, 4, 512], F32)) for u in range(STREAMS)]

        m.tile = lambda u, r: 2 * r + u
        m.x_of = lambda u, r: m.x[:, 2 * r + u, :]
        m.ctx_of = lambda u, r: m.ctx[:, 2 * r + u, :]
        m.encT_of = lambda u, r: m.encT[:, :, bass.ds((2 * r + u) * P, P)]
        m.hT_of = lambda k, u, r: m.hT[:, k, bass.ds((2 * r + u) * P, P)]
        m.acc = lambda t: m.ps[t % 2][:, 2 + t // 4, (t // 2 % 2) * D:(t // 2 % 2 + 1) * D]
        m.col = lambda name, k=0: m.colbuf[:, COL[name] + k:COL[name] + k + 1]
        m.cols = lambda name: m.colbuf[:, COL[name]:COL[name] + dict(COLS)[name]]
        m.row = lambda name: m.rowbuf[:, ROWS.index(name), :]
        m.head_col = lambda u, n: m.wa[u][:, 3 * KD * P + n:3 * KD * P + n + 1]

        m.s_const, m.s_wqkv, m.s_x, m.s_enc, m.s_w0, m.s_mask, m.s_wr, m.s_ctx, m.s_row = (
            sem(n) for n in ("const_in", "wqkv_in", "x_in", "encT_in", "w0_in", "mask_in", "rwkv_in", "ctx_in", "rows_in"))
        m.s_pT, m.s_zero, m.s_gn, m.s_masks, m.s_acc, m.s_pad, m.s_out = (
            sem(n) for n in ("turned_probs_zeroed", "zeroed", "group_norm_rows", "masks", "acc_added", "padded", "out_stored"))
        m.s_wa = [sem(f"wa_in_{u}") for u in range(STREAMS)]
        m.s_wb = [sem(f"wb_in_{u}") for u in range(STREAMS)]
        m.n_const = 4

        names = ("attn0_in", "attn0", "attn0_rows", "mlp0", "inorm", "heads1", "close1", "norm2", "heads2", "close2", "norm3", "mlp2", "rwkv")
        ph = {n: Phase(sem, n, orders) for n in names}
        last = NH2 // 2 - 1
        end_of = lambda steps, name, rounds: [steps.at(name, u, rounds - 1) for u in range(STREAMS)]

        block = ctx.enter_context(nc.Block())

        @block.sync
        def _(sp):
            for t, name in ((m.colbuf, "cols"), (m.ident, "ident"), (m.headmask, "headmask"), (m.ones, "ones")):
                sp.dma_start(t[:, :], dram[name]).then_inc(m.s_const, 16)
            sp.dma_start(m.x[:, :, :], dram["x"].rearrange("t p d -> p t d")).then_inc(m.s_x, 16)
            for half in (slice(0, S), slice(S, P)):
                sp.dma_start(m.mask_mul["self"][half, :], dram["mask_self"]).then_inc(m.s_mask, 16)
            sp.dma_start(m.mask_mul["cross"][:, :, :], dram["mask_cross"].rearrange("t p s -> p t s"))\
                .then_inc(m.s_mask, 16)
            sp.dma_start(m.wqkv0[:, :, :], dram["w_qkv"]).then_inc(m.s_wqkv, 16)
            sp.dma_start(m.encT[:, :, :], dram["encT"]).then_inc(m.s_enc, 16)
            sp.dma_start(m.rowbuf[:, :, :], dram["rows"].partition_broadcast(P)).then_inc(m.s_w0, 16)
            for t, name in ((m.wao0, "w_ao"), (m.wkv0, "w_kv"), (m.wq0, "w_q"), (m.wco0, "w_co")):
                sp.dma_start(t[:, :, :], dram[name]).then_inc(m.s_w0, 16)
            stream_in(sp, m, ph["mlp0"], dram["mlp0_a"], dram["mlp0_b"], MLP_A, F // P // 2,
                      [(ph["mlp0"].act, "gelu1")], [(ph["mlp0"].pe, "fc2")], [])
            sp.dma_start(m.ctx[:, :, :], dram["ctx"].rearrange("t p d -> p t d")).then_inc(m.s_ctx, 16)
            sp.wait_ge(m.s_pad, 1)
            for b in range(2):
                half = slice(b * S, (b + 1) * S)
                sp.dma_start(m.w1x1[half, :, half], dram["w1x1"]).then_inc(m.s_ctx, 16)
            for f in range(4):
                sp.dma_start(m.maa_w2[f * DM:(f + 1) * DM, f, :], dram["maa_w2"][f]).then_inc(m.s_wr, 16)
            sp.dma_start(m.maa_w2l[:, :], dram["maa_w2"][4]).then_inc(m.s_wr, 16)
            for t, name in ((m.wr, "w_r"), (m.maa_w1, "maa_w1"), (m.td_w1, "td_w1"), (m.td_w2, "td_w2"), (m.s0, "s0"),
                            (m.sel, "sel"), (m.gather, "gather"), (m.headsum, "headsum")):
                sp.dma_start(t[:], dram[name]).then_inc(m.s_wr, 16)
            if stop_after >= 3:
                stream_in(sp, m, ph["heads1"], dram["heads1_a"], dram["heads1_b"], PACK_A, NH2 // 2,
                          [(ph["heads1"].pe, "v1"), (ph["heads1"].act, "ctx")], [(ph["heads1"].pe, "out")],
                          end_of(ph["mlp0"].pe, "fc2", F // P // 2))
            if stop_after >= 4:
                stream_in(sp, m, ph["heads2"], dram["heads2_a"], dram["heads2_b"], PACK_A, NH2 // 2,
                          [(ph["heads2"].pe, "v1"), (ph["heads2"].act, "ctx")], [(ph["heads2"].pe, "out")],
                          end_of(ph["heads1"].pe, "out", NH2 // 2))
            if stop_after >= 5:
                stream_in(sp, m, ph["mlp2"], dram["mlp2_a"], dram["mlp2_b"], MLP_A, F // P // 2,
                          [(ph["mlp2"].act, "gelu1")], [(ph["mlp2"].pe, "fc2")],
                          end_of(ph["heads2"].pe, "out", NH2 // 2))
            if stop_after >= 6:
                with sp.Fori(0, ROUNDS) as r:
                    for u in range(STREAMS):
                        sp.wait_ge(*ph["rwkv"].vec.at("out", u, r))
                        sp.wait_ge(m.s_x, 16)
                        sp.dma_start(out[2 * r + u], m.x_of(u, r)).then_inc(m.s_out, 16)
                sp.wait_ge(m.s_out, 16 * TILES)
            else:
                if stop_after == 2:
                    for s, v in end_of(ph["inorm"].vec, "sum", ROUNDS):
                        sp.wait_ge(s, v)
                else:
                    sp.wait_ge(m.s_acc, {1: 2, 3: 4, 4: 6, 5: 8}[stop_after])
                sp.dma_start(out.rearrange("t p d -> p t d"), m.x[:, :, :]).then_inc(m.s_out, 16)
                sp.wait_ge(m.s_out, 16)

        @block.gpsimd
        def _(pool):
            for u in range(STREAMS):
                last = pool.memset(m.vdiag[u][:, :, :, :], 0.0)
            last.then_inc(m.s_zero, 1)
            pool.memset(m.w1x1[:, :, :], 0.0)
            pool.memset(m.maa_w2[:, :, :], 0.0).then_inc(m.s_pad, 1)
            attn0_gpsimd(pool, ph["attn0"], ph["attn0_in"], m)
            if stop_after >= 2:
                inorm_gpsimd(pool, ph["inorm"], m, [(m.s_ctx, 48)])
            if stop_after >= 4:
                norm_all(pool, "gpsimd", ph["norm2"], m, None, None, [])
            if stop_after >= 5:
                norm_all(pool, "gpsimd", ph["norm3"], m, None, None, [])
            if stop_after >= 6:
                rwkv_gpsimd(pool, ph["rwkv"], m)

        @block.scalar
        def _(act):
            attn0_scalar(act, ph["attn0"], ph["attn0_rows"], m)
            mlp_scalar(act, ph["mlp0"], m, ACT.Gelu_apprx_tanh)
            if stop_after >= 2:
                inorm_scalar(act, ph["inorm"], m)
            if stop_after >= 3:
                heads_scalar(act, ph["heads1"], m)
            if stop_after >= 4:
                norm_all(act, "scalar", ph["norm2"], m, "w2_s", "w2_b", [])
                heads_scalar(act, ph["heads2"], m)
            if stop_after >= 5:
                norm_all(act, "scalar", ph["norm3"], m, "wm_s", "wm_b", [])
                mlp_scalar(act, ph["mlp2"], m, ACT.Gelu)
            if stop_after >= 6:
                rwkv_scalar(act, ph["rwkv"], m)

        @block.vector
        def _(vec):
            attn0_vector(vec, ph["attn0"], ph["attn0_in"], m)
            add_acc_vector(vec, m, m.s_acc, end_of(ph["mlp0"].pe, "fc2", F // P // 2))
            if stop_after >= 2:
                inorm_vector(vec, ph["inorm"], m, [(m.s_acc, 2), (m.s_ctx, 48)])
            if stop_after >= 3:
                heads_vector(vec, ph["heads1"], m, 4)
                bias_token_vector(vec, ph["close1"], m)
                add_acc_vector(vec, m, m.s_acc, [ph["close1"].pe.at("acc", 0, 0)])
            if stop_after >= 4:
                norm_all(vec, "vector", ph["norm2"], m, None, None, [(m.s_acc, 4)])
                heads_vector(vec, ph["heads2"], m, 12)
                bias_token_vector(vec, ph["close2"], m)
                add_acc_vector(vec, m, m.s_acc, [ph["close2"].pe.at("acc", 0, 0)])
            if stop_after >= 5:
                norm_all(vec, "vector", ph["norm3"], m, None, None, [(m.s_acc, 6)])
                add_acc_vector(vec, m, m.s_acc, end_of(ph["mlp2"].pe, "fc2", F // P // 2))
            if stop_after >= 6:
                rwkv_vector(vec, ph["rwkv"], m, [(m.s_acc, 8)])

        @block.tensor
        def _(pe):
            attn0_tensor(pe, ph["attn0"], ph["attn0_in"], ph["attn0_rows"], m)
            mlp_tensor(pe, ph["mlp0"], m, "b2", 0, end_of(ph["attn0_rows"].act, "mlp_hT", ROUNDS))
            if stop_after >= 2:
                inorm_tensor(pe, ph["inorm"], m, [(m.s_acc, 2), (m.s_ctx, 48)])
            if stop_after >= 3:
                heads_tensor(pe, ph["heads1"], m, "bo1", 4, end_of(ph["inorm"].act, "n_hT", ROUNDS))
                bias_token_tensor(pe, ph["heads1"], ph["close1"], m)
            if stop_after >= 4:
                norm_all(pe, "tensor", ph["norm2"], m, None, None, [])
                heads_tensor(pe, ph["heads2"], m, "bo2", 12, end_of(ph["norm2"].act, "n_hT", ROUNDS))
                bias_token_tensor(pe, ph["heads2"], ph["close2"], m)
            if stop_after >= 5:
                norm_all(pe, "tensor", ph["norm3"], m, None, None, [])
                mlp_tensor(pe, ph["mlp2"], m, "b_fc2", 20, end_of(ph["norm3"].act, "n_hT", ROUNDS))
            if stop_after >= 6:
                rwkv_tensor(pe, ph["rwkv"], m, [(m.s_acc, 8), (m.s_wr, 16 * 13)])


def lay_out(inputs):
    import numpy as np

    a = {k: np.asarray(v) for k, v in inputs.items()}
    L0, L1, L2, L3 = (lambda n, i=i: a[f"L{i}_xattn_{n}"] for i in range(4))
    block = lambda w: np.ascontiguousarray(w.reshape(-1, P, w.shape[-1]).transpose(1, 0, 2))
    col = lambda v: v.reshape(-1, P).T
    twice = lambda v: np.concatenate([v, v]).reshape(P, 1)
    qkv, kv = L0("b_qkv"), L0("b_kv")
    cols = [L0("ln1_s"), L0("ln1_b"), qkv[:D], qkv[D:2 * D], qkv[2 * D:], L0("ln2_s"), L0("ln2_b"), L0("b_q"),
            kv[:D], kv[D:], L0("ln3_s"), L0("ln3_b")]
    cols = [col(v) for v in cols] + [twice(L1(n)) for n in ("bn", "bm", "bl", "bo")]
    cols += [col(L2(n)) for n in ("ln1_scale", "ln1_offset", "ln2_scale", "ln2_offset", "ln_mlp_scale",
                                  "ln_mlp_offset")]
    cols += [col(L3(n).reshape(-1)) for n in ("ln1_w", "ln1_b", "ln2_w", "ln2_b", "maa_x", "maa_stack", "time_decay",
                                              "u", "ffn_maa_k", "ffn_maa_r")]
    cols += [np.full((P, 1), -0.5, np.float32)]
    rows = [L0("b_ao"), L0("b_co"), L0("b2"), L2("bo1"), L2("bo2"), L2("b_fc2"), L3("gn_w"), L3("gn_b")]

    def heads(i):
        w = [L2(f"w{n}{i}").reshape(KD, P, NH2, HD2).transpose(2, 1, 0, 3).reshape(NH2, P, KD * HD2) for n in "qkv"]
        c = [L2(n).reshape(NH2, HD2, 1) for n in (f"bq{i}", f"bk{i}", f"bv{i}", f"bias_k{i}", f"bias_v{i}")]
        return np.ascontiguousarray(np.concatenate(w + c, axis=2)), L2(f"wo{i}").reshape(NH2, HD2, D)

    def mlp(w1, b1, w2):
        w = w1.reshape(KD, P, F // P, P).transpose(2, 1, 0, 3).reshape(F // P, P, KD * P)
        return np.ascontiguousarray(np.concatenate([w, b1.reshape(F // P, P, 1)], axis=2)), w2.reshape(F // P, P, D)

    ctx = a["ctx_2048"]
    p, n = np.arange(P)[:, None], np.arange(P)[None, :]
    same = p // HS == n // HS
    got = {
        "x": a["x"].reshape(TILES, P, D), "ctx": ctx.reshape(TILES, P, D),
        "encT": np.ascontiguousarray(ctx.reshape(B * S, KD, P).transpose(2, 1, 0)),
        "ident": np.eye(P, dtype=np.float32),
        "headmask": (np.arange(P)[:, None] // HD0 == np.arange(HB)[None, :]).astype(np.float32),
        "cols": np.ascontiguousarray(np.concatenate(cols, axis=1)), "rows": np.stack(rows),
        "ones": np.ones((1, P), np.float32),
        "mask_self": a["mask_1x1xSxS2_fc1"].reshape(S, S), "mask_cross": a["mask_Bx1xSxS2_ff1"].reshape(TILES, P, S),
        "w_qkv": block(L0("w_qkv")), "w_ao": block(L0("w_ao")), "w_q": block(L0("w_q")), "w_kv": block(L0("w_kv")),
        "w_co": block(L0("w_co")),
        "w1x1": np.ascontiguousarray(np.stack([L1(n) for n in ("Wn", "Wm", "Wl", "Wo")]).transpose(2, 0, 1)),
        "maa_w2": L3("maa_w2"), "maa_w1": block(L3("maa_w1")), "td_w1": block(L3("td_w1")), "td_w2": L3("td_w2"),
        "w_r": np.ascontiguousarray(np.stack([L3(n) for n in ("Wr", "Wk", "Wv", "Wg", "Wo", "Wfk", "Wfr", "Wfv")])
                                    .transpose(2, 0, 1).reshape(KD, P, 8, D).transpose(1, 2, 0, 3)),
        "s0": np.ascontiguousarray(ctx[:, 2:2 + HS, :].reshape(TILES, 2, KD, P, HS).transpose(3, 0, 4, 2, 1)
                                   .reshape(P, TILES, HS * 4)),
        "sel": np.stack([same & (p % HS == j) for j in range(HS)], axis=1).astype(np.float32),
        "gather": np.stack([same & (n % HS == j) for j in range(HS)], axis=1).astype(np.float32),
        "headsum": same.astype(np.float32),
    }
    got["mlp0_a"], got["mlp0_b"] = mlp(L0("w1"), L0("b1"), L0("w2"))
    got["mlp2_a"], got["mlp2_b"] = mlp(L2("w_fc1"), L2("b_fc1"), L2("w_fc2"))
    for i in (1, 2):
        got[f"heads{i}_a"], got[f"heads{i}_b"] = heads(i)
    return {k: np.ascontiguousarray(v) for k, v in got.items()}


def kernel(**inputs):
    import concourse.bacc as bacc
    from concourse.bass_utils import run_bass_kernel_spmd

    arrays = lay_out(inputs)
    nc = bacc.Bacc("TRN2", target_bir_lowering=False, num_devices=1)
    dram = {k: nc.dram_tensor(f"in_{k}", v.shape, F32, kind="ExternalInput").ap() for k, v in arrays.items()}
    out = nc.dram_tensor("out_x", (TILES, P, D), F32, kind="ExternalOutput").ap()
    build(nc, dram, out)
    result = run_bass_kernel_spmd(nc, [{f"in_{k}": v for k, v in arrays.items()}], core_ids=[0])
    return result.results[0]["out_x"].reshape(B, S, D)
```

```python
from contextlib import ExitStack

import concourse.bass as bass
from concourse import mybir

F32 = mybir.dt.float32
F32R = mybir.dt.float32r
ALU = mybir.AluOpType
ACT = mybir.ActivationFunctionType
AX = mybir.AxisListType.X

P = 128
B, S, D = 16, 64, 256
TILES = B * S // P
KD = D // P
STREAMS = 2
ROUNDS = TILES // STREAMS
EPS = 1e-5
MASKED = 10000.0

NH0, HD0 = 16, 16
HB = P // HD0
NH2, HD2 = 16, 128
T2 = S + 1
F = 1024
HS = 8
DM, ND = 32, 5
DD = 64

COLS = [("ln1_s", 2), ("ln1_b", 2), ("bq_self", 2), ("bk_self", 2), ("bv_self", 2), ("ln2_s", 2), ("ln2_b", 2),
        ("bq_cross", 2), ("bk_cross", 2), ("bv_cross", 2), ("ln3_s", 2), ("ln3_b", 2),
        ("bn", 1), ("bm", 1), ("bl", 1), ("bo", 1),
        ("w1_s", 2), ("w1_b", 2), ("w2_s", 2), ("w2_b", 2), ("wm_s", 2), ("wm_b", 2),
        ("r1_w", 2), ("r1_b", 2), ("r2_w", 2), ("r2_b", 2), ("maa_x", 2), ("maa_stack", 10), ("decay", 2),
        ("u", 2), ("ffn_k", 2), ("ffn_r", 2), ("pow", 1), ("one", 1)]
COL = {}
for _name, _n in COLS:
    COL[_name] = sum(n for m, n in COLS if m in COL)
NCOL = sum(n for _, n in COLS)
ROWS = ["b_ao", "b_co", "b2", "bo1", "bo2", "b_fc2", "gn_w", "gn_b"]
PACK_A = 3 * KD * P + 5
MLP_A = KD * P + 1


STEPS = {
    "attn0_in tensor": [],
    "attn0_in scalar": [],
    "attn0_in vector": ["self_stats", "self_mv", "self_eps", "self_xn"],
    "attn0_in gpsimd": ["self_rstd", "enc"],
    "attn0 tensor": [
        "self_turned", "self_q", "self_k0", "self_k1", "self_v", "self_scores0", "self_scores1", "self_pT0",
        "self_pT1", "self_ctx", "self_out", "cross_k0", "cross_k1", "cross_turned", "cross_q", "cross_v",
        "cross_scores0", "cross_scores1", "cross_pT0", "cross_pT1", "cross_ctx", "cross_out"
    ],
    "attn0 scalar": [
        "self_hT", "self_q", "self_k1", "self_v", "self_exp0", "self_exp1", "self_pT0", "self_pT1",
        "self_ctx", "cross_k1", "cross_hT", "cross_q", "cross_v", "cross_exp0", "cross_exp1", "cross_pT0",
        "cross_pT1", "cross_ctx"
    ],
    "attn0 vector": [
        "self_k0", "self_mul0", "self_masked0", "self_max0", "self_shifted0", "self_mul1", "self_masked1",
        "self_max1", "self_shifted1", "self_rc0", "self_p0", "self_psum1", "self_rc1", "self_p1", "self_sum",
        "cross_stats", "cross_mv", "cross_eps", "cross_xn", "cross_k0", "cross_mul0", "cross_masked0",
        "cross_max0", "cross_shifted0", "cross_mul1", "cross_masked1", "cross_max1", "cross_shifted1",
        "cross_rc0", "cross_p0", "cross_psum1", "cross_rc1", "cross_p1", "cross_sum", "mlp_stats", "mlp_mv",
        "mlp_eps", "mlp_xn"
    ],
    "attn0 gpsimd": ["cross_rstd", "mlp_rstd"],
    "attn0_rows tensor": ["mlp_turned"],
    "attn0_rows scalar": ["mlp_hT"],
    "attn0_rows vector": [],
    "attn0_rows gpsimd": [],
    "mlp0 tensor": ["fc1_0", "fc1_1", "fc2"],
    "mlp0 scalar": ["gelu0", "gelu1"],
    "mlp0 vector": ["g_high0", "g_low0", "g_high1", "g_low1"],
    "mlp0 gpsimd": ["w_high", "w", "wb_high", "wb"],
    "inorm_in tensor": [],
    "inorm_in scalar": [],
    "inorm_in vector": ["x_stats", "c_stats", "x_mv", "c_mv", "x_eps", "c_eps", "x_xn", "c_xn"],
    "inorm_in gpsimd": ["x_rstd", "c_rstd", "copy"],
    "inorm tensor": ["mmm", "scores", "pT0", "pT1", "mo", "out", "n_turned"],
    "inorm scalar": ["mm", "ml", "exp", "pT", "mo", "n_hT"],
    "inorm vector": ["max", "neg", "rc", "p", "pT", "sum", "n_stats", "n_mv", "n_eps", "n_xn"],
    "inorm gpsimd": ["n_rstd"],
    "heads1 tensor": ["q0", "q1", "k0", "k1", "scores", "v0", "v1", "pT", "ctx", "out"],
    "heads1 scalar": ["q0", "q1", "exp", "v0", "v1", "pT", "ctx0", "ctx1"],
    "heads1 vector": [
        "dv", "bv", "k_bias", "k0", "k1", "max", "bw", "shifted", "sum", "rc", "p", "pb", "pT", "ctx_low0",
        "ctx_low1"
    ],
    "heads1 gpsimd": ["w_high", "w", "wv_high", "wv", "wb_high", "wb"],
    "close1 tensor": ["bwT", "pbT", "acc"],
    "close1 scalar": [],
    "close1 vector": ["bw", "pb"],
    "close1 gpsimd": [],
    "norm2 tensor": ["turned0", "turned1", "turned2", "turned3"],
    "norm2 scalar": ["hT0", "hT1", "hT2"],
    "norm2 vector": ["mv", "eps", "xn0", "xn1", "xn2", "xn3", "hT"],
    "norm2 gpsimd": ["rstd"],
    "heads2 tensor": ["q0", "q1", "k0", "k1", "scores", "v0", "v1", "pT", "ctx", "out"],
    "heads2 scalar": ["q0", "q1", "exp", "v0", "v1", "pT", "ctx0", "ctx1"],
    "heads2 vector": [
        "dv", "bv", "k_bias", "k0", "k1", "max", "bw", "shifted", "sum", "rc", "p", "pb", "pT", "ctx_low0",
        "ctx_low1"
    ],
    "heads2 gpsimd": ["w_high", "w", "wv_high", "wv", "wb_high", "wb"],
    "close2 tensor": ["bwT", "pbT", "acc"],
    "close2 scalar": [],
    "close2 vector": ["bw", "pb"],
    "close2 gpsimd": [],
    "norm3 tensor": ["turned0", "turned1", "turned2", "turned3"],
    "norm3 scalar": ["hT0", "hT1", "hT2"],
    "norm3 vector": ["mv", "eps", "xn0", "xn1", "xn2", "xn3", "hT"],
    "norm3 gpsimd": ["rstd"],
    "mlp2 tensor": ["fc1_0", "fc1_1", "fc2"],
    "mlp2 scalar": ["gelu0", "gelu1"],
    "mlp2 vector": ["g_high0", "g_low0", "g_high1", "g_low1"],
    "mlp2 gpsimd": ["w_high", "w", "wb_high", "wb"],
    "rwkv_in tensor": [],
    "rwkv_in scalar": [],
    "rwkv_in vector": ["a_stats", "a_mv", "a_eps", "a_xn"],
    "rwkv_in gpsimd": ["a_rstd"],
    "rwkv tensor": [
        "a_turned", "lora", "mixes", "td1", "rkvg", "td2", "vrep", "o", "ogT", "yT", "wo", "f_turned", "kk",
        "rr", "ffn"
    ],
    "rwkv scalar": ["a_hT", "lora", "td1", "rkv", "g", "ew", "w", "gstd", "yT", "f_hT", "relu", "kk", "rr"],
    "rwkv vector": [
        "a_sx", "a_mul", "mix", "xm1", "xm2", "xm", "gate", "gates", "s0", "av", "scan", "rs", "cv", "og",
        "gsum", "cen", "sq", "gsq", "gvar", "grstd", "y1", "y2", "y", "x1", "f_stats", "f_mv", "f_eps",
        "f_xn", "f_sx", "f_mul", "mk", "mr1", "mr", "rf", "out"
    ],
    "rwkv gpsimd": ["rs", "f_rstd"],
}


class Steps:

    def __init__(self, sems, names):
        self.sems, self.names, self.seen = sems, names, [0] * len(sems)

    def did(self, name, u):
        assert name == self.names[self.seen[u] % len(self.names)], (name, self.names)
        self.seen[u] += 1
        return self.sems[u], 1

    def at(self, name, u, r):
        return self.sems[u], self.names.index(name) + 1 + r * len(self.names)


class Phase:
    def __init__(self, new_sem, name, orders):
        def steps(engine):
            return Steps([new_sem(f"{name}_{engine}_{u}") for u in range(STREAMS)], orders[f"{name} {engine}"])

        self.pe, self.act, self.vec, self.pool = (steps(e) for e in ("tensor", "scalar", "vector", "gpsimd"))


class Memory:
    pass


def bc(ap, axis, shape):
    return ap.unsqueeze(axis).to_broadcast(shape)




def norm_vec(vec, ph, m, r, rows):
    V, G = ph.vec, ph.pool
    vec.drain()
    for u, src, tag, dst, at in rows:
        vec.bn_stats(m.stats[u][:, at, :], src).then_inc(*V.did(tag + "_stats", u))
    vec.drain()
    for u, src, tag, dst, at in rows:
        vec.bn_aggr(m.mv[u][:, at, :], m.stats[u][:, at, :]).then_inc(*V.did(tag + "_mv", u))
    for u, src, tag, dst, at in rows:
        vec.wait_ge(*V.at(tag + "_mv", u, r))
        vec.tensor_scalar(m.rstd[u][:, at:at + 1], m.mv[u][:, at, 1:2], EPS, None, ALU.add)\
            .then_inc(*V.did(tag + "_eps", u))
    for u, src, tag, dst, at in rows:
        vec.wait_ge(*G.at(tag + "_rstd", u, r))
        vec.tensor_scalar(dst, src, m.mv[u][:, at, 0:1], m.rstd2[u][:, at:at + 1], ALU.subtract, ALU.mult)\
            .then_inc(*V.did(tag + "_xn", u))


def norm_pool(pool, ph, m, u, r, tag, stat=0):
    pool.wait_ge(*ph.vec.at(tag + "_eps", u, r))
    pool.tensor_tensor(m.rstd2[u][:, stat:stat + 1], m.rstd[u][:, stat:stat + 1], m.col("pow"), ALU.pow)\
        .then_inc(*ph.pool.did(tag + "_rstd", u))


def turn_tensor(pe, ph, m, u, r, tag, out, src=None):
    src = (src or m.xn)[u]
    for k in range(KD):
        last = pe.transpose(out[:, k * P:(k + 1) * P], src[:, k * P:(k + 1) * P], m.ident[:, :])
    last.then_inc(*ph.pe.did(tag + "_turned", u))


def turn_act(act, ph, m, u, r, tag, src, dst, scale, shift):
    act.wait_ge(*ph.pe.at(tag + "_turned", u, r))
    for k in range(KD):
        last = act.activation(dst(k), src[:, k * P:(k + 1) * P], ACT.Identity,
                              bias=m.col(shift, k), scale=m.col(scale, k))
    last.then_inc(*ph.act.did(tag + "_hT", u))




ATTN0 = ("self", "cross")
BY_HEAD = 0
WARM, WARM_RWKV = 4, 3


def later(r):
    return not isinstance(r, int)


def nothing(*stage):
    pass


def attn0_rounds(eng, enter=nothing, front=nothing, turn=nothing, scores=nothing, back=nothing, late=nothing,
                 keys=nothing, mlp_rows=nothing):
    def step(a, b, new=None):
        front(*a)
        if b:
            turn(*b)
        scores(*a)
        if new:
            enter(*new)
        if b:
            back(*b)
        late(*a, 0)
        if b and b[1] == "self":
            keys(b[0], "cross", b[2])
        late(*a, 1)

    def rest(r):
        step((1, "self", r), (0, "self", r))
        step((0, "cross", r), (1, "self", r))

    enter(0, 0)
    enter(1, 0)
    step((0, "self", 0), None)
    rest(0)
    with eng.Fori(1, ROUNDS) as r:
        step((1, "cross", r - 1), (0, "cross", r - 1), (0, r))
        step((0, "self", r), (1, "cross", r - 1), (1, r))
        rest(r)
    end = ROUNDS - 1
    step((1, "cross", end), (0, "cross", end))
    turn(1, "cross", end)
    back(1, "cross", end)
    for u in range(STREAMS):
        mlp_rows(u, end)


def keep_warm(pe, bank, x, n):
    for _ in range(n):
        pe.matmul(bank, x[:, 0:P], x, start=True, stop=True)


def attn0_tensor(pe, ph, ph_in, ph_rows, m):
    T, A, V, G = ph.pe, ph.act, ph.vec, ph.pool
    weights = {"self": (m.wqkv0[:, :, 0:D], m.wqkv0[:, :, D:2 * D], m.wqkv0[:, :, 2 * D:3 * D], m.wao0, "b_ao"),
               "cross": (m.wq0[:, :, :], m.wkv0[:, :, 0:D], m.wkv0[:, :, D:2 * D], m.wco0, "b_co")}

    def mlp_rows(u, r):
        pe.wait_ge(*V.at("mlp_xn", u, r))
        turn_tensor(pe, ph_rows, m, u, r, "mlp", m.ps[u][:, 0, :], m.xn_last)

    def turned(out, w, f, x):
        for k in range(KD):
            last = pe.matmul(out, w[:, k, f * P:(f + 1) * P], x[:, k, :], start=k == 0, stop=k == KD - 1)
        return last

    def keys(u, kind, r):
        if kind == "cross":
            pe.wait_ge(*ph_in.pool.at("enc", u, r))
        for f in range(KD):
            turned(m.ps[u][:, 2 + f, 0:P], weights[kind][1], f, m.hT_s[u] if kind == "self" else m.encT_t[u])\
                .then_inc(*T.did(f"{kind}_k{f}", u))
        if kind == "cross":
            keep_warm(pe, m.ps[u][:, 0, :], m.wqkv0[:, 0, 0:512], WARM)

    def front(u, kind, r):
        wq, _, wv, _, _ = weights[kind]
        x = m.hT_s[u] if kind == "self" else m.encT_t[u]
        pe.wait_ge(*(ph_in.vec if kind == "self" else V).at(kind + "_xn", u, r))
        turn_tensor(pe, ph, m, u, r, kind, m.ps[u][:, 0, :])
        pe.wait_ge(*A.at(kind + "_hT", u, r))
        if kind == "self" and later(r):
            pe.wait_ge(*V.at("cross_sum", u, r - 1))
        for f in range(KD):
            last = turned(m.ps[u][:, 1, f * P:(f + 1) * P], wq, f, m.hT_s[u])
        last.then_inc(*T.did(kind + "_q", u))
        if kind == "self":
            if later(r):
                mlp_rows(u, r - 1)
            keys(u, kind, r)
        pe.wait_ge(*V.at(kind + "_k0", u, r))
        for k in range(KD):
            last = pe.matmul(m.ps[u][:, 2, D:2 * D], x[:, k, :], wv[:, k, :], start=k == 0, stop=k == KD - 1)
        last.then_inc(*T.did(kind + "_v", u))

    def scores(u, kind, r):
        pe.wait_ge(*A.at(kind + "_q", u, r))
        if kind == "self" and later(r):
            pe.wait_ge(*ph_rows.act.at("mlp_hT", u, r - 1))
        for f in range(KD):
            if f == 1:
                pe.wait_ge(*A.at(kind + "_k1", u, r))
            for b in range(2):
                last = pe.matmul(m.ps[u][b * S:(b + 1) * S, f, :], m.qT0[u][:, f, b * S:(b + 1) * S],
                                 m.kdiag[u][:, f, b, :, :], start=True, stop=True)
            last.then_inc(*T.did(f"{kind}_scores{f}", u))

    def turn(u, kind, r):
        pe.wait_ge(*A.at(kind + "_v", u, r))
        for f in range(KD):
            pe.wait_ge(*V.at(f"{kind}_p{f}", u, r))
            for j in range(4):
                n = 4 * f + j
                last = pe.transpose(m.ps[u][:, 2 + f, j * P:(j + 1) * P], m.p0[u][:, 2 * n * S:(2 * n + 2) * S],
                                    m.ident[:, :])
            last.then_inc(*T.did(f"{kind}_pT{f}", u))

    def back(u, kind, r):
        _, _, _, wo, bias = weights[kind]
        pe.wait_ge(m.s_w0, 80)
        for f in range(KD):
            pe.wait_ge(*A.at(f"{kind}_pT{f}", u, r))
            for j in range(4):
                for b in range(2):
                    last = pe.matmul(m.ps[u][j * 2 * HD0:(j + 1) * 2 * HD0, 0, f * P + b * S:f * P + (b + 1) * S],
                                     m.vdiag[u][:, b, 4 * f + j, :], m.pT0[u][:, 4 * f + j, b * S:(b + 1) * S],
                                     start=True, stop=True)
        last.then_inc(*T.did(kind + "_ctx", u))
        pe.matmul(m.ps[u][:, 1, D:2 * D], m.ones[0:1, :], m.row(bias)[0:1, :], start=True, stop=False)
        pe.wait_ge(*A.at(kind + "_ctx", u, r))
        for k in range(KD):
            last = pe.matmul(m.ps[u][:, 1, D:2 * D], m.cT0[u][:, k, :], wo[:, k, :], start=False, stop=k == KD - 1)
        last.then_inc(*T.did(kind + "_out", u))
        if kind == "cross":
            keep_warm(pe, m.ps[u][:, 0, :], m.wqkv0[:, 0, 0:512], WARM)

    pe.wait_ge(m.s_zero, 1)
    keep_warm(pe, m.ps[0][:, 0, :], m.vdiag[0][:, :, :, :].rearrange("p b n c -> p (b n c)"), 10)
    pe.wait_ge(m.s_const, 16 * m.n_const)
    pe.wait_ge(m.s_wqkv, 16)
    attn0_rounds(pe, front=front, turn=turn, scores=scores, back=back, keys=keys, mlp_rows=mlp_rows)


def attn0_scalar(act, ph, ph_rows, m):
    T, A, V, G = ph.pe, ph.act, ph.vec, ph.pool

    def mlp_rows(u, r):
        turn_act(act, ph_rows, m, u, r, "mlp", m.ps[u][:, 0, :], lambda k: m.hT_of(k, u, r), "ln3_s", "ln3_b")

    def keys(u, kind, r):
        act.wait_ge(*T.at(kind + "_k1", u, r))
        k = m.ps[u][:, 3, 0:P].rearrange("p (b s) -> p b s", b=2)
        for h in range(HB):
            last = act.activation(m.kdiag[u][:, 1, :, h, :], k, ACT.Identity, scale=m.headmask[:, h:h + 1],
                                  bias=m.kmask[kind][:, h:h + 1])
        last.then_inc(*A.did(kind + "_k1", u))

    def front(u, kind, r):
        turn_act(act, ph, m, u, r, kind, m.ps[u][:, 0, :], lambda k: m.hT_s[u][:, k, :],
                 "ln1_s" if kind == "self" else "ln2_s", "ln1_b" if kind == "self" else "ln2_b")
        act.wait_ge(*T.at(kind + "_q", u, r))
        for f in range(KD):
            last = act.activation(m.qT0[u][:, f, :], m.ps[u][:, 1, f * P:(f + 1) * P], ACT.Identity,
                                  bias=m.col("bq_" + kind, f))
        last.then_inc(*A.did(kind + "_q", u))
        if kind == "self":
            if later(r):
                mlp_rows(u, r - 1)
            keys(u, kind, r)
        act.wait_ge(*T.at(kind + "_v", u, r))
        for b in range(2):
            for o in range(2):
                last = act.activation(m.vdiag[u][o * S:(o + 1) * S, b, :, o * HD0:(o + 1) * HD0],
                                      m.ps[u][b * S:(b + 1) * S, 2, D:2 * D].rearrange(
                                          "p (n o e) -> p n o e", o=2, e=HD0)[:, :, o, :], ACT.Copy)
        last.then_inc(*A.did(kind + "_v", u))

    def late(u, kind, r, f):
        act.wait_ge(*V.at(f"{kind}_shifted{f}", u, r))
        if f != BY_HEAD:
            p = m.p0[u][:, f * 512:(f + 1) * 512]
            act.activation(p, p, ACT.Exp).then_inc(*A.did(f"{kind}_exp{f}", u))
            return
        for h in range(f * HB, (f + 1) * HB):
            p = m.p0[u][:, h * S:(h + 1) * S]
            last = act.activation(p, p, ACT.Exp, bias=m.mx[u][:, h:h + 1], accum_out=m.sm[u][:, h:h + 1])
        last.then_inc(*A.did(f"{kind}_exp{f}", u))

    def turn(u, kind, r):
        for b in range(2):
            act.wait_ge(*T.at(f"{kind}_pT{b}", u, r))
            act.activation(m.pT0[u][:, 4 * b:4 * b + 4, :], m.ps[u][:, 2 + b, :], ACT.Copy)\
                .then_inc(*A.did(f"{kind}_pT{b}", u))

    def back(u, kind, r):
        act.wait_ge(*T.at(kind + "_ctx", u, r))
        for f in range(KD):
            last = act.activation(m.cT0[u][:, f, :], m.ps[u][:, 0, f * P:(f + 1) * P], ACT.Identity,
                                  bias=m.col("bv_" + kind, f))
        last.then_inc(*A.did(kind + "_ctx", u))

    act.wait_ge(m.s_const, 16 * m.n_const)
    act.wait_ge(m.s_masks, 1)
    act.wait_ge(m.s_zero, 1)
    attn0_rounds(act, front=front, turn=turn, back=back, late=late, keys=keys, mlp_rows=mlp_rows)


def attn0_vector(vec, ph, ph_in, m):
    T, A, V, G = ph.pe, ph.act, ph.vec, ph.pool
    half = [P, HB, S]

    def norm(u, kind, r, ph=ph):
        norm_vec(vec, ph, m, r, [(u, m.x_of(u, r), kind, (m.xn_last if kind == "mlp" else m.xn)[u][:, :], 0)])

    def probs(u, b):
        return m.p0[u][:, b * 512:(b + 1) * 512].rearrange("p (n t) -> p n t", t=S)

    def enter(u, r):
        norm(u, "self", r, ph_in)

    def keys(u, kind, r):
        vec.wait_ge(*T.at(kind + "_k0", u, r))
        for b in range(2):
            last = vec.scalar_tensor_tensor(
                out=m.kdiag[u][:, 0, b, :, :], in0=bc(m.ps[u][:, 2, b * S:(b + 1) * S], 1, half),
                scalar=m.col("bk_" + kind, 0), in1=bc(m.headmask[:, :], 2, half), op0=ALU.add, op1=ALU.mult)
        last.then_inc(*V.did(kind + "_k0", u))

    def front(u, kind, r):
        if kind == "self":
            keys(u, kind, r)

    def scores(u, kind, r):
        for b in range(2):
            s = m.ps[u][:, b, :].rearrange("p (n t) -> p n t", t=S)
            mul, add = (bc(x[kind] if kind == "self" else x[kind][:, m.tile(u, r), :], 1, half)
                        for x in (m.mask_mul, m.mask_add))
            mx, top = (x[u][:, b * HB:(b + 1) * HB] for x in (m.mx, m.rc))
            vec.wait_ge(*T.at(f"{kind}_scores{b}", u, r))
            vec.tensor_tensor(probs(u, b), s, mul, ALU.mult).then_inc(*V.did(f"{kind}_mul{b}", u))
            vec.wait_ge(*V.at(f"{kind}_mul{b}", u, r))
            vec.tensor_tensor(probs(u, b), probs(u, b), add, ALU.add).then_inc(*V.did(f"{kind}_masked{b}", u))
            vec.wait_ge(*V.at(f"{kind}_masked{b}", u, r))
            vec.tensor_reduce(top, probs(u, b), AX, ALU.max).then_inc(*V.did(f"{kind}_max{b}", u))
            vec.wait_ge(*V.at(f"{kind}_max{b}", u, r))
            if b == BY_HEAD:
                vec.tensor_scalar(mx, top, -1.0, None, ALU.mult).then_inc(*V.did(f"{kind}_shifted{b}", u))
            else:
                vec.tensor_tensor(probs(u, b), probs(u, b), bc(top, 2, half), ALU.subtract)\
                    .then_inc(*V.did(f"{kind}_shifted{b}", u))

    def late(u, kind, r, f):
        sums, rc = (x[u][:, f * HB:(f + 1) * HB] for x in (m.sm, m.rc))
        vec.wait_ge(*A.at(f"{kind}_exp{f}", u, r))
        if f != BY_HEAD:
            vec.tensor_reduce(sums, probs(u, f), AX, ALU.add).then_inc(*V.did(f"{kind}_psum{f}", u))
            vec.wait_ge(*V.at(f"{kind}_psum{f}", u, r))
        vec.reciprocal(rc, sums).then_inc(*V.did(f"{kind}_rc{f}", u))
        vec.wait_ge(*V.at(f"{kind}_rc{f}", u, r))
        vec.tensor_tensor(probs(u, f), probs(u, f), bc(rc, 2, half), ALU.mult).then_inc(*V.did(f"{kind}_p{f}", u))

    def back(u, kind, r):
        vec.wait_ge(*T.at(kind + "_out", u, r))
        vec.tensor_tensor(m.x_of(u, r), m.ps[u][:, 1, D:2 * D], m.x_of(u, r), ALU.add)\
            .then_inc(*V.did(kind + "_sum", u))
        norm(u, "cross" if kind == "self" else "mlp", r)

    vec.wait_ge(m.s_const, 16 * m.n_const)
    vec.wait_ge(m.s_mask, 48)
    for kind in ATTN0:
        vec.tensor_scalar(m.mask_add[kind], m.mask_mul[kind], MASKED, -MASKED, ALU.mult, ALU.add)
        vec.tensor_scalar(m.mask_mul[kind], m.mask_mul[kind], HD0 ** -0.5, None, ALU.mult)
        last = vec.tensor_scalar(m.kmask[kind][:, :], m.headmask[:, :], m.col("bk_" + kind, 1), None, ALU.mult)
    last.then_inc(m.s_masks, 1)
    vec.wait_ge(m.s_masks, 1)
    vec.wait_ge(m.s_x, 16)
    attn0_rounds(vec, enter=enter, front=front, scores=scores, back=back, late=late,
                 keys=keys)


def attn0_gpsimd(pool, ph, ph_in, m):

    def enter(u, r):
        norm_pool(pool, ph_in, m, u, r, "self")
        pool.tensor_copy(m.encT_t[u][:, :, :], m.encT_of(u, r)).then_inc(*ph_in.pool.did("enc", u))

    def back(u, kind, r):
        norm_pool(pool, ph, m, u, r, "cross" if kind == "self" else "mlp")

    pool.wait_ge(m.s_const, 16 * m.n_const)
    pool.wait_ge(m.s_enc, 16)
    attn0_rounds(pool, enter=enter, back=back)




def start_acc(pe, m, row):
    for u in range(STREAMS):
        for c in range(2):
            pe.matmul(m.ps[u][:, 2 + c, :], m.ones[0:1, :], bc(m.row(row)[0:1, :], 1, [1, 2, D]),
                      start=True, stop=True)


def stream_in(sp, m, ph, pack_a, pack_b, width, rounds, free_a, free_b, before):
    for sem, value in before:
        sp.wait_ge(sem, value)
    for u in range(STREAMS):
        sp.dma_start(m.wa[u][:, 0:width], pack_a[u]).then_inc(m.s_wa[u], 16)
        sp.dma_start(m.wb[u][:, :], pack_b[u]).then_inc(m.s_wb[u], 16)
    with sp.Fori(0, rounds - 1) as r:
        for u in range(STREAMS):
            for steps, name in free_a:
                sp.wait_ge(*steps.at(name, u, r))
            sp.wait_ge(m.s_wa[u], 16)
            sp.dma_start(m.wa[u][:, 0:width], pack_a[2 * r + 2 + u]).then_inc(m.s_wa[u], 16)
        for u in range(STREAMS):
            for steps, name in free_b:
                sp.wait_ge(*steps.at(name, u, r))
            sp.wait_ge(m.s_wb[u], 16)
            sp.dma_start(m.wb[u][:, :], pack_b[2 * r + 2 + u]).then_inc(m.s_wb[u], 16)




PARTS = ((0, 0), (0, 1), (1, 0))


def split_weights_gpsimd(pool, ph, m, loads, rounds, width, product_a, product_b, values=False):
    T, G = ph.pe, ph.pool

    def round_of(r, again):
        for u in range(STREAMS):
            high, low = (x[:, 0:width] for x in m.w_parts[u])
            pool.wait_ge(m.s_wa[u], 16 * (loads + 1) + r * 16)
            if again:
                pool.wait_ge(*T.at(product_a, u, r - 1))
            pool.tensor_tensor(high, m.wa[u][:, 0:width], m.col("one").to_broadcast([P, width]), ALU.mult)\
                .then_inc(*G.did("w_high", u))
            pool.wait_ge(*G.at("w_high", u, r))
            pool.tensor_tensor(low, m.wa[u][:, 0:width], high.bitcast(F32), ALU.subtract).then_inc(*G.did("w", u))
        if values:
            for u in range(STREAMS):
                high, low = (x[:, :, u * P:(u + 1) * P] for x in m.wv_parts)
                src = m.wa[u][:, 2 * KD * P:3 * KD * P].rearrange("p (k q) -> p k q", q=P)
                if again:
                    pool.wait_ge(*T.at("v1", 1, r - 1))
                pool.tensor_tensor(high, src, bc(m.col("one"), 1, [P, KD, P]), ALU.mult)\
                    .then_inc(*G.did("wv_high", u))
                pool.wait_ge(*G.at("wv_high", u, r))
                pool.tensor_tensor(low, src, high.bitcast(F32), ALU.subtract).then_inc(*G.did("wv", u))
        for u in range(STREAMS):
            high, low = (x[:, :] for x in m.wb_parts[u])
            pool.wait_ge(m.s_wb[u], 16 * (loads + 1) + r * 16)
            if again:
                pool.wait_ge(*T.at(product_b, u, r - 1))
            pool.tensor_tensor(high, m.wb[u][:, :], m.col("one").to_broadcast([P, D]), ALU.mult)\
                .then_inc(*G.did("wb_high", u))
            pool.wait_ge(*G.at("wb_high", u, r))
            pool.tensor_tensor(low, m.wb[u][:, :], high.bitcast(F32), ALU.subtract).then_inc(*G.did("wb", u))

    round_of(0, False)
    with pool.Fori(1, rounds) as r:
        round_of(r, True)


def split_rows(eng, m, c, done, before):
    high, low = (x[:, :, c * 512:(c + 1) * 512] for x in m.h_parts)
    src = m.hT[:, :, c * 512:(c + 1) * 512]
    for sem, value in before:
        eng.wait_ge(sem, value)
    eng.tensor_copy(high, src).then_inc(m.s_h[c], 1)
    eng.wait_ge(m.s_h[c], done + 1)
    eng.tensor_tensor(low, src, high.bitcast(F32), ALU.subtract).then_inc(m.s_h[c], 1)




def mlp_tensor(pe, ph, m, row, loads, rows_split, before):
    T, A = ph.pe, ph.act
    for sem, value in before:
        pe.wait_ge(sem, value)
    start_acc(pe, m, row)
    with pe.Fori(0, F // P // 2) as r:
        for u in range(STREAMS):
            pe.wait_ge(*ph.pool.at("w", u, r))
            for c in range(2):
                pe.wait_ge(m.s_h[c], rows_split)
                for n, (w, x) in enumerate(PARTS):
                    for k in range(KD):
                        last = pe.matmul(m.ps[u][:, c, :], m.w_parts[u][w][:, k * P:(k + 1) * P],
                                         m.h_parts[x][:, k, c * 512:(c + 1) * 512], start=n == k == 0,
                                         stop=n == len(PARTS) - 1 and k == KD - 1)
                last.then_inc(*T.did(f"fc1_{c}", u))
        for u in range(STREAMS):
            pe.wait_ge(*ph.pool.at("wb", u, r))
            for t in range(TILES):
                if t % 4 == 0:
                    pe.wait_ge(*ph.vec.at(f"g_low{t // 4}", u, r))
                for w, g in PARTS:
                    last = pe.matmul(m.acc(t), m.g_parts[g][u][:, t * P:(t + 1) * P], m.wb_parts[u][w][:, :],
                                     start=False, stop=False, skip_group_check=True)
            last.then_inc(*T.did("fc2", u))


def mlp_scalar(act, ph, m, gelu):
    with act.Fori(0, F // P // 2) as r:
        for u in range(STREAMS):
            for c in range(2):
                act.wait_ge(*ph.pe.at(f"fc1_{c}", u, r))
                act.activation(m.g[u][:, c * 512:(c + 1) * 512], m.ps[u][:, c, :], gelu,
                               bias=m.wa[u][:, KD * P:KD * P + 1]).then_inc(*ph.act.did(f"gelu{c}", u))


def mlp_vector(vec, ph, m):
    with vec.Fori(0, F // P // 2) as r:
        for u in range(STREAMS):
            for c in range(2):
                g, high, low = (x[:, c * 512:(c + 1) * 512] for x in (m.g[u], m.g_parts[0][u], m.g_parts[1][u]))
                vec.wait_ge(*ph.act.at(f"gelu{c}", u, r))
                vec.tensor_copy(high, g).then_inc(*ph.vec.did(f"g_high{c}", u))
                vec.wait_ge(*ph.vec.at(f"g_high{c}", u, r))
                vec.tensor_tensor(low, g, high.bitcast(F32), ALU.subtract).then_inc(*ph.vec.did(f"g_low{c}", u))


def add_acc_vector(vec, m, sem, before):
    for s, value in before:
        vec.wait_ge(s, value)
    for u in range(STREAMS):
        xs = m.x[:, :, :].rearrange("p (r u) d -> p r u d", u=2)[:, :, u, :]
        vec.tensor_tensor(xs, m.ps[u][:, 2:4, :].rearrange("p c (r d) -> p (c r) d", d=D), xs, ALU.add)\
            .then_inc(sem, 1)




SHARED = ((0, 2), (1, 3), (4, 6), (5, 7))


def norm_all_vector(vec, ph, m, scale, shift, before, split_done):
    V, G = ph.vec, ph.pool
    for sem, value in before:
        vec.wait_ge(sem, value)
    vec.drain()
    for t in range(TILES):
        vec.bn_stats(m.all_stats[:, t, :], m.x[:, t, :])
    vec.drain()
    for t in range(TILES):
        last = vec.bn_aggr(m.all_mv[:, t, :], m.all_stats[:, t, :])
    last.then_inc(*V.did("mv", 0))
    vec.wait_ge(*V.at("mv", 0, 0))
    vec.tensor_scalar(m.all_rstd[:, 0, :], m.all_mv[:, :, 1], EPS, None, ALU.add).then_inc(*V.did("eps", 0))
    vec.wait_ge(*G.at("rstd", 0, 0))
    for i, tiles in enumerate(SHARED):
        for t in tiles:
            last = vec.tensor_scalar(m.all_xn[:, t, :], m.x[:, t, :], m.all_mv[:, t, 0:1],
                                     m.all_rstd[:, 1, t:t + 1], ALU.subtract, ALU.mult)
        last.then_inc(*V.did(f"xn{i}", 0))
    split_rows(vec, m, 0, split_done, [ph.act.at("hT1", 0, 0)])
    i = len(SHARED) - 1
    vec.wait_ge(*ph.pe.at(f"turned{i}", 0, 0))
    for k in range(KD):
        last = vec.tensor_scalar(m.hT_pair(k, i), m.turned(k, i), m.col(scale, k), m.col(shift, k), ALU.mult, ALU.add)
    last.then_inc(*V.did("hT", 0))
    split_rows(vec, m, 1, split_done, norm_all_done(ph))


def norm_all_gpsimd(pool, ph, m):
    pool.wait_ge(*ph.vec.at("eps", 0, 0))
    pool.tensor_tensor(m.all_rstd[:, 1, :], m.all_rstd[:, 0, :], m.col("pow").to_broadcast([P, TILES]), ALU.pow)\
        .then_inc(*ph.pool.did("rstd", 0))


def norm_all_tensor(pe, ph, m):
    for i, tiles in enumerate(SHARED):
        pe.wait_ge(*ph.vec.at(f"xn{i}", 0, 0))
        for n, t in enumerate(tiles):
            for k in range(KD):
                last = pe.transpose(m.ps[i % 2][:, i // 2, (2 * n + k) * P:(2 * n + k + 1) * P],
                                    m.all_xn[:, t, k * P:(k + 1) * P], m.ident[:, :])
        last.then_inc(*ph.pe.did(f"turned{i}", 0))


def norm_all_scalar(act, ph, m, scale, shift):
    for i in range(len(SHARED) - 1):
        act.wait_ge(*ph.pe.at(f"turned{i}", 0, 0))
        for k in range(KD):
            last = act.activation(m.hT_pair(k, i), m.turned(k, i), ACT.Identity, bias=m.col(shift, k),
                                  scale=m.col(scale, k))
        last.then_inc(*ph.act.did(f"hT{i}", 0))


def norm_all_done(ph):
    return [ph.act.at("hT2", 0, 0), ph.vec.at("hT", 0, 0)]




def split_context_gpsimd(pool, m):
    high, low = (x[:, :, :] for x in m.enc_parts)
    pool.wait_ge(m.s_enc, 16)
    pool.tensor_copy(high, m.encT[:, :, :]).then_inc(m.s_split, 1)
    pool.wait_ge(m.s_split, 1)
    pool.tensor_tensor(low, m.encT[:, :, :], high.bitcast(F32), ALU.subtract).then_inc(m.s_split, 1)


def heads_tensor(pe, ph, m, row, loads, rows_split, before):
    T, A, V = ph.pe, ph.act, ph.vec
    for sem, value in before:
        pe.wait_ge(sem, value)
    start_acc(pe, m, row)
    with pe.Fori(0, NH2 // 2) as r:
        for u in range(STREAMS):
            pe.wait_ge(m.s_wa[u], 16 * (loads + 1) + r * 16)
            pe.wait_ge(*ph.pool.at("w", u, r))
            for q, rows in enumerate((m.h_parts, m.enc_parts)):
                for c in range(2):
                    if q == 0:
                        pe.wait_ge(m.s_h[c], rows_split)
                    else:
                        pe.wait_ge(*A.at(f"q{c}", u, r))
                    for n, (w, x) in enumerate(PARTS):
                        for k in range(KD):
                            last = pe.matmul(m.ps[u][:, c, :],
                                             m.w_parts[u][w][:, (KD * q + k) * P:(KD * q + k + 1) * P],
                                             rows[x][:, k, c * 512:(c + 1) * 512], start=n == k == 0,
                                             stop=n == len(PARTS) - 1 and k == KD - 1)
                    last.then_inc(*T.did(f"{'qk'[q]}{c}", u))
        for u in range(STREAMS):
            pe.wait_ge(*V.at("k1", u, r))
            for t in range(TILES):
                for b in range(2):
                    last = pe.matmul(m.ps[u][b * S:(b + 1) * S, t // 4, (t % 4) * T2:(t % 4 + 1) * T2],
                                     m.qT[u][:, t * P + b * S:t * P + (b + 1) * S], m.kT[u][:, t, b, :],
                                     start=True, stop=True)
            pe.wait_ge(m.s_wb[u], 16 * (loads + 1) + r * 16)
            for f in range(KD):
                last = pe.matmul(m.ps[u][:, 1, 300 + f:301 + f], m.wb[u][:, f * P:(f + 1) * P], m.dv[u][:, :],
                                 start=True, stop=True)
            last.then_inc(*T.did("scores", u))
        for u in range(STREAMS):
            pe.wait_ge(*ph.pool.at("wv", u, r))
        for half in range(STREAMS):
            pe.wait_ge(*V.at("shifted", half, r))
            for t in range(4):
                tile = 4 * half + t
                for n, (w, x) in enumerate(PARTS):
                    for k in range(KD):
                        last = pe.matmul(m.ps[half][:, t // 2, (t % 2) * 2 * P:(t % 2 + 1) * 2 * P],
                                         m.enc_parts[x][:, k, tile * P:(tile + 1) * P], m.wv_parts[w][:, k, :],
                                         start=n == k == 0, stop=n == len(PARTS) - 1 and k == KD - 1)
                if t % 2 == 1:
                    last.then_inc(*T.did(f"v{t // 2}", half))
        for u in range(STREAMS):
            pe.wait_ge(*V.at("p", u, r))
            pe.wait_ge(*A.at("v0", u, r))
            for j in range(TILES // 2):
                last = pe.transpose(m.ps[u][:, 0, j * P:(j + 1) * P], m.pn[u][:, 2 * j:2 * j + 2, :], m.ident[:, :])
            last.then_inc(*T.did("pT", u))
        for u in range(STREAMS):
            pe.wait_ge(*A.at("pT", u, r))
            pe.wait_ge(*V.at("pT", u, r))
            for t in range(TILES):
                last = pe.matmul(m.ps[u][:, t // 4, (t % 4) * P:(t % 4 + 1) * P], m.v[t // 4][:, t % 4, u, :],
                                 m.pT[u][:, t, :, :], start=True, stop=True)
            last.then_inc(*T.did("ctx", u))
        for u in range(STREAMS):
            pe.wait_ge(*ph.pool.at("wb", u, r))
            for t in range(TILES):
                if t % 4 == 0:
                    pe.wait_ge(*V.at(f"ctx_low{t // 4}", u, r))
                for w, c in PARTS:
                    last = pe.matmul(m.acc(t), m.cT_parts[c][u][:, t, :], m.wb_parts[u][w][:, :],
                                     start=False, stop=False, skip_group_check=True)
            last.then_inc(*T.did("out", u))


def heads_scalar(act, ph, m):
    T, A, V = ph.pe, ph.act, ph.vec
    with act.Fori(0, NH2 // 2) as r:
        for u in range(STREAMS):
            for c in range(2):
                act.wait_ge(*T.at(f"q{c}", u, r))
                act.activation(m.qT[u][:, c * 512:(c + 1) * 512], m.ps[u][:, c, :], ACT.Identity,
                               bias=m.head_col(u, 0)).then_inc(*A.did(f"q{c}", u))
        for u in range(STREAMS):
            act.wait_ge(*V.at("shifted", u, r))
            act.activation(m.p[u][:, :, :], m.p[u][:, :, :], ACT.Exp, scale=HD2 ** -0.5).then_inc(*A.did("exp", u))
        for u in range(STREAMS):
            for c in range(2):
                act.wait_ge(*T.at(f"v{c}", u, r))
                act.activation(m.v[u][:, 2 * c:2 * c + 2, :, :], m.ps[u][:, c, :], ACT.Copy)\
                    .then_inc(*A.did(f"v{c}", u))
        for u in range(STREAMS):
            act.wait_ge(*T.at("pT", u, r))
            turn_probs(lambda o, i: act.activation(o, i, ACT.Copy), m, u, 0).then_inc(*A.did("pT", u))
        for u in range(STREAMS):
            act.wait_ge(*T.at("ctx", u, r))
            for c in range(2):
                act.activation(m.cT_parts[0][u][:, 4 * c:4 * c + 4, :], m.ps[u][:, c, :], ACT.Identity,
                               bias=m.bv[u][:, :]).then_inc(*A.did(f"ctx{c}", u))


def turn_probs(copy, m, u, odd):
    src = m.ps[u][:, 0, :].rearrange("p (j b q) -> p j b q", b=2, q=S)
    for b in range(2):
        dst = m.pT[u][b * S:(b + 1) * S, :, b, :].rearrange("p (j o) q -> p j o q", o=2)
        last = copy(dst[:, :, odd, :], src[odd * S:(odd + 1) * S, :, b, :])
    return last


def heads_vector(vec, ph, m, loads):
    T, A, V = ph.pe, ph.act, ph.vec
    for u in range(STREAMS):
        vec.memset(m.pT[u][:, :, :, :], 0.0).then_inc(m.s_pT, 1)
    with vec.Fori(0, NH2 // 2) as r:
        for u in range(STREAMS):
            vec.wait_ge(m.s_wa[u], 16 * (loads + 1) + r * 16)
            vec.tensor_tensor(m.dv[u][:, :], m.head_col(u, 4), m.head_col(u, 2), ALU.subtract)\
                .then_inc(*V.did("dv", u))
            for c in range(2):
                vec.wait_ge(*T.at(f"k{c}", u, r))
                if c == 0:
                    vec.tensor_copy(m.bv[u][:, :], m.head_col(u, 2)).then_inc(*V.did("bv", u))
                    vec.tensor_copy(m.kT[u][:, :, :, S], bc(m.head_col(u, 3), 1, [P, TILES, 2])).then_inc(
                        *V.did("k_bias", u))
                vec.tensor_scalar(m.kT[u][:, 4 * c:4 * c + 4, :, 0:S],
                                  m.ps[u][:, c, :].rearrange("p (t b k) -> p t b k", b=2, k=S),
                                  m.head_col(u, 1), None, ALU.add).then_inc(*V.did(f"k{c}", u))
        for u in range(STREAMS):
            s = m.ps[u][:, 0:2, 0:4 * T2].rearrange("p c (t k) -> p c t k", k=T2)
            p = m.p[u][:, :, :].rearrange("p (c t) k -> p c t k", c=2)
            mx = m.mx[u][:, 0:TILES].rearrange("p (c t) -> p c t", c=2)
            vec.wait_ge(*T.at("scores", u, r))
            vec.tensor_reduce(mx, s, AX, ALU.max).then_inc(*V.did("max", u))
            vec.tensor_scalar(m.bwT[:, :, bass.ds(2 * r + u, 1)], bc(m.ps[u][:, 1, 300:302], 2, [P, 2, 1]),
                              1.0, None, ALU.mult).then_inc(*V.did("bw", u))
            vec.wait_ge(*V.at("max", u, r))
            vec.tensor_tensor(p, s, bc(mx, 3, [P, 2, 4, T2]), ALU.subtract).then_inc(*V.did("shifted", u))
        for u in range(STREAMS):
            p = m.p[u][:, :, :]
            vec.wait_ge(*A.at("exp", u, r))
            vec.tensor_reduce(m.sm[u][:, 0:TILES], p, AX, ALU.add).then_inc(*V.did("sum", u))
            vec.wait_ge(*V.at("sum", u, r))
            vec.reciprocal(m.rc[u][:, 0:TILES], m.sm[u][:, 0:TILES]).then_inc(*V.did("rc", u))
            vec.wait_ge(*V.at("rc", u, r))
            vec.tensor_tensor(m.pn[u][:, :, :], p[:, :, 0:S], bc(m.rc[u][:, 0:TILES], 2, [P, TILES, S]), ALU.mult)\
                .then_inc(*V.did("p", u))
            vec.tensor_tensor(m.pb[:, :, bass.ds(2 * r + u, 1)], p[:, :, S:T2],
                              m.rc[u][:, 0:TILES].unsqueeze(2), ALU.mult).then_inc(*V.did("pb", u))
        for u in range(STREAMS):
            vec.wait_ge(*T.at("pT", u, r))
            turn_probs(vec.tensor_copy, m, u, 1).then_inc(*V.did("pT", u))
        for u in range(STREAMS):
            for c in range(2):
                high, low = (x[u][:, 4 * c:4 * c + 4, :].rearrange("p t q -> p (t q)") for x in m.cT_parts)
                vec.wait_ge(*A.at(f"ctx{c}", u, r))
                vec.scalar_tensor_tensor(out=low, in0=m.ps[u][:, c, :], scalar=m.bv[u][:, :],
                                         in1=high.bitcast(F32), op0=ALU.add, op1=ALU.subtract)\
                    .then_inc(*V.did(f"ctx_low{c}", u))


def bias_token_tensor(pe, ph, cl, m):
    V = ph.vec
    for u in range(STREAMS):
        pe.wait_ge(*V.at("ctx_low1", u, NH2 // 2 - 1))
    for f in range(KD):
        last = pe.transpose(m.ps[0][0:NH2, 0, f * P:(f + 1) * P], m.bwT[:, f, :], m.ident[:, :])
    last.then_inc(*cl.pe.did("bwT", 0))
    for t in range(TILES):
        last = pe.transpose(m.ps[1][0:NH2, t // 4, (t % 4) * P:(t % 4 + 1) * P], m.pb[:, t, :], m.ident[:, :])
    last.then_inc(*cl.pe.did("pbT", 0))
    pe.wait_ge(*cl.vec.at("bw", 0, 0))
    pe.wait_ge(*cl.vec.at("pb", 0, 0))
    for t in range(TILES):
        last = pe.matmul(m.acc(t), m.pbT[:, t * P:(t + 1) * P], m.bw[:, :], start=False, stop=False,
                         skip_group_check=True)
    last.then_inc(*cl.pe.did("acc", 0))


def bias_token_vector(vec, cl, m):
    vec.wait_ge(*cl.pe.at("bwT", 0, 0))
    vec.tensor_copy(m.bw[:, :], m.ps[0][0:NH2, 0, 0:D]).then_inc(*cl.vec.did("bw", 0))
    vec.wait_ge(*cl.pe.at("pbT", 0, 0))
    vec.tensor_copy(m.pbT[:, :], m.ps[1][0:NH2, 0:2, :].rearrange("p c n -> p (c n)")).then_inc(*cl.vec.did("pb", 0))




def inorm_tensor(pe, ph, ph_in, m, before):
    T, A, V, G = ph.pe, ph.act, ph.vec, ph.pool
    for sem, value in before:
        pe.wait_ge(sem, value)
    with pe.Fori(0, ROUNDS) as r:
        for u in range(STREAMS):
            pe.wait_ge(*ph_in.vec.at("c_xn", u, r))
            pe.wait_ge(*ph_in.pool.at("copy", u, r))
            for n, x in enumerate((m.xn[u], m.cn[u])):
                last = pe.matmul(m.ps[u][:, 0, n * D:(n + 1) * D], m.w1x1[:, n, :], x[:, :], start=True, stop=True)
            for c in range(2):
                last = pe.matmul(m.ps[u][:, 1, c * P:(c + 1) * P], m.ctx_t[u][:, c * P:(c + 1) * P], m.w1x1[:, 2, :],
                                 start=True, stop=True)
            last.then_inc(*T.did("mmm", u))
        for u in range(STREAMS):
            pe.wait_ge(*A.at("mm", u, r))
            for b in range(2):
                half = slice(b * S, (b + 1) * S)
                for c in range(2):
                    last = pe.matmul(m.ps[u][:, 2 + b, c * D:(c + 1) * D], m.mnm[u][half, c * P:(c + 1) * P],
                                     m.mnm[u][half, D:2 * D], start=True, stop=True)
            last.then_inc(*T.did("scores", u))
        for u in range(STREAMS):
            pe.wait_ge(*V.at("p", u, r))
            pe.wait_ge(*A.at("ml", u, r))
            for b in range(2):
                for s in range(2):
                    for c in range(2):
                        last = pe.transpose(m.ps[u][:, b, s * D + c * P:s * D + (c + 1) * P],
                                            m.p1[u][:, 2 * b + c, s * P:(s + 1) * P], m.ident[:, :])
                last.then_inc(*T.did(f"pT{b}", u))
        for u in range(STREAMS):
            for b in range(2):
                pe.wait_ge(*(A, V)[b].at("pT", u, r))
                for s in range(2):
                    last = pe.matmul(m.ps[u][b * S:(b + 1) * S, 2, 0:D], m.mlT[u][:, s, b * S:(b + 1) * S],
                                     m.p1T[u][:, b, s * D:(s + 1) * D], start=s == 0, stop=s == 1)
            last.then_inc(*T.did("mo", u))
        for u in range(STREAMS):
            pe.wait_ge(*A.at("mo", u, r))
            pe.matmul(m.ps[u][:, 3, 0:D], m.w1x1[:, 3, :], m.mo[u][:, :], start=True, stop=True)\
                .then_inc(*T.did("out", u))
        for u in range(STREAMS):
            pe.wait_ge(*V.at("n_xn", u, r))
            turn_tensor(pe, ph, m, u, r, "n", m.ps[u][:, 3, :], m.xn_last)


def inorm_scalar(act, ph, m):
    T, A, V, G = ph.pe, ph.act, ph.vec, ph.pool
    with act.Fori(0, ROUNDS) as r:
        for u in range(STREAMS):
            act.wait_ge(*T.at("mmm", u, r))
            for n, bias in enumerate(("bn", "bm")):
                last = act.activation(m.mnm[u][:, n * D:(n + 1) * D], m.ps[u][:, 0, n * D:(n + 1) * D], ACT.Identity,
                                      bias=m.col(bias))
            last.then_inc(*A.did("mm", u))
            act.activation(m.mlT[u][:, :, :], m.ps[u][:, 1, 0:2 * P], ACT.Copy).then_inc(*A.did("ml", u))
        for u in range(STREAMS):
            act.wait_ge(*V.at("neg", u, r))
            for n in range(4):
                last = act.activation(m.p1[u][:, n, :], m.ps[u][:, 2 + n // 2, (n % 2) * D:(n % 2 + 1) * D], ACT.Exp,
                                      bias=m.mx[u][:, n:n + 1], accum_out=m.sm[u][:, n:n + 1])
            last.then_inc(*A.did("exp", u))
        for u in range(STREAMS):
            act.wait_ge(*T.at("pT0", u, r))
            act.activation(m.p1T[u][:, 0, :], m.ps[u][:, 0, :], ACT.Copy).then_inc(*A.did("pT", u))
        for u in range(STREAMS):
            act.wait_ge(*T.at("mo", u, r))
            act.activation(m.mo[u][:, :], m.ps[u][:, 2, 0:D], ACT.Identity, bias=m.col("bl"))\
                .then_inc(*A.did("mo", u))
        for u in range(STREAMS):
            turn_act(act, ph, m, u, r, "n", m.ps[u][:, 3, :], lambda k: m.hT_of(k, u, r), "w1_s", "w1_b")


def inorm_vector(vec, ph, ph_in, m, before):
    T, A, V, G = ph.pe, ph.act, ph.vec, ph.pool
    for sem, value in before:
        vec.wait_ge(sem, value)

    def norm(r):
        norm_vec(vec, ph_in, m, r, [row for u in range(STREAMS) for row in (
            (u, m.x_of(u, r), "x", m.xn[u][:, :], 0), (u, m.ctx_of(u, r), "c", m.cn[u][:, :], 1))])

    def round_of(r, more):
        for u in range(STREAMS):
            s = m.ps[u][:, 2:4, :].rearrange("p b (c s) -> p (b c) s", c=2)
            vec.wait_ge(*T.at("scores", u, r))
            vec.tensor_reduce(m.rc[u][:, 0:4], s, AX, ALU.max).then_inc(*V.did("max", u))
            vec.wait_ge(*V.at("max", u, r))
            vec.tensor_scalar(m.mx[u][:, 0:4], m.rc[u][:, 0:4], -1.0, None, ALU.mult).then_inc(*V.did("neg", u))
        for u in range(STREAMS):
            vec.wait_ge(*A.at("exp", u, r))
            vec.reciprocal(m.rc[u][:, 0:4], m.sm[u][:, 0:4]).then_inc(*V.did("rc", u))
            vec.wait_ge(*V.at("rc", u, r))
            vec.tensor_tensor(m.p1[u][:, :, :], m.p1[u][:, :, :], bc(m.rc[u][:, 0:4], 2, [P, 4, D]), ALU.mult)\
                .then_inc(*V.did("p", u))
        for u in range(STREAMS):
            vec.wait_ge(*T.at("pT1", u, r))
            vec.tensor_copy(m.p1T[u][:, 1, :], m.ps[u][:, 1, :]).then_inc(*V.did("pT", u))
        if more:
            norm(r + 1)
        for u in range(STREAMS):
            vec.wait_ge(*T.at("out", u, r))
            vec.scalar_tensor_tensor(out=m.x_of(u, r), in0=m.ps[u][:, 3, 0:D], scalar=m.col("bo"), in1=m.x_of(u, r),
                                     op0=ALU.add, op1=ALU.add).then_inc(*V.did("sum", u))
        norm_vec(vec, ph, m, r, [(u, m.x_of(u, r), "n", m.xn_last[u][:, :], 0) for u in range(STREAMS)])

    norm(0)
    with vec.Fori(0, ROUNDS - 1) as r:
        round_of(r, True)
    round_of(ROUNDS - 1, False)


def inorm_gpsimd(pool, ph, ph_in, m, before):
    def norm(r):
        for u in range(STREAMS):
            norm_pool(pool, ph_in, m, u, r, "x")
            norm_pool(pool, ph_in, m, u, r, "c", stat=1)
        for u in range(STREAMS):
            pool.tensor_copy(m.ctx_t[u][:, :], m.ctx_of(u, r)).then_inc(*ph_in.pool.did("copy", u))

    def norm_out(r):
        for u in range(STREAMS):
            norm_pool(pool, ph, m, u, r, "n")

    for sem, value in before:
        pool.wait_ge(sem, value)
    norm(0)
    with pool.Fori(1, ROUNDS) as r:
        norm(r)
        norm_out(r - 1)
    norm_out(ROUNDS - 1)




MIX_K, MIX_W, MIX_V, MIX_R, MIX_G = range(ND)
W_R, W_K, W_V, W_G, W_O, W_FK, W_FR, W_FV = range(8)


def rwkv_rounds(eng, norm=nothing, rows=nothing, mixed=nothing, lora=nothing, mixes=nothing, project=nothing,
                spread=nothing, scan=nothing, gather=nothing, heads=nothing, gated=nothing, attended=nothing,
                norm_out=nothing, shifted=nothing, ffn=nothing, close=nothing):
    def both(r, *stages):
        for stage in stages:
            for u in range(STREAMS):
                stage(u, r)

    def round_of(r, more):
        both(r, rows, mixed, lora, mixes, project, spread, scan)
        gather(0, r)
        heads(0, r)
        gather(1, r)
        gated(0, r)
        heads(1, r)
        gated(1, r)
        both(r, attended)
        norm_out(r)
        both(r, shifted, ffn)
        if more:
            norm(r + 1)
        both(r, close)

    norm(0)
    if norm is nothing:
        with eng.Fori(0, ROUNDS) as r:
            round_of(r, False)
    else:
        with eng.Fori(0, ROUNDS - 1) as r:
            round_of(r, True)
        round_of(ROUNDS - 1, False)


def rwkv_tensor(pe, ph, ph_in, m, before):
    T, A, V, G = ph.pe, ph.act, ph.vec, ph.pool

    def warm(bank):
        keep_warm(pe, bank, m.wr[:, 0, :, :].rearrange("p k d -> p (k d)"), WARM_RWKV)

    def product(out, lhsT, rhs):
        for k in range(KD):
            last = pe.matmul(out, lhsT(k), rhs(k), start=k == 0, stop=k == KD - 1)
        return last

    def rows(u, r):
        pe.wait_ge(*ph_in.vec.at("a_xn", u, r))
        turn_tensor(pe, ph, m, u, r, "a", m.ps[u][:, 1, :])
        if u == 1:
            warm(m.ps[u][:, 2, :])

    def lora(u, r):
        pe.wait_ge(*V.at("mix", u, r))
        product(m.ps[u][:, 0, 0:P], lambda k: m.maa_w1[:, k, 0:P], lambda k: m.mix[u][:, k, :])
        product(m.ps[u][0:DM, 0, P:2 * P], lambda k: m.maa_w1[:, k, P:ND * DM], lambda k: m.mix[u][:, k, :])\
            .then_inc(*T.did("lora", u))
        pe.wait_ge(*A.at("lora", u, r))
        for f in range(ND):
            for e in range(KD):
                n = KD * f + e
                out = m.ps[u][:, 1 + n // 4, (n % 4) * P:(n % 4 + 1) * P]
                if f < 4:
                    pe.matmul(out, m.maa_w2[:, f, e * P:(e + 1) * P], m.xx[u][:, 0:P], start=True, stop=True)
                else:
                    last = pe.matmul(out, m.maa_w2l[:, e * P:(e + 1) * P], m.xx[u][0:DM, P:2 * P],
                                     start=True, stop=True)
        last.then_inc(*T.did("mixes", u))

    def project(u, r):
        pe.wait_ge(*V.at("xm", u, r))
        xm = lambda f, k: m.xm[u][:, KD * f + k, :]
        product(m.ps[u][0:DD, 0, 0:P], lambda k: m.td_w1[:, k, :], lambda k: xm(MIX_W, k)).then_inc(*T.did("td1", u))
        for n, (w, f) in enumerate(((W_R, MIX_R), (W_K, MIX_K), (W_V, MIX_V))):
            for e in range(KD):
                last = product(m.ps[u][:, 1 + n // 2, (n % 2) * D + e * P:(n % 2) * D + (e + 1) * P],
                               lambda k: m.wr[:, w, k, e * P:(e + 1) * P], lambda k: xm(f, k))
        product(m.ps[u][:, 2, D:2 * D], lambda k: xm(MIX_G, k), lambda k: m.wr[:, W_G, k, :])\
            .then_inc(*T.did("rkvg", u))
        pe.wait_ge(*A.at("td1", u, r))
        for e in range(KD):
            last = pe.matmul(m.ps[u][:, 3, e * P:(e + 1) * P], m.td_w2[:, e * P:(e + 1) * P], m.td[u][:, :],
                             start=True, stop=True)
        last.then_inc(*T.did("td2", u))

    def spread(u, r):
        pe.wait_ge(*A.at("ew", u, r))
        pe.wait_ge(*V.at("gate", u, r))
        for j in range(HS):
            last = pe.matmul(m.ps[u][:, j // 2, (j % 2) * D:(j % 2 + 1) * D], m.sel[:, j, :], m.rkv[u][:, 2, :],
                             start=True, stop=True)
        last.then_inc(*T.did("vrep", u))

    def gather(u, r):
        pe.wait_ge(*V.at("rs", u, r))
        pe.wait_ge(*G.at("rs", u, r))
        for j in range(HS):
            pe.matmul(m.ps[u][:, 0, 0:D], m.gather[:, j, :], m.sc[u][:, j, :], start=j == 0, stop=j == HS - 1)
        pe.matmul(m.ps[u][:, 1, 0:D], m.headsum[:, :], m.ruk[u][:, :], start=True, stop=True).then_inc(*T.did("o", u))

    def heads(u, r):
        pe.wait_ge(*V.at("og", u, r))
        for e in range(KD):
            last = pe.transpose(m.ps[u][:, 2, e * P:(e + 1) * P], m.og[u][:, e * P:(e + 1) * P], m.ident[:, :])
        last.then_inc(*T.did("ogT", u))
        if u == 1:
            warm(m.ps[u][:, 0, :])

    def attended(u, r):
        pe.wait_ge(*V.at("y", u, r))
        for e in range(KD):
            last = pe.transpose(m.ps[u][:, 3, e * P:(e + 1) * P], m.tok[u][:, e * P:(e + 1) * P], m.ident[:, :])
        last.then_inc(*T.did("yT", u))
        pe.wait_ge(*A.at("yT", u, r))
        product(m.ps[u][:, 0, 0:D], lambda k: m.yT[u][:, k, :], lambda k: m.wr[:, W_O, k, :])\
            .then_inc(*T.did("wo", u))

    def shifted(u, r):
        pe.wait_ge(*V.at("f_xn", u, r))
        turn_tensor(pe, ph, m, u, r, "f", m.ps[u][:, 1, :])

    def ffn(u, r):
        pe.wait_ge(*V.at("mk", u, r))
        for e in range(KD):
            last = product(m.ps[u][:, 2, e * P:(e + 1) * P], lambda k: m.wr[:, W_FK, k, e * P:(e + 1) * P],
                           lambda k: m.mk[u][:, k, :])
        last.then_inc(*T.did("kk", u))
        pe.wait_ge(*V.at("mr", u, r))
        product(m.ps[u][:, 3, 0:D], lambda k: m.mr[u][:, k, :], lambda k: m.wr[:, W_FR, k, :])\
            .then_inc(*T.did("rr", u))

    def close(u, r):
        pe.wait_ge(*A.at("kk", u, r))
        product(m.ps[u][:, 0, 0:D], lambda k: m.kk[u][:, k * P:(k + 1) * P], lambda k: m.wr[:, W_FV, k, :])\
            .then_inc(*T.did("ffn", u))

    for sem, value in before:
        pe.wait_ge(sem, value)
    rwkv_rounds(pe, gather=gather, rows=rows, heads=heads, lora=lora, attended=attended, project=project,
                shifted=shifted, ffn=ffn, spread=spread, close=close)


def rwkv_scalar(act, ph, m):
    T, A, V, G = ph.pe, ph.act, ph.vec, ph.pool

    def rows(u, r):
        turn_act(act, ph, m, u, r, "a", m.ps[u][:, 1, :], lambda k: m.xa[u][:, k, :], "r1_w", "r1_b")

    def lora(u, r):
        act.wait_ge(*T.at("lora", u, r))
        act.activation(m.xx[u][:, 0:P], m.ps[u][:, 0, 0:P], ACT.Tanh)
        act.activation(m.xx[u][0:DM, P:2 * P], m.ps[u][0:DM, 0, P:2 * P], ACT.Tanh).then_inc(*A.did("lora", u))

    def project(u, r):
        act.wait_ge(*T.at("td1", u, r))
        act.activation(m.td[u][:, :], m.ps[u][0:DD, 0, 0:P], ACT.Tanh).then_inc(*A.did("td1", u))
        act.wait_ge(*T.at("rkvg", u, r))
        act.activation(m.rkv[u][:, :, :], m.ps[u][:, 1:3, :].rearrange("p c n -> p (c n)")[:, 0:3 * D], ACT.Copy)\
            .then_inc(*A.did("rkv", u))
        act.activation(m.th[u][:, :], m.ps[u][:, 2, D:2 * D], ACT.Tanh, scale=0.5).then_inc(*A.did("g", u))
        act.wait_ge(*T.at("td2", u, r))
        for e in range(KD):
            last = act.activation(m.ew[u][:, e * P:(e + 1) * P], m.ps[u][:, 3, e * P:(e + 1) * P], ACT.Exp,
                                  bias=m.col("decay", e))
        last.then_inc(*A.did("ew", u))
        act.wait_ge(*A.at("ew", u, r))
        act.activation(m.wS[u][:, :, 1:S], m.ew[u][:, :].rearrange("p (n s) -> p n s", s=S)[:, :, 0:S - 1],
                       ACT.Exp, scale=-1.0).then_inc(*A.did("w", u))

    def heads(u, r):
        act.wait_ge(*V.at("gvar", u, r))
        n = D // HS
        act.activation(m.sm[u][:, 0:n], m.sm[u][:, 0:n], ACT.Sqrt).then_inc(*A.did("gstd", u))

    def attended(u, r):
        act.wait_ge(*T.at("yT", u, r))
        act.activation(m.yT[u][:, :, :], m.ps[u][:, 3, 0:D], ACT.Copy).then_inc(*A.did("yT", u))

    def shifted(u, r):
        turn_act(act, ph, m, u, r, "f", m.ps[u][:, 1, :], lambda k: m.xa[u][:, k, :], "r2_w", "r2_b")

    def ffn(u, r):
        act.wait_ge(*T.at("kk", u, r))
        act.activation(m.kr[u][:, :], m.ps[u][:, 2, 0:D], ACT.Relu).then_inc(*A.did("relu", u))
        act.wait_ge(*A.at("relu", u, r))
        act.activation(m.kk[u][:, :], m.kr[u][:, :], ACT.Square).then_inc(*A.did("kk", u))
        act.wait_ge(*T.at("rr", u, r))
        act.activation(m.th[u][:, :], m.ps[u][:, 3, 0:D], ACT.Tanh, scale=0.5).then_inc(*A.did("rr", u))

    act.wait_ge(m.s_gn, 1)
    rwkv_rounds(act, rows=rows, lora=lora, project=project, heads=heads, attended=attended, shifted=shifted, ffn=ffn)


def rwkv_shift(vec, V, m, u, r, tag, state):
    xa = m.xa[u][:, :, :].rearrange("p k (b s) -> p k b s", b=2)
    sx = m.sx[u][:, :, :].rearrange("p k (b s) -> p k b s", b=2)
    first = m.encT_of(u, r).rearrange("p k (b s) -> p k b s", b=2)[:, :, :, state:state + 1]
    vec.tensor_tensor(sx[:, :, :, 1:S], xa[:, :, :, 0:S - 1], xa[:, :, :, 1:S], ALU.subtract)
    vec.tensor_tensor(sx[:, :, :, 0:1], first, xa[:, :, :, 0:1], ALU.subtract).then_inc(*V.did(tag + "_sx", u))


def rwkv_mix(vec, V, m, u, r, tag, dst, factor):
    vec.wait_ge(*V.at(tag + "_sx", u, r))
    vec.tensor_tensor(dst[:, :, :], m.sx[u][:, :, :], bc(factor, 2, [P, KD, P]), ALU.mult)\
        .then_inc(*V.did(f"{tag}_mul", u))
    vec.wait_ge(*V.at(f"{tag}_mul", u, r))
    return vec.tensor_tensor(dst[:, :, :], dst[:, :, :], m.xa[u][:, :, :], ALU.add)


def rwkv_vector(vec, ph, ph_in, m, before):
    T, A, V, G = ph.pe, ph.act, ph.vec, ph.pool
    n = D // HS
    head = lambda x: x.rearrange("p (h j) -> p h j", j=HS)

    def norm(r, tag="a", ph=ph_in):
        norm_vec(vec, ph, m, r, [(u, m.x_of(u, r), tag, m.xn[u][:, :], 0) for u in range(STREAMS)])

    def norm_out(r):
        norm(r, "f", ph)

    def mixed(u, r):
        vec.wait_ge(*A.at("a_hT", u, r))
        rwkv_shift(vec, V, m, u, r, "a", 1)
        rwkv_mix(vec, V, m, u, r, "a", m.mix[u], m.cols("maa_x")).then_inc(*V.did("mix", u))

    def mixes(u, r):
        vec.wait_ge(*T.at("mixes", u, r))
        xm = m.xm[u][:, :, :]
        wide = m.xm[u][:, :, :].rearrange("p (f k) t -> p f (k t)", k=KD)
        flat = lambda x: bc(x[u][:, :, :].rearrange("p k t -> p (k t)"), 1, [P, ND, D])
        vec.tensor_tensor(xm, m.ps[u][:, 1:4, :].rearrange("p c (n t) -> p (c n) t", t=P)[:, 0:ND * KD, :],
                          bc(m.cols("maa_stack"), 2, [P, ND * KD, P]), ALU.add).then_inc(*V.did("xm1", u))
        vec.wait_ge(*V.at("xm1", u, r))
        vec.tensor_tensor(wide, wide, flat(m.sx), ALU.mult).then_inc(*V.did("xm2", u))
        vec.wait_ge(*V.at("xm2", u, r))
        vec.tensor_tensor(wide, wide, flat(m.xa), ALU.add).then_inc(*V.did("xm", u))

    def project(u, r):
        vec.wait_ge(*A.at("rkv", u, r))
        for e in range(KD):
            part = slice(e * P, (e + 1) * P)
            vec.scalar_tensor_tensor(out=m.ruk[u][:, part], in0=m.rkv[u][:, 0, part], scalar=m.col("u", e),
                                     in1=m.rkv[u][:, 1, part], op0=ALU.mult, op1=ALU.mult)
        vec.wait_ge(*A.at("g", u, r))
        vec.scalar_tensor_tensor(out=m.gate[u][:, :], in0=m.th[u][:, :], scalar=1.0, in1=m.ps[u][:, 2, D:2 * D],
                                 op0=ALU.add, op1=ALU.mult).then_inc(*V.did("gate", u))
        vec.wait_ge(*V.at("gate", u, r))
        vec.tensor_tensor(m.gate_b[u][:, :], m.gate[u][:, :], m.row("gn_b"), ALU.mult)
        vec.tensor_tensor(m.gate[u][:, :], m.gate[u][:, :], m.row("gn_w"), ALU.mult).then_inc(*V.did("gates", u))
        vec.tensor_scalar(m.av[u][:, :, :, 0:1], m.s0[:, m.tile(u, r), :].rearrange(
            "p (j n o) -> p j n o", n=4, o=1), 1.0, None, ALU.mult).then_inc(*V.did("s0", u))

    def scan(u, r):
        vec.wait_ge(*T.at("vrep", u, r))
        keys = m.rkv[u][:, 1, :].rearrange("p (n s) -> p n s", s=S)[:, :, 0:S - 1]
        vals = m.ps[u][:, :, :].rearrange("p c (j n s) -> p (c j) n s", j=2, s=S)[:, :, :, 0:S - 1]
        vec.tensor_tensor(m.av[u][:, :, :, 1:S], vals, bc(keys, 1, [P, HS, 4, S - 1]), ALU.mult)\
            .then_inc(*V.did("av", u))
        vec.wait_ge(*V.at("av", u, r))
        vec.wait_ge(*A.at("w", u, r))
        for j in range(HS):
            last = vec.tensor_tensor_scan(m.sc[u][:, j, :], m.wS[u][:, :, :].rearrange("p n s -> p (n s)"),
                                          m.av[u][:, j, :, :].rearrange("p n s -> p (n s)"), 0.0,
                                          ALU.mult, ALU.add)
        last.then_inc(*V.did("scan", u))
        vec.wait_ge(*V.at("scan", u, r))
        vec.tensor_tensor(m.sc[u][:, 0:m.vj, :], m.sc[u][:, 0:m.vj, :],
                          bc(m.rkv[u][:, 0, :], 1, [P, m.vj, D]), ALU.mult).then_inc(*V.did("rs", u))

    def gather(u, r):
        vec.wait_ge(*T.at("o", u, r))
        vec.tensor_tensor(m.og[u][:, :], m.ps[u][:, 1, 0:D], m.rkv[u][:, 2, :], ALU.mult).then_inc(*V.did("cv", u))
        vec.wait_ge(*V.at("cv", u, r))
        vec.tensor_tensor(m.og[u][:, :], m.ps[u][:, 0, 0:D], m.og[u][:, :], ALU.add).then_inc(*V.did("og", u))

    def heads(u, r):
        tok = m.tok[u][:, :]
        vec.wait_ge(*T.at("ogT", u, r))
        vec.tensor_reduce(m.mx[u][:, 0:n], head(m.ps[u][:, 2, 0:D]), AX, ALU.add).then_inc(*V.did("gsum", u))
        vec.wait_ge(*V.at("gsum", u, r))
        vec.scalar_tensor_tensor(out=head(tok), in0=bc(m.mx[u][:, 0:n], 2, [P, n, HS]), scalar=-1.0 / HS,
                                 in1=head(m.ps[u][:, 2, 0:D]), op0=ALU.mult, op1=ALU.add).then_inc(*V.did("cen", u))
        vec.wait_ge(*V.at("cen", u, r))
        vec.tensor_tensor(m.sq[u][:, :], tok, tok, ALU.mult).then_inc(*V.did("sq", u))
        vec.wait_ge(*V.at("sq", u, r))
        vec.tensor_reduce(m.sm[u][:, 0:n], head(m.sq[u][:, :]), AX, ALU.add).then_inc(*V.did("gsq", u))
        vec.wait_ge(*V.at("gsq", u, r))
        vec.tensor_scalar(m.sm[u][:, 0:n], m.sm[u][:, 0:n], 1.0 / HS, EPS, ALU.mult, ALU.add)\
            .then_inc(*V.did("gvar", u))

    def gated(u, r):
        tok = m.tok[u][:, :]
        vec.wait_ge(*A.at("gstd", u, r))
        vec.reciprocal(m.rc[u][:, 0:n], m.sm[u][:, 0:n]).then_inc(*V.did("grstd", u))
        vec.wait_ge(*V.at("grstd", u, r))
        vec.tensor_tensor(head(tok), head(tok), bc(m.rc[u][:, 0:n], 2, [P, n, HS]), ALU.mult)\
            .then_inc(*V.did("y1", u))
        vec.wait_ge(*V.at("y1", u, r))
        vec.tensor_tensor(tok, tok, m.gate[u][:, :], ALU.mult).then_inc(*V.did("y2", u))
        vec.wait_ge(*V.at("y2", u, r))
        vec.tensor_tensor(tok, tok, m.gate_b[u][:, :], ALU.add).then_inc(*V.did("y", u))

    def attended(u, r):
        vec.wait_ge(*T.at("wo", u, r))
        vec.tensor_tensor(m.x_of(u, r), m.ps[u][:, 0, 0:D], m.x_of(u, r), ALU.add).then_inc(*V.did("x1", u))

    def shifted(u, r):
        vec.wait_ge(*A.at("f_hT", u, r))
        rwkv_shift(vec, V, m, u, r, "f", 0)
        rwkv_mix(vec, V, m, u, r, "f", m.mk[u], m.cols("ffn_k")).then_inc(*V.did("mk", u))
        vec.tensor_tensor(m.mr[u][:, :, :], m.sx[u][:, :, :], bc(m.cols("ffn_r"), 2, [P, KD, P]), ALU.mult)\
            .then_inc(*V.did("mr1", u))
        vec.wait_ge(*V.at("mr1", u, r))
        vec.tensor_tensor(m.mr[u][:, :, :], m.mr[u][:, :, :], m.xa[u][:, :, :], ALU.add).then_inc(*V.did("mr", u))

    def close(u, r):
        vec.wait_ge(*A.at("rr", u, r))
        vec.wait_ge(*T.at("ffn", u, r))
        vec.scalar_tensor_tensor(out=m.tok[u][:, :], in0=m.th[u][:, :], scalar=1.0, in1=m.ps[u][:, 0, 0:D],
                                 op0=ALU.add, op1=ALU.mult).then_inc(*V.did("rf", u))
        vec.wait_ge(*V.at("rf", u, r))
        vec.scalar_tensor_tensor(out=m.x_of(u, r), in0=m.tok[u][:, :], scalar=0.5, in1=m.x_of(u, r),
                                 op0=ALU.mult, op1=ALU.add).then_inc(*V.did("out", u))

    for sem, value in before:
        vec.wait_ge(sem, value)
    for u in range(STREAMS):
        vec.memset(m.wS[u][:, :, 0:1], 0.0)
    vec.tensor_scalar(m.row("gn_w"), m.row("gn_w"), 0.5, None, ALU.mult)
    vec.tensor_scalar(m.row("gn_b"), m.row("gn_b"), 0.5, None, ALU.mult).then_inc(m.s_gn, 1)
    vec.wait_ge(m.s_gn, 1)
    rwkv_rounds(vec, norm=norm, gather=gather, heads=heads, mixed=mixed, gated=gated, mixes=mixes,
                attended=attended, norm_out=norm_out, project=project, shifted=shifted, close=close, scan=scan)


def rwkv_gpsimd(pool, ph, ph_in, m):
    V, G = ph.vec, ph.pool

    def norm(r, tag="a", ph=ph_in):
        for u in range(STREAMS):
            norm_pool(pool, ph, m, u, r, tag)

    def norm_out(r):
        norm(r, "f", ph)

    def scan(u, r):
        pool.wait_ge(*V.at("scan", u, r))
        pool.tensor_tensor(m.sc[u][:, m.vj:HS, :], m.sc[u][:, m.vj:HS, :],
                           bc(m.rkv[u][:, 0, :], 1, [P, HS - m.vj, D]), ALU.mult).then_inc(*G.did("rs", u))

    rwkv_rounds(pool, norm=norm, scan=scan, norm_out=norm_out)




def build(nc, dram, out, orders=STEPS, stop_after=99):
    m = Memory()
    with ExitStack() as ctx:
        n_sb = [0]

        def sb(shape):
            n_sb[0] += 1
            return ctx.enter_context(nc.sbuf_tensor(f"sb{n_sb[0]}", shape, F32))

        def sbr(shape):
            n_sb[0] += 1
            return ctx.enter_context(nc.sbuf_tensor(f"sb{n_sb[0]}", shape, F32R))

        def pair(shape):
            return [sb(shape) for _ in range(STREAMS)]

        def sem(name):
            return ctx.enter_context(nc.semaphore(name))

        m.x = sb([P, TILES, D])
        m.encT, m.ctx = sb([P, KD, B * S]), sb([P, TILES, D])
        m.ident, m.headmask, m.headsum = sb([P, P]), sb([P, HB]), sb([P, P])
        m.hT = sb([P, KD, B * S])
        m.sel, m.gather = (m.hT[:, k, :].rearrange("p (j q) -> p j q", q=P) for k in range(KD))
        m.colbuf, m.rowbuf, m.ones = sb([P, NCOL]), sb([P, len(ROWS), D]), sb([1, P])
        m.w1x1 = sb([P, 4, P])
        m.wr = sb([P, 8, KD, D])
        m.wqkv0, m.wao0, m.wq0, m.wkv0, m.wco0 = (
            m.wr[:, a:b, :, :].rearrange("p n k d -> p (n k d)").rearrange("p (k c) -> p k c", k=KD)
            for a, b in ((0, 3), (3, 4), (4, 5), (5, 7), (7, 8)))
        m.mask_mul, m.mask_add = (
            {"self": sb([P, S])[:, :], "cross": sb([P, TILES * S])[:, :]} for _ in range(2))
        m.s0 = m.mask_mul["cross"][:, 0:TILES * HS * 4].rearrange("p (t n) -> p t n", t=TILES)
        m.td_w2 = m.mask_mul["cross"][0:DD, TILES * HS * 4:TILES * HS * 4 + D]
        for masks in (m.mask_mul, m.mask_add):
            masks["cross"] = masks["cross"].rearrange("p (t s) -> p t s", s=S)
        m.kmask = {kind: sb([P, HB]) for kind in ATTN0}
        m.maa_w1, m.maa_w2, m.maa_w2l = sb([P, KD, ND * DM]), sb([P, 4, D]), sb([DM, D])
        m.td_w1 = sb([P, KD, DD])
        m.vj = 5
        m.wa, m.wb = pair([P, PACK_A]), pair([P, D])
        m.enc_parts = [sbr([P, KD, B * S]) for _ in range(2)]
        m.h_parts = [sbr([P, KD, B * S]) for _ in range(2)]
        m.w_parts = [[sbr([P, 2 * KD * P]) for _ in range(2)] for _ in range(STREAMS)]
        m.cT_parts = [[sbr([P, TILES, P]) for _ in range(STREAMS)] for _ in range(2)]
        m.g_parts = [[x[:, :, :].rearrange("p t q -> p (t q)") for x in part] for part in m.cT_parts]
        m.wv_parts = [sbr([P, KD, STREAMS * P]) for _ in range(2)]
        m.wb_parts = [[sbr([P, D]) for _ in range(2)] for _ in range(STREAMS)]
        m.all_stats, m.all_mv, m.all_rstd = sb([P, TILES, 6]), sb([P, TILES, 2]), sb([P, 2, TILES])
        m.stats, m.mv, m.rstd, m.rstd2 = pair([P, 2, 6]), pair([P, 2, 2]), pair([P, 2]), pair([P, 2])
        m.mx, m.sm, m.rc, m.dv, m.bv = pair([P, 32]), pair([P, 32]), pair([P, 32]), pair([P, 1]), pair([P, 1])
        m.xn, m.xn_last = pair([P, D]), pair([P, D])

        AREA = 7040
        area = pair([P, AREA])

        def cut(u, at, shape, rows=P):
            n = 1
            for s in shape:
                n *= s
            ap = area[u][0:rows, at[0]:at[0] + n]
            at[0] += n
            assert at[0] <= AREA, at
            if len(shape) == 1:
                return ap
            names = "abcde"[:len(shape)]
            return ap.rearrange(f"p ({' '.join(names)}) -> p {' '.join(names)}",
                                **{c: s for c, s in zip(names[1:], shape[1:])})

        def cuts(shape, at, rows=P):
            start = at[0]
            both = []
            for u in range(STREAMS):
                at[0] = start
                both.append(cut(u, at, shape, rows))
            return both

        at = [0]
        m.hT_s = cuts([KD, P], at)
        m.encT_t, m.cT0 = cuts([KD, P], at), cuts([KD, P], at)
        m.kdiag = cuts([KD, 2, HB, S], at)
        m.vdiag, m.qT0 = cuts([2, NH0 // 2, 2 * HD0], at), cuts([KD, P], at)
        m.p0 = cuts([NH0 * S], at)
        m.pT0 = cuts([NH0 // 2, P], at)
        m.all_xn = cut(0, [0], [TILES, D])
        at = [0]
        m.g = cuts([B * S], at)
        at = [0]
        m.cn, m.ctx_t, m.mnm, m.mlT = cuts([D], at), cuts([D], at), cuts([2 * D], at), cuts([2, P], at)
        m.p1, m.p1T, m.mo = cuts([4, D], at), cuts([2, 2 * D], at), cuts([D], at)
        at = [0]
        m.qT, m.kT, m.v = cuts([B * S], at), cuts([TILES, 2, T2], at), cuts([4, STREAMS, P], at)
        m.p, m.pT = cuts([TILES, T2], at), cuts([TILES, 2, S], at)
        m.pn = cuts([TILES, S], at)
        m.pb, m.bwT = cut(0, at, [TILES, NH2]), cut(0, at, [KD, NH2])
        m.bw, m.pbT = cut(0, at, [D], NH2), cut(0, at, [B * S], NH2)
        at = [0]
        m.xa, m.sx, m.mix = ([m.ctx[:, 4 * u + i, :].rearrange("p (k q) -> p k q", q=P) for u in range(STREAMS)]
                             for i in range(3))
        m.ruk = [m.ctx[:, 4 * u + 3, :] for u in range(STREAMS)]
        m.rkv = [x[:, 0:3 * D].rearrange("p (n d) -> p n d", d=D) for x in m.wa]
        m.gate_b = m.wb
        m.xm = cuts([ND * KD, P], at)
        m.xx, m.td, m.ew, m.wS = cuts([2 * P], at), cuts([P], at, DD), cuts([D], at), cuts([4, S], at)
        m.th, m.gate = cuts([D], at), cuts([D], at)
        m.av = cuts([HS, 4, S], at)
        m.tok, m.sc = cuts([D], at), cuts([HS, D], at)
        m.og = [x[:, 2:4, :].rearrange("p a b -> p (a b)")[:, 0:D] for x in m.xm]
        m.sq = [x[:, 4:6, :].rearrange("p a b -> p (a b)") for x in m.xm]
        m.yT = [x[:, 6:8, :] for x in m.xm]
        m.mk = m.mix
        m.mr = [x[:, 8:10, :] for x in m.xm]
        m.kr = m.xx
        m.kk = [x[:, 0:2, :].rearrange("p a b -> p (a b)") for x in m.xm]

        m.ps = [ctx.enter_context(nc.psum_tensor(f"ps{u}", [P, 4, 512], F32)) for u in range(STREAMS)]

        m.tile = lambda u, r: 2 * r + u
        m.x_of = lambda u, r: m.x[:, 2 * r + u, :]
        m.ctx_of = lambda u, r: m.ctx[:, 2 * r + u, :]
        m.encT_of = lambda u, r: m.encT[:, :, bass.ds((2 * r + u) * P, P)]
        m.hT_of = lambda k, u, r: m.hT[:, k, bass.ds((2 * r + u) * P, P)]
        m.hT_pair = lambda k, i: m.hT[:, k, :].rearrange("p (t q) -> p t q", q=P)[:, SHARED[i][0]:SHARED[i][1] + 1:2, :]
        m.turned = lambda k, i: m.ps[i % 2][:, i // 2, :].rearrange("p (t k q) -> p t k q", t=2, k=KD)[:, :, k, :]
        m.acc = lambda t: m.ps[t % 2][:, 2 + t // 4, (t // 2 % 2) * D:(t // 2 % 2 + 1) * D]
        m.col = lambda name, k=0: m.colbuf[:, COL[name] + k:COL[name] + k + 1]
        m.cols = lambda name: m.colbuf[:, COL[name]:COL[name] + dict(COLS)[name]]
        m.row = lambda name: m.rowbuf[:, ROWS.index(name), :]
        m.head_col = lambda u, n: m.wa[u][:, 3 * KD * P + n:3 * KD * P + n + 1]

        m.s_const, m.s_wqkv, m.s_x, m.s_enc, m.s_w0, m.s_mask, m.s_wr, m.s_ctx = (
            sem(n) for n in ("const_in", "wqkv_in", "x_in", "encT_in", "w0_in", "mask_in", "rwkv_in", "ctx_in"))
        m.s_pT, m.s_split, m.s_zero, m.s_gn, m.s_masks, m.s_acc, m.s_pad, m.s_out = (
            sem(n) for n in ("turned_probs_zeroed", "context_split", "zeroed", "group_norm_rows", "masks",
                             "acc_added", "padded", "out_stored"))
        m.s_h = [sem(f"rows_split_{c}") for c in range(2)]
        m.s_wa = [sem(f"wa_in_{u}") for u in range(STREAMS)]
        m.s_wb = [sem(f"wb_in_{u}") for u in range(STREAMS)]
        m.n_const = 4

        names = ("attn0_in", "attn0", "attn0_rows", "mlp0", "inorm_in", "inorm", "heads1", "close1", "norm2",
                 "heads2", "close2", "norm3", "mlp2", "rwkv_in", "rwkv")
        ph = {n: Phase(sem, n, orders) for n in names}
        last = NH2 // 2 - 1
        end_of = lambda steps, name, rounds: [steps.at(name, u, rounds - 1) for u in range(STREAMS)]

        block = ctx.enter_context(nc.Block())

        @block.sync
        def _(sp):
            for t, name in ((m.colbuf, "cols"), (m.ident, "ident"), (m.headmask, "headmask"), (m.ones, "ones")):
                sp.dma_start(t[:, :], dram[name]).then_inc(m.s_const, 16)
            sp.dma_start(m.x[:, :, :], dram["x"].rearrange("t p d -> p t d")).then_inc(m.s_x, 16)
            for half in (slice(0, S), slice(S, P)):
                sp.dma_start(m.mask_mul["self"][half, :], dram["mask_self"]).then_inc(m.s_mask, 16)
            sp.dma_start(m.mask_mul["cross"][:, :, :], dram["mask_cross"].rearrange("t p s -> p t s"))\
                .then_inc(m.s_mask, 16)
            sp.dma_start(m.wqkv0[:, :, :], dram["w_qkv"]).then_inc(m.s_wqkv, 16)
            sp.dma_start(m.encT[:, :, :], dram["encT"]).then_inc(m.s_enc, 16)
            sp.dma_start(m.rowbuf[:, :, :], dram["rows"].partition_broadcast(P)).then_inc(m.s_w0, 16)
            for t, name in ((m.wao0, "w_ao"), (m.wkv0, "w_kv"), (m.wq0, "w_q"), (m.wco0, "w_co")):
                sp.dma_start(t[:, :, :], dram[name]).then_inc(m.s_w0, 16)
            stream_in(sp, m, ph["mlp0"], dram["mlp0_a"], dram["mlp0_b"], MLP_A, F // P // 2,
                      [(ph["mlp0"].act, "gelu1")], [(ph["mlp0"].pe, "fc2")], [])
            sp.dma_start(m.ctx[:, :, :], dram["ctx"].rearrange("t p d -> p t d")).then_inc(m.s_ctx, 16)
            sp.wait_ge(m.s_pad, 1)
            for b in range(2):
                half = slice(b * S, (b + 1) * S)
                sp.dma_start(m.w1x1[half, :, half], dram["w1x1"]).then_inc(m.s_ctx, 16)
            for f in range(4):
                sp.dma_start(m.maa_w2[f * DM:(f + 1) * DM, f, :], dram["maa_w2"][f]).then_inc(m.s_wr, 16)
            sp.dma_start(m.maa_w2l[:, :], dram["maa_w2"][4]).then_inc(m.s_wr, 16)
            for t, name in ((m.maa_w1, "maa_w1"), (m.td_w1, "td_w1"), (m.headsum, "headsum")):
                sp.dma_start(t[:], dram[name]).then_inc(m.s_wr, 16)
            for s, v in end_of(ph["attn0"].pe, "cross_out", ROUNDS):
                sp.wait_ge(s, v)
            for t, name in ((m.wr, "w_r"), (m.td_w2, "td_w2"), (m.s0, "s0")):
                sp.dma_start(t[:], dram[name]).then_inc(m.s_wr, 16)
            if stop_after >= 3:
                stream_in(sp, m, ph["heads1"], dram["heads1_a"], dram["heads1_b"], PACK_A, NH2 // 2,
                          [(ph["heads1"].pe, "v1")], [(ph["heads1"].pe, "out")],
                          end_of(ph["mlp0"].pe, "fc2", F // P // 2))
            if stop_after >= 4:
                stream_in(sp, m, ph["heads2"], dram["heads2_a"], dram["heads2_b"], PACK_A, NH2 // 2,
                          [(ph["heads2"].pe, "v1")], [(ph["heads2"].pe, "out")],
                          end_of(ph["heads1"].pe, "out", NH2 // 2))
            if stop_after >= 5:
                stream_in(sp, m, ph["mlp2"], dram["mlp2_a"], dram["mlp2_b"], MLP_A, F // P // 2,
                          [(ph["mlp2"].act, "gelu1")], [(ph["mlp2"].pe, "fc2")],
                          end_of(ph["heads2"].pe, "out", NH2 // 2))
            for s, v in [ph["mlp2"].pe.at("fc1_1", u, F // P // 2 - 1) for u in range(STREAMS)]:
                sp.wait_ge(s, v)
            for t, name in ((m.sel, "sel"), (m.gather, "gather")):
                sp.dma_start(t, dram[name]).then_inc(m.s_wr, 16)
            if stop_after >= 6:
                with sp.Fori(0, ROUNDS) as r:
                    for u in range(STREAMS):
                        sp.wait_ge(*ph["rwkv"].vec.at("out", u, r))
                        sp.wait_ge(m.s_x, 16)
                        sp.dma_start(out[2 * r + u], m.x_of(u, r)).then_inc(m.s_out, 16)
                sp.wait_ge(m.s_out, 16 * TILES)
            else:
                if stop_after == 2:
                    for s, v in end_of(ph["inorm"].vec, "sum", ROUNDS):
                        sp.wait_ge(s, v)
                else:
                    sp.wait_ge(m.s_acc, {1: 2, 3: 4, 4: 6, 5: 8}[stop_after])
                sp.dma_start(out.rearrange("t p d -> p t d"), m.x[:, :, :]).then_inc(m.s_out, 16)
                sp.wait_ge(m.s_out, 16)

        @block.gpsimd
        def _(pool):
            for u in range(STREAMS):
                last = pool.memset(m.vdiag[u][:, :, :, :], 0.0)
            last.then_inc(m.s_zero, 1)
            pool.memset(m.w1x1[:, :, :], 0.0)
            pool.memset(m.maa_w2[:, :, :], 0.0).then_inc(m.s_pad, 1)
            attn0_gpsimd(pool, ph["attn0"], ph["attn0_in"], m)
            split_weights_gpsimd(pool, ph["mlp0"], m, 0, F // P // 2, KD * P, "fc1_1", "fc2")
            split_context_gpsimd(pool, m)
            if stop_after >= 2:
                inorm_gpsimd(pool, ph["inorm"], ph["inorm_in"], m, [(m.s_ctx, 48)])
            if stop_after >= 3:
                split_rows(pool, m, 0, 2, [ph["inorm"].act.at("n_hT", u, ROUNDS // 2 - 1) for u in range(STREAMS)])
                split_weights_gpsimd(pool, ph["heads1"], m, 4, NH2 // 2, 2 * KD * P, "k1", "out", True)
            if stop_after >= 4:
                norm_all_gpsimd(pool, ph["norm2"], m)
                split_weights_gpsimd(pool, ph["heads2"], m, 12, NH2 // 2, 2 * KD * P, "k1", "out", True)
            if stop_after >= 5:
                norm_all_gpsimd(pool, ph["norm3"], m)
                split_weights_gpsimd(pool, ph["mlp2"], m, 20, F // P // 2, KD * P, "fc1_1", "fc2")
            if stop_after >= 6:
                rwkv_gpsimd(pool, ph["rwkv"], ph["rwkv_in"], m)

        @block.scalar
        def _(act):
            attn0_scalar(act, ph["attn0"], ph["attn0_rows"], m)
            mlp_scalar(act, ph["mlp0"], m, ACT.Gelu_apprx_tanh)
            if stop_after >= 2:
                inorm_scalar(act, ph["inorm"], m)
            if stop_after >= 3:
                heads_scalar(act, ph["heads1"], m)
            if stop_after >= 4:
                norm_all_scalar(act, ph["norm2"], m, "w2_s", "w2_b")
                heads_scalar(act, ph["heads2"], m)
            if stop_after >= 5:
                norm_all_scalar(act, ph["norm3"], m, "wm_s", "wm_b")
                mlp_scalar(act, ph["mlp2"], m, ACT.Gelu)
            if stop_after >= 6:
                rwkv_scalar(act, ph["rwkv"], m)

        @block.vector
        def _(vec):
            attn0_vector(vec, ph["attn0"], ph["attn0_in"], m)
            split_rows(vec, m, 0, 0, [ph["attn0_rows"].act.at("mlp_hT", u, ROUNDS // 2 - 1) for u in range(STREAMS)])
            split_rows(vec, m, 1, 0, end_of(ph["attn0_rows"].act, "mlp_hT", ROUNDS))
            mlp_vector(vec, ph["mlp0"], m)
            add_acc_vector(vec, m, m.s_acc, end_of(ph["mlp0"].pe, "fc2", F // P // 2))
            if stop_after >= 2:
                inorm_vector(vec, ph["inorm"], ph["inorm_in"], m, [(m.s_acc, 2), (m.s_ctx, 48)])
            if stop_after >= 3:
                split_rows(vec, m, 1, 2, end_of(ph["inorm"].act, "n_hT", ROUNDS))
                heads_vector(vec, ph["heads1"], m, 4)
                bias_token_vector(vec, ph["close1"], m)
                add_acc_vector(vec, m, m.s_acc, [ph["close1"].pe.at("acc", 0, 0)])
            if stop_after >= 4:
                norm_all_vector(vec, ph["norm2"], m, "w2_s", "w2_b", [(m.s_acc, 4)], 4)
                heads_vector(vec, ph["heads2"], m, 12)
                bias_token_vector(vec, ph["close2"], m)
                add_acc_vector(vec, m, m.s_acc, [ph["close2"].pe.at("acc", 0, 0)])
            if stop_after >= 5:
                norm_all_vector(vec, ph["norm3"], m, "wm_s", "wm_b", [(m.s_acc, 6)], 6)
                mlp_vector(vec, ph["mlp2"], m)
                add_acc_vector(vec, m, m.s_acc, end_of(ph["mlp2"].pe, "fc2", F // P // 2))
            if stop_after >= 6:
                rwkv_vector(vec, ph["rwkv"], ph["rwkv_in"], m, [(m.s_acc, 8)])

        @block.tensor
        def _(pe):
            attn0_tensor(pe, ph["attn0"], ph["attn0_in"], ph["attn0_rows"], m)
            mlp_tensor(pe, ph["mlp0"], m, "b2", 0, 2, end_of(ph["attn0_rows"].act, "mlp_hT", ROUNDS))
            if stop_after >= 2:
                inorm_tensor(pe, ph["inorm"], ph["inorm_in"], m, [(m.s_acc, 2), (m.s_ctx, 48)])
            if stop_after >= 3:
                heads_tensor(pe, ph["heads1"], m, "bo1", 4, 4, [(m.s_split, 2)]
                             + end_of(ph["inorm"].act, "n_hT", ROUNDS))
                bias_token_tensor(pe, ph["heads1"], ph["close1"], m)
            if stop_after >= 4:
                norm_all_tensor(pe, ph["norm2"], m)
                heads_tensor(pe, ph["heads2"], m, "bo2", 12, 6, [])
                bias_token_tensor(pe, ph["heads2"], ph["close2"], m)
            if stop_after >= 5:
                norm_all_tensor(pe, ph["norm3"], m)
                mlp_tensor(pe, ph["mlp2"], m, "b_fc2", 20, 8, [])
            if stop_after >= 6:
                rwkv_tensor(pe, ph["rwkv"], ph["rwkv_in"], m, [(m.s_acc, 8), (m.s_wr, 16 * 13)])


def lay_out(inputs):
    import numpy as np

    a = {k: np.asarray(v) for k, v in inputs.items()}
    L0, L1, L2, L3 = (lambda n, i=i: a[f"L{i}_xattn_{n}"] for i in range(4))
    block = lambda w: np.ascontiguousarray(w.reshape(-1, P, w.shape[-1]).transpose(1, 0, 2))
    col = lambda v: v.reshape(-1, P).T
    twice = lambda v: np.concatenate([v, v]).reshape(P, 1)
    qkv, kv = L0("b_qkv"), L0("b_kv")
    cols = [L0("ln1_s"), L0("ln1_b"), qkv[:D], qkv[D:2 * D], qkv[2 * D:], L0("ln2_s"), L0("ln2_b"), L0("b_q"),
            kv[:D], kv[D:], L0("ln3_s"), L0("ln3_b")]
    cols = [col(v) for v in cols] + [twice(L1(n)) for n in ("bn", "bm", "bl", "bo")]
    cols += [col(L2(n)) for n in ("ln1_scale", "ln1_offset", "ln2_scale", "ln2_offset", "ln_mlp_scale",
                                  "ln_mlp_offset")]
    cols += [col(L3(n).reshape(-1)) for n in ("ln1_w", "ln1_b", "ln2_w", "ln2_b", "maa_x", "maa_stack", "time_decay",
                                              "u", "ffn_maa_k", "ffn_maa_r")]
    cols += [np.full((P, 1), -0.5, np.float32), np.ones((P, 1), np.float32)]
    rows = [L0("b_ao"), L0("b_co"), L0("b2"), L2("bo1"), L2("bo2"), L2("b_fc2"), L3("gn_w"), L3("gn_b")]

    def heads(i):
        w = [L2(f"w{n}{i}").reshape(KD, P, NH2, HD2).transpose(2, 1, 0, 3).reshape(NH2, P, KD * HD2) for n in "qkv"]
        c = [L2(n).reshape(NH2, HD2, 1) for n in (f"bq{i}", f"bk{i}", f"bv{i}", f"bias_k{i}", f"bias_v{i}")]
        return np.ascontiguousarray(np.concatenate(w + c, axis=2)), L2(f"wo{i}").reshape(NH2, HD2, D)

    def mlp(w1, b1, w2):
        w = w1.reshape(KD, P, F // P, P).transpose(2, 1, 0, 3).reshape(F // P, P, KD * P)
        return np.ascontiguousarray(np.concatenate([w, b1.reshape(F // P, P, 1)], axis=2)), w2.reshape(F // P, P, D)

    ctx = a["ctx_2048"]
    p, n = np.arange(P)[:, None], np.arange(P)[None, :]
    same = p // HS == n // HS
    got = {
        "x": a["x"].reshape(TILES, P, D), "ctx": ctx.reshape(TILES, P, D),
        "encT": np.ascontiguousarray(ctx.reshape(B * S, KD, P).transpose(2, 1, 0)),
        "ident": np.eye(P, dtype=np.float32),
        "headmask": (np.arange(P)[:, None] // HD0 == np.arange(HB)[None, :]).astype(np.float32),
        "cols": np.ascontiguousarray(np.concatenate(cols, axis=1)), "rows": np.stack(rows),
        "ones": np.ones((1, P), np.float32),
        "mask_self": a["mask_1x1xSxS2_fc1"].reshape(S, S), "mask_cross": a["mask_Bx1xSxS2_ff1"].reshape(TILES, P, S),
        "w_qkv": block(L0("w_qkv")), "w_ao": block(L0("w_ao")), "w_q": block(L0("w_q")), "w_kv": block(L0("w_kv")),
        "w_co": block(L0("w_co")),
        "w1x1": np.ascontiguousarray(np.stack([L1(n) for n in ("Wn", "Wm", "Wl", "Wo")]).transpose(2, 0, 1)),
        "maa_w2": L3("maa_w2"), "maa_w1": block(L3("maa_w1")), "td_w1": block(L3("td_w1")), "td_w2": L3("td_w2"),
        "w_r": np.ascontiguousarray(np.stack([L3(n) for n in ("Wr", "Wk", "Wv", "Wg", "Wo", "Wfk", "Wfr", "Wfv")])
                                    .transpose(2, 0, 1).reshape(KD, P, 8, D).transpose(1, 2, 0, 3)),
        "s0": np.ascontiguousarray(ctx[:, 2:2 + HS, :].reshape(TILES, 2, KD, P, HS).transpose(3, 0, 4, 2, 1)
                                   .reshape(P, TILES, HS * 4)),
        "sel": np.stack([same & (p % HS == j) for j in range(HS)], axis=1).astype(np.float32),
        "gather": np.stack([same & (n % HS == j) for j in range(HS)], axis=1).astype(np.float32),
        "headsum": same.astype(np.float32),
    }
    got["mlp0_a"], got["mlp0_b"] = mlp(L0("w1"), L0("b1"), L0("w2"))
    got["mlp2_a"], got["mlp2_b"] = mlp(L2("w_fc1"), L2("b_fc1"), L2("w_fc2"))
    for i in (1, 2):
        got[f"heads{i}_a"], got[f"heads{i}_b"] = heads(i)
    return {k: np.ascontiguousarray(v) for k, v in got.items()}


def kernel(**inputs):
    import concourse.bacc as bacc
    from concourse.bass_utils import run_bass_kernel_spmd

    arrays = lay_out(inputs)
    nc = bacc.Bacc("TRN2", target_bir_lowering=False, num_devices=1)
    dram = {k: nc.dram_tensor(f"in_{k}", v.shape, F32, kind="ExternalInput").ap() for k, v in arrays.items()}
    out = nc.dram_tensor("out_x", (TILES, P, D), F32, kind="ExternalOutput").ap()
    build(nc, dram, out)
    result = run_bass_kernel_spmd(nc, [{f"in_{k}": v for k, v in arrays.items()}], core_ids=[0])
    return result.results[0]["out_x"].reshape(B, S, D)
```
